# Optimizing a Trainium2 kernel written in Bass

```python
import numpy as np
import jax
import jax.numpy as jnp

def _softmax(x, axis=-1):
    return jax.nn.softmax(x, axis=axis)

def _gelu(x):
    return jax.nn.gelu(x, approximate=True)

def _silu(x):
    return jax.nn.silu(x)

def _sigmoid(x):
    return jax.nn.sigmoid(x)

def _layernorm(x, axis=-1, eps=1e-05):
    m = jnp.mean(x, axis=axis, keepdims=True)
    v = jnp.var(x, axis=axis, keepdims=True)
    return (x - m) / jnp.sqrt(v + eps)

def _scatter_add(tgt, idx, src, axis=0):
    return tgt.at[idx].add(src)

def _segment_sum(src, seg, n):
    return jax.ops.segment_sum(src, seg, n)
kernel_name = 'mk_seq_postln_d2_jaxref_r8_7caa44'

def setup_inputs(seed: int=0):
    np.random.seed(seed)
    _w = jnp.asarray

    def _L0_attn_setup():
        import jax, jax.numpy as jnp
        import numpy as np
        EMBED_DIM = 128
        NUM_HEADS = 16
        HEAD_DIM = EMBED_DIM // NUM_HEADS
        ROPE_BASE = 10000.0

        def rotate_half(x):
            d = x.shape[-1] // 2
            x1, x2 = (x[..., :d], x[..., d:])
            return jnp.concatenate((-x2, x1), axis=-1)
        key = jax.random.key(seed)
        k_x, k_wqkv, k_bqkv, k_wo, k_bo = jax.random.split(key, 5)
        C = EMBED_DIM
        x = jax.random.normal(k_x, (4, 256, C), dtype=jnp.float32)
        s = 1.0 / np.sqrt(C)
        W_qkv = jax.random.uniform(k_wqkv, (C, 3 * C), minval=-s, maxval=s, dtype=jnp.float32)
        b_qkv = jax.random.uniform(k_bqkv, (3 * C,), minval=-s, maxval=s, dtype=jnp.float32)
        W_out = jax.random.uniform(k_wo, (C, C), minval=-s, maxval=s, dtype=jnp.float32)
        b_out = jax.random.uniform(k_bo, (C,), minval=-s, maxval=s, dtype=jnp.float32)
        return {'x': x, 'W_qkv': W_qkv, 'b_qkv': b_qkv, 'W_out': W_out, 'b_out': b_out}
    _L0_attn_in = _L0_attn_setup()

    def _L0_ffn_setup():
        import jax, jax.numpy as jnp
        import numpy as np
        B, S, H = (2, 128, 128)
        E, F = (16, 64)
        G, TOPK_G, TOPK = (4, 2, 4)
        N_SHARED = 2
        ROUTE_SCALE = 1.0
        FS = N_SHARED * F

        def _gate(x, w_gate):
            T = x.shape[0]
            scores = jax.nn.sigmoid(x @ w_gate.T)
            sv = scores.reshape(T, G, E // G)
            group_scores = jax.lax.top_k(sv, 2)[0].sum(-1)
            top_groups = jax.lax.top_k(group_scores, TOPK_G)[1]
            allowed = jnp.zeros((T, G), dtype=bool).at[jnp.arange(T)[:, None], top_groups].set(True)
            masked = jnp.where(allowed[:, :, None], sv, -jnp.inf).reshape(T, E)
            _, idx = jax.lax.top_k(masked, TOPK)
            w = jnp.take_along_axis(scores, idx, axis=1)
            w = w / (w.sum(-1, keepdims=True) + 1e-06) * ROUTE_SCALE
            return (w, idx)

        def _swiglu(x, w1, w3, w2):
            return jax.nn.silu(x @ w1.T) * (x @ w3.T) @ w2.T
        key = jax.random.key(seed)
        ks = jax.random.split(key, 8)
        scale = 0.02
        return {'hidden_states': jax.random.normal(ks[0], (B, S, H), dtype=jnp.float32), 'w_gate': jax.random.normal(ks[1], (E, H), dtype=jnp.float32) * scale, 'w1_e': jax.random.normal(ks[2], (E, F, H), dtype=jnp.float32) * scale, 'w3_e': jax.random.normal(ks[3], (E, F, H), dtype=jnp.float32) * scale, 'w2_e': jax.random.normal(ks[4], (E, H, F), dtype=jnp.float32) * scale, 'w1_s': jax.random.normal(ks[5], (FS, H), dtype=jnp.float32) * scale, 'w3_s': jax.random.normal(ks[6], (FS, H), dtype=jnp.float32) * scale, 'w2_s': jax.random.normal(ks[7], (H, FS), dtype=jnp.float32) * scale}
    _L0_ffn_in = _L0_ffn_setup()

    def _L1_attn_setup():
        import jax, jax.numpy as jnp
        import numpy as np
        INV_SQRT_M = 1.0 / np.sqrt(256.0).astype(np.float32)

        def _kernel_features(x, random_matrix):
            x_proj = jnp.einsum('bhsd,dm->bhsm', x, random_matrix)
            return (jax.nn.elu(x_proj) + 1.0) * INV_SQRT_M
        key = jax.random.key(seed)
        ks = jax.random.split(key, 7)
        B, S, D, H, M = (4, 512, 128, 16, 32)
        hd = D // H
        std = 1.0 / np.sqrt(D)
        return {'x': jax.random.normal(ks[0], (B, S, D), jnp.float32), 'Wq': jax.random.normal(ks[1], (D, D), jnp.float32) * std, 'bq': jnp.zeros((D,), jnp.float32), 'Wk': jax.random.normal(ks[2], (D, D), jnp.float32) * std, 'bk': jnp.zeros((D,), jnp.float32), 'Wv': jax.random.normal(ks[3], (D, D), jnp.float32) * std, 'bv': jnp.zeros((D,), jnp.float32), 'Wo': jax.random.normal(ks[4], (D, D), jnp.float32) * std, 'bo': jnp.zeros((D,), jnp.float32), 'random_matrix': jax.random.normal(ks[5], (hd, M), jnp.float32)}
    _L1_attn_in = _L1_attn_setup()

    def _L1_ffn_setup():
        import jax, jax.numpy as jnp
        import numpy as np
        TOP_K = 2
        EPS = 1e-06
        key = jax.random.key(seed)
        ks = jax.random.split(key, 6)
        B_, T, D = (8, 256, 128)
        E, R_ = (8, 16)
        scale = 1.0 / np.sqrt(D)
        x = jax.random.normal(ks[0], (B_, T, D), dtype=jnp.float32)
        W = jax.random.normal(ks[1], (D, D), dtype=jnp.float32) * scale
        b = jax.random.normal(ks[2], (D,), dtype=jnp.float32)
        R = jax.random.normal(ks[3], (E, D), dtype=jnp.float32) * scale
        A = jax.random.normal(ks[4], (E, R_, D), dtype=jnp.float32) * scale
        B = jax.random.normal(ks[5], (D, R_), dtype=jnp.float32)[None] * jnp.ones((E, 1, 1), jnp.float32)
        B = jax.random.normal(ks[5], (E, D, R_), dtype=jnp.float32) * (1.0 / np.sqrt(R_))
        return {'x': x, 'W': W, 'b': b, 'R': R, 'A': A, 'B': B}
    _L1_ffn_in = _L1_ffn_setup()
    _d = {'L0_attn_x': _L0_attn_in['x'], 'L0_attn_W_qkv': _L0_attn_in['W_qkv'], 'L0_attn_b_qkv': _L0_attn_in['b_qkv'], 'L0_attn_W_out': _L0_attn_in['W_out'], 'L0_attn_b_out': _L0_attn_in['b_out'], 'L0_ffn_w_gate': _L0_ffn_in['w_gate'], 'L0_ffn_w1_e': _L0_ffn_in['w1_e'], 'L0_ffn_w3_e': _L0_ffn_in['w3_e'], 'L0_ffn_w2_e': _L0_ffn_in['w2_e'], 'L0_ffn_w1_s': _L0_ffn_in['w1_s'], 'L0_ffn_w3_s': _L0_ffn_in['w3_s'], 'L0_ffn_w2_s': _L0_ffn_in['w2_s'], 'L1_attn_Wq': _L1_attn_in['Wq'], 'L1_attn_bq': _L1_attn_in['bq'], 'L1_attn_Wk': _L1_attn_in['Wk'], 'L1_attn_bk': _L1_attn_in['bk'], 'L1_attn_Wv': _L1_attn_in['Wv'], 'L1_attn_bv': _L1_attn_in['bv'], 'L1_attn_Wo': _L1_attn_in['Wo'], 'L1_attn_bo': _L1_attn_in['bo'], 'L1_attn_random_matrix': _L1_attn_in['random_matrix'], 'L1_ffn_W': _L1_ffn_in['W'], 'L1_ffn_b': _L1_ffn_in['b'], 'L1_ffn_R': _L1_ffn_in['R'], 'L1_ffn_A': _L1_ffn_in['A'], 'L1_ffn_B': _L1_ffn_in['B']}
    _x0 = _d['L0_attn_x']
    _d['L0_attn_x'] = jax.random.normal(jax.random.fold_in(jax.random.key(seed), 1), (4, 512, 128), dtype=_x0.dtype)
    del _x0
    return _d

def reference(L0_attn_x, L0_attn_W_qkv, L0_attn_b_qkv, L0_attn_W_out, L0_attn_b_out, L0_ffn_w_gate, L0_ffn_w1_e, L0_ffn_w3_e, L0_ffn_w2_e, L0_ffn_w1_s, L0_ffn_w3_s, L0_ffn_w2_s, L1_attn_Wq, L1_attn_bq, L1_attn_Wk, L1_attn_bk, L1_attn_Wv, L1_attn_bv, L1_attn_Wo, L1_attn_bo, L1_attn_random_matrix, L1_ffn_W, L1_ffn_b, L1_ffn_R, L1_ffn_A, L1_ffn_B):

    def _L0_attn_ref(x, W_qkv, b_qkv, W_out, b_out):
        import jax, jax.numpy as jnp
        import numpy as np
        EMBED_DIM = 128
        NUM_HEADS = 16
        HEAD_DIM = EMBED_DIM // NUM_HEADS
        ROPE_BASE = 10000.0

        def rotate_half(x):
            d = x.shape[-1] // 2
            x1, x2 = (x[..., :d], x[..., d:])
            return jnp.concatenate((-x2, x1), axis=-1)
        B, T, C = x.shape
        H, Dh = (NUM_HEADS, HEAD_DIM)
        qkv = (x @ W_qkv + b_qkv).reshape(B, T, 3, H, Dh).transpose(2, 0, 3, 1, 4)
        q, k, v = (qkv[0], qkv[1], qkv[2])
        inv_freq = 1.0 / ROPE_BASE ** (jnp.arange(0, Dh, 2, dtype=jnp.float32) / Dh)
        freqs = jnp.arange(T, dtype=jnp.float32)[:, None] * inv_freq[None, :]
        emb = jnp.concatenate((freqs, freqs), axis=-1)
        cos, sin = (jnp.cos(emb), jnp.sin(emb))
        q = q * cos + rotate_half(q) * sin
        k = k * cos + rotate_half(k) * sin
        scale = 1.0 / np.sqrt(Dh)
        attn = jax.nn.softmax(jnp.einsum('bhqd,bhkd->bhqk', q, k) * scale, axis=-1)
        out = jnp.einsum('bhqk,bhkd->bhqd', attn, v)
        out = out.transpose(0, 2, 1, 3).reshape(B, T, C)
        return out @ W_out + b_out

    def _L0_ffn_ref(hidden_states, w_gate, w1_e, w3_e, w2_e, w1_s, w3_s, w2_s):
        import jax, jax.numpy as jnp
        import numpy as np
        B, S, H = (2, 128, 128)
        E, F = (16, 64)
        G, TOPK_G, TOPK = (4, 2, 4)
        N_SHARED = 2
        ROUTE_SCALE = 1.0
        FS = N_SHARED * F

        def _gate(x, w_gate):
            T = x.shape[0]
            scores = jax.nn.sigmoid(x @ w_gate.T)
            sv = scores.reshape(T, G, E // G)
            group_scores = jax.lax.top_k(sv, 2)[0].sum(-1)
            top_groups = jax.lax.top_k(group_scores, TOPK_G)[1]
            allowed = jnp.zeros((T, G), dtype=bool).at[jnp.arange(T)[:, None], top_groups].set(True)
            masked = jnp.where(allowed[:, :, None], sv, -jnp.inf).reshape(T, E)
            _, idx = jax.lax.top_k(masked, TOPK)
            w = jnp.take_along_axis(scores, idx, axis=1)
            w = w / (w.sum(-1, keepdims=True) + 1e-06) * ROUTE_SCALE
            return (w, idx)

        def _swiglu(x, w1, w3, w2):
            return jax.nn.silu(x @ w1.T) * (x @ w3.T) @ w2.T
        shape = hidden_states.shape
        x = hidden_states.reshape(-1, H)
        weights, idx = _gate(x, w_gate)
        combine = (jax.nn.one_hot(idx, E, dtype=x.dtype) * weights[..., None]).sum(1)
        g = jax.nn.silu(jnp.einsum('th,efh->tef', x, w1_e))
        u = jnp.einsum('th,efh->tef', x, w3_e)
        routed = jnp.einsum('tef,ehf,te->th', g * u, w2_e, combine)
        shared = _swiglu(x, w1_s, w3_s, w2_s)
        return (routed + shared).reshape(shape)

    def _L1_attn_ref(x, Wq, bq, Wk, bk, Wv, bv, Wo, bo, random_matrix):
        import jax, jax.numpy as jnp
        import numpy as np
        INV_SQRT_M = 1.0 / np.sqrt(256.0).astype(np.float32)

        def _kernel_features(x, random_matrix):
            x_proj = jnp.einsum('bhsd,dm->bhsm', x, random_matrix)
            return (jax.nn.elu(x_proj) + 1.0) * INV_SQRT_M
        B, S, D = x.shape
        hd, M = random_matrix.shape
        H = D // hd
        q = (x @ Wq + bq).reshape(B, S, H, hd).transpose(0, 2, 1, 3)
        k = (x @ Wk + bk).reshape(B, S, H, hd).transpose(0, 2, 1, 3)
        v = (x @ Wv + bv).reshape(B, S, H, hd).transpose(0, 2, 1, 3)
        q_prime = _kernel_features(q, random_matrix)
        k_prime = _kernel_features(k, random_matrix)
        kv = jnp.einsum('bhsm,bhsd->bhmd', k_prime, v)
        k_sum = k_prime.sum(axis=2)
        out = jnp.einsum('bhsm,bhmd->bhsd', q_prime, kv)
        normalizer = jnp.einsum('bhsm,bhm->bhs', q_prime, k_sum)[..., None]
        normalizer = jnp.maximum(normalizer, 1e-06)
        out = out / normalizer
        out = out.transpose(0, 2, 1, 3).reshape(B, S, D)
        return out @ Wo + bo

    def _L1_ffn_ref(x, W, b, R, A, B):
        import jax, jax.numpy as jnp
        import numpy as np
        TOP_K = 2
        EPS = 1e-06
        base_out = jnp.einsum('btd,od->bto', x, W) + b
        logits = jnp.einsum('btd,ed->bte', x, R)
        gate = jax.nn.softmax(logits, axis=-1)
        E = gate.shape[-1]
        _, idx = jax.lax.top_k(gate, TOP_K)
        mask = jax.nn.one_hot(idx, E, dtype=gate.dtype).sum(axis=-2)
        gate = gate * mask
        gate = gate / (gate.sum(axis=-1, keepdims=True) + EPS)
        h = jnp.einsum('btd,erd->bter', x, A)
        gh = gate[..., None] * h
        lora_out = jnp.einsum('bter,eor->bto', gh, B)
        return base_out + lora_out
    x = L0_attn_x
    x = _layernorm(x + _L0_attn_ref(x, L0_attn_W_qkv, L0_attn_b_qkv, L0_attn_W_out, L0_attn_b_out), axis=-1)
    x = _layernorm(x + _L0_ffn_ref(x, L0_ffn_w_gate, L0_ffn_w1_e, L0_ffn_w3_e, L0_ffn_w2_e, L0_ffn_w1_s, L0_ffn_w3_s, L0_ffn_w2_s), axis=-1)
    x = _layernorm(x + _L1_attn_ref(x, L1_attn_Wq, L1_attn_bq, L1_attn_Wk, L1_attn_bk, L1_attn_Wv, L1_attn_bv, L1_attn_Wo, L1_attn_bo, L1_attn_random_matrix), axis=-1)
    x = _layernorm(x + _L1_ffn_ref(x, L1_ffn_W, L1_ffn_b, L1_ffn_R, L1_ffn_A, L1_ffn_B), axis=-1)
    return x

_drawn_inputs = setup_inputs


def setup_inputs(seed=0):
    import zlib

    import numpy as np

    out = dict(_drawn_inputs(seed))
    spreads = {'L1_attn_bq': (0.0, 0.371),
     'L1_attn_bk': (0.0, 0.648),
     'L1_attn_bv': (0.0, 0.1),
     'L1_attn_bo': (0.0, 0.1)}
    factors = {'L0_ffn_w_gate': 3.929,
     'L0_ffn_w1_e': 5.153,
     'L0_ffn_w3_e': 4.19,
     'L0_ffn_w2_e': 3.74,
     'L0_ffn_w3_s': 3.48,
     'L0_ffn_w2_s': 2.922}
    for name, (base, spread) in spreads.items():
        noise = np.random.default_rng([zlib.crc32(name.encode()), seed]).standard_normal(out[name].shape)
        drawn = base * np.exp(spread * noise) if base else spread * noise
        out[name] = jnp.asarray(drawn.astype(out[name].dtype))
    for name, factor in factors.items():
        out[name] = (out[name] * factor).astype(out[name].dtype)
    return out
```

```python
from contextlib import ExitStack

import numpy as np

import concourse.bass as bass
from concourse import mybir

P = 128
F32 = mybir.dt.float32
BF16 = mybir.dt.bfloat16
ALU = mybir.AluOpType
ACT = mybir.ActivationFunctionType
X = mybir.AxisListType.X

NB, T, D = 4, 512, 128
NT = T // P
H, DH = 16, 8
HG = 4
NG = H // HG
GROUPS = NB * NG
SLOTS = 9
KROW = 96
E0, F0, EP = 16, 64, 8
E1, R1 = 8, 16
M1 = 32
KVW = HG * DH + HG
LN_EPS = 1e-5

EARLY = dict(w_qkv=5 * D, b_rope=4, cos=T, sin=T, ident=P, bv_row=D)
LATE = dict(w_out=D, bout_row=D, wg=E0, w1=E0 * F0, w3=E0 * F0, w2=EP * D, w1s=D, w3s=D, w2s=D, reset16=NT * E0,
            wqT=D, wkT=D, wv1=D, wo1=D, rbd=H * M1, bq_col=1, bk_rep=P, bv1_row=D, bo1_row=D, mask=KVW,
            lr=E1, la=E1 * R1, lw=D, lb=D, lb_row=D, reset8=NT * E1)


def columns(widths):
    at, out = 0, {}
    for name, n in widths.items():
        out[name] = (at, at + n)
        at += n
    return out, at


EARLY_AT, EARLY_N = columns(EARLY)
LATE_AT, LATE_N = columns(LATE)


def program(nc, x_in, xT_in, early_in, late_in, sel_in, identb_in, parts_dram, out):
    with ExitStack() as ctx:
        def sb(name, shape, dt=F32):
            return ctx.enter_context(nc.sbuf_tensor(name, shape, dt))

        def sem(name):
            return ctx.enter_context(nc.semaphore(name))

        early = sb("early", [P, EARLY_N])
        late = sb("late", [P, LATE_N])
        c_ = {k: early[:, a:b] for k, (a, b) in EARLY_AT.items()}
        c_.update({k: late[:, a:b] for k, (a, b) in LATE_AT.items()})
        ident = c_["ident"]
        identb = sb("identb", [P, P], BF16)
        sel = sb("sel", [3 * E0, EP, P], BF16)
        xT = sb("xT", [P, NB * T])
        res = sb("res", [P, NB * NT, D])
        z = sb("z", [P, 2, NT, D])
        rot = sb("rot", [P, 4, T])
        parts = sb("parts", [P, 2, 3, T], BF16)
        QS = [sb(f"QS{i}", [P, H, T], BF16) for i in range(2)]
        KS = [sb(f"KS{i}", [P, H, T], BF16) for i in range(2)]
        VA = [sb(f"VA{i}", [P, NT, H, 32]) for i in range(2)]
        probs = sb("probs", [P, 2, HG, T])
        OU = sb("OU", [P, 2, NG, T])
        negmax = sb("negmax", [P, 4, HG * NT])
        maxT = sb("maxT", [HG * NT, 2, P])
        maxp = sb("maxp", [HG * NT, 2, 3, P], BF16)
        rden = sb("rden", [P, NT, H])
        attn = sb("attn", [P, 2, NT, D])
        attnT = sb("attnT", [P, T])
        stats = sb("stats", [P, NT, 6])
        mv = sb("mv", [P, NB, NT, 2])
        var = sb("var", [P, NB, NT])
        rstd = sb("rstd", [P, NB, NT])
        minus_half = sb("minus_half", [P, NT])
        minus1 = sb("minus1", [P, 1])
        rt = sb("rt", [P, 24, NT * E0])
        cT = sb("cT", [3 * E0, NB, T], BF16)
        cparts = sb("cparts", [P, NT, 3 * E0], BF16)
        qb = sb("qb", [P, NT])
        qb1 = sb("qb1", [P, NT])
        kparts = sb("kparts", [1, 3, H * M1], BF16)
        kstack = sb("kstack", [3, H * M1], BF16)
        onesb = sb("onesb", [3, P], BF16)
        V36 = sb("V36", [P, NT, NG, KVW])
        KVB = sb("KVB", [P, NG, KVW])
        A0, A1 = (q[:, :, :].rearrange("p h t -> p (h t)").bitcast(F32) for q in QS)
        B0, B1 = (k[:, :, :].rearrange("p h t -> p (h t)").bitcast(F32) for k in KS)
        gate_s = A0[:, 0:2 * T].rearrange("p (i t) -> p i t", t=T)
        prod = A0[:, 2 * T:4 * T].rearrange("p (i t) -> p i t", t=T)
        hid = A0[:, 4 * T:7 * T].rearrange("p (i t) -> p i t", t=T)
        eq_ = B0[:, 0:2 * T].rearrange("p (i t) -> p i t", t=T)
        ek_ = B0[:, 2 * T:4 * T].rearrange("p (i t) -> p i t", t=T)
        mq_ = B0[:, 4 * T:6 * T].rearrange("p (i t) -> p i t", t=T)
        gh = B0[:, 6 * T:7 * T].rearrange("p (n d) -> p n d", n=NT)
        ghT = B0[:, 7 * T:8 * T]
        QF = A1.rearrange("p (i c t) -> p i c t", i=2, c=NT)
        KF = B1[:, 0:4 * T].rearrange("p (n f) -> p n f", n=NT)
        outb = B1[:, 4 * T:8 * T].rearrange("p (n d) -> p n d", d=D)
        wqR, wkR, kbias = (probs[:, 0, i, :] for i in range(3))
        gate8 = sb("gate8", [P, NT, E1])

        ps = [ctx.enter_context(nc.psum_tensor(f"ps{i}", [P, 512], F32)) for i in range(8)]

        x_ld, early_ld, late_ld, init = (sem(n) for n in ("x_ld", "early_ld", "late_ld", "init"))
        sm_full, sm_free, s_full, exp_done, pv_done, o_evac = (
            sem(n) for n in ("sm_full", "sm_free", "s_full", "exp_done", "pv_done", "o_evac"))
        ps_full = [sem(f"ps_full{i}") for i in range(8)]
        ps_free = [sem(f"ps_free{i}") for i in range(8)]
        rot_done, split_done, parts_st, v_done, maxT_done, maxp_done = (
            sem(n) for n in ("rot_done", "split_done", "parts_st", "v_done", "maxT_done", "maxp_done"))
        qk_ld = [sem(f"qk_ld{i}") for i in range(2)]
        maxrow_ld = [sem(f"maxrow_ld{i}") for i in range(2)]
        attn_done, attnT_done, res_done, resT_done = (sem(n) for n in ("attn_done", "attnT_done", "res_done", "resT_done"))
        var_done = [sem(f"var_done{k}") for k in range(4)]
        rstd_done = [sem(f"rstd_done{k}") for k in range(4)]
        expneg_done, cparts_done, cT_done = (sem(n) for n in ("expneg_done", "cparts_done", "cT_done"))
        silu_done, hid_done, down_done = (sem(n) for n in ("silu_done", "hid_done", "down_done"))
        dve_chain, pool_chain, act_chain = (sem(n) for n in ("dve_chain", "pool_chain", "act_chain"))
        wr_done, row_done, kb_done, ks_ld, expq_done, minq_done, qf_done, expk_done, kf_done, v36_done, kvb_done = (
            sem(n) for n in ("wr_done", "row_done", "kb_done", "ks_ld", "expq_done", "minq_done", "qf_done", "expk_done", "kf_done",
                             "v36_done", "kvb_done"))
        lsub_done, lexp_done, gh_done, ghT_done, store_in, stored, bias_done = (
            sem(n) for n in ("lsub_done", "lexp_done", "gh_done", "ghT_done", "store_in", "stored", "bias_done"))

        MISC = 7
        HALVES = GROUPS * NT * 2
        slots = [[] for _ in range(HALVES)]
        prologue = [("rope", 0, 0), ("rope", 0, 1), ("rope", 0, 2), ("rope", 0, 3), ("val", 0, 0), ("max", 0, 0)]
        for b in range(NB):
            w = 32 * b
            if b + 1 < NB:
                for m in range(4):
                    slots[w + m].append(("rope", b + 1, m))
                slots[w + 4].append(("val", b + 1, 0))
            for g in range(4):
                if 4 * b + g + 1 < GROUPS:
                    slots[w + 8 * g + 5].append(("max", 4 * b + g + 1, 0))
            if b:
                for i, s in enumerate((6, 8, 10, 12)):
                    slots[w + s].append(("heads", b - 1, i))
                for kind, s in (("attnT", 14), ("proj", 16), ("resT", 20), ("gate", 22), ("combine", 28)):
                    slots[w + s].append((kind, b - 1, 0))
        last = NB - 1
        epilogue = [("heads", last, i) for i in range(4)] + [(k, last, 0) for k in ("attnT", "proj", "resT", "gate", "combine")]
        misc = prologue + [s for one in slots for s in one] + epilogue

        uses = [[] for _ in range(8)]
        uses[MISC] = [("m",) + s for s in misc]
        PAIRS = EP + 1
        for i in range(NB * PAIRS):
            uses[i % 2].append(("gate_e", i))
            uses[2 + i % 2].append(("up_e", i))
            if i % PAIRS < EP:
                uses[4].append(("comb_e", i))
        for b in range(NB):
            uses[6].append(("y_e", b))
        pieces2 = []
        for b in range(NB):
            pieces2 += [("moe", b)]
            if b:
                pieces2 += [("x2T", b - 1)]
        pieces2 += [("x2T", NB - 1)]
        for k, b in pieces2:
            if k == "x2T":
                uses[MISC].append(("x2T", b))
        uses[0].append(("wqR", 0))
        uses[1].append(("wkR", 0))
        uses[2].append(("qb", 0))
        uses[3].append(("kb", 0))
        pieces3 = [("L", 0), ("L", 1), ("M", 0), ("N", 0), ("L", 2), ("M", 1), ("R", 0), ("N", 1), ("L", 3), ("M", 2),
                   ("R", 1), ("N", 2), ("M", 3), ("R", 2), ("N", 3), ("R", 3)]
        for k, b in pieces3:
            if k == "L":
                for c in range(4):
                    uses[c % 2].append(("Q", b, c))
                    uses[2 + c % 2].append(("K", b, c))
                uses[4].append(("V", b))
                uses[5].append(("KV", b))
                uses[6].append(("O", b, 0))
                uses[6].append(("O", b, 1))
            if k == "M":
                uses[7].append(("AT", b))
                uses[4].append(("Y1", b))
            if k == "N":
                uses[7].append(("x3T", b))
                uses[5].append(("lg", b))
                uses[6].append(("lh", b))
            if k == "R":
                uses[7].append(("ghT", b))
                uses[4].append(("Y2", b))
        turn = {u: (bank, n) for bank in range(8) for n, u in enumerate(uses[bank])}

        def bank_of(u):
            return ps[turn[u][0]]

        def wait_free(eng, u):
            bank, n = turn[u]
            if n:
                eng.wait_ge(ps_free[bank], n)

        def wait_full(eng, u):
            bank, n = turn[u]
            eng.wait_ge(ps_full[bank], n + 1)

        def fullness(u):
            return ps_full[turn[u][0]]

        def freedom(u):
            return ps_free[turn[u][0]]

        block = ctx.enter_context(nc.Block())

        @block.sync
        def _(sp):
            sp.dma_start(early[:, :], early_in).then_inc(early_ld, 16)
            sp.dma_start(xT[:, 0:T], xT_in[:, 0:T]).then_inc(early_ld, 16)
            sp.dma_start(xT[:, T:], xT_in[:, T:]).then_inc(x_ld, 16)
            sp.dma_start(res[:, :, :], x_in.rearrange("(n p) d -> p n d", p=P)).then_inc(x_ld, 16)
            sp.dma_start(late[:, :], late_in).then_inc(late_ld, 16)
            sp.dma_start(sel[:, :, :], sel_in).then_inc(late_ld, 16)
            sp.dma_start(identb[:, :], identb_in).then_inc(late_ld, 16)

            def load_stacks(b):
                for i in range(2):
                    sp.wait_ge(split_done, 2 * b + i + 1)
                    sp.dma_start(parts_dram[b, i], parts[:, i, :, :]).then_inc(parts_st, 16)
                    sp.wait_ge(parts_st, 16 * (2 * b + i + 1))
                    if b >= 2 and i == 0:
                        sp.wait_ge(s_full, 32 * (b - 1))
                    if b < 2 and i == 0:
                        sp.wait_ge(init, 1)
                    src = parts_dram[b, i].rearrange("(h d) p t -> p d h t", d=DH)
                    for s in range(SLOTS):
                        part = s // 3 if i == 0 else s % 3
                        dst = (QS, KS)[i][b % 2]
                        sp.dma_start(dst[s * DH:(s + 1) * DH, :, :], src[part]).then_inc(qk_ld[b % 2], 16)

            def load_max(G):
                sp.wait_ge(maxp_done, G + 1)
                if G >= 2:
                    sp.wait_ge(maxrow_ld[G % 2], 48 * (G // 2))
                g = G % NG
                for i in range(3):
                    dst = QS[(G // NG) % 2][KROW + i:KROW + i + 1, HG * g:HG * (g + 1), :]
                    sp.dma_start(dst.rearrange("i h (q t) -> i (h q) t", q=NT), maxp[:, G % 2, i, :])\
                        .then_inc(maxrow_ld[G % 2], 16)

            load_stacks(0)
            load_max(0)
            for w in range(HALVES):
                for kind, a, m in slots[w]:
                    if kind == "max":
                        load_max(a)
                    if kind == "rope" and m == 3:
                        load_stacks(a)
            sp.wait_ge(kb_done, 1)
            for i in range(3):
                sp.dma_start(kstack[i:i + 1, :], kparts[0:1, i, :]).then_inc(ks_ld, 16)
            for b in range(NB):
                sp.wait_ge(store_in, b + 1)
                sp.dma_start(out[b * T:(b + 1) * T, :].rearrange("(n p) d -> p n d", p=P),
                             outb[:, b * NT:(b + 1) * NT, :]).then_inc(stored, 16)
            sp.wait_ge(stored, 16 * NB)

        @block.gpsimd
        def _(pool):
            n = [0]

            def link(ins):
                n[0] += 1
                ins.then_inc(pool_chain, 1)
                pool.wait_ge(pool_chain, n[0])

            for t in QS + KS:
                link(nc.gpsimd.memset(t[64:KROW, :, :].rearrange("p a b -> p (a b)"), 0.0))
            for t in KS:
                link(nc.gpsimd.memset(t[KROW:P, :, :].rearrange("p a b -> p (a b)"), 1.0))
            link(nc.gpsimd.memset(minus_half[:, :], -0.5))
            link(nc.gpsimd.memset(onesb[:, :], 1.0))
            nc.gpsimd.memset(V36[:, :, :, :], 1.0).then_inc(init, 1)
            pool.wait_ge(init, 1)

            def rope_split(b, i):
                pool.wait_ge(rot_done, 4 * b + 2 * i + 2)
                if b:
                    pool.wait_ge(parts_st, 16 * (2 * (b - 1) + i + 1))
                v = rot[:, 2 * i, :]
                link(nc.gpsimd.tensor_tensor(out=v, in0=rot[:, 2 * i, :], in1=rot[:, 2 * i + 1, :], op=ALU.add))
                link(nc.gpsimd.tensor_scalar(parts[:, i, 0, :], v, 1.0, None, ALU.mult))
                link(nc.gpsimd.tensor_tensor(out=v, in0=v, in1=parts[:, i, 0, :], op=ALU.subtract))
                link(nc.gpsimd.tensor_scalar(parts[:, i, 1, :], v, 1.0, None, ALU.mult))
                nc.gpsimd.tensor_tensor(out=parts[:, i, 2, :], in0=v, in1=parts[:, i, 1, :],
                                        op=ALU.subtract).then_inc(split_done, 1)

            def max_split(G):
                pool.wait_ge(maxT_done, G + 1)
                if G >= 2:
                    pool.wait_ge(maxrow_ld[G % 2], 48 * (G // 2))
                v = maxT[:, G % 2, :]
                o = maxp[:, G % 2, :, :]
                link(nc.gpsimd.tensor_scalar(o[:, 0, :], v, 1.0, None, ALU.mult))
                link(nc.gpsimd.tensor_tensor(out=v, in0=v, in1=o[:, 0, :], op=ALU.subtract))
                link(nc.gpsimd.tensor_scalar(o[:, 1, :], v, 1.0, None, ALU.mult))
                nc.gpsimd.tensor_tensor(out=o[:, 2, :], in0=v, in1=o[:, 1, :], op=ALU.subtract).then_inc(maxp_done, 1)

            def rstd_of(k, b):
                pool.wait_ge(var_done[k], b + 1)
                nc.gpsimd.tensor_tensor(out=rstd[:, b, :], in0=var[:, b, :], in1=minus_half[:, :],
                                        op=ALU.pow).then_inc(rstd_done[k], 1)

            def add_row(name, b, count):
                v = res[:, b * NT:(b + 1) * NT, :]
                nc.gpsimd.tensor_tensor(out=v, in0=v, in1=c_[name].unsqueeze(1).to_broadcast([P, NT, D]),
                                        op=ALU.add).then_inc(bias_done, 1)

            def misc_pool(kind, a, m):
                if kind == "rope" and m % 2 == 1:
                    rope_split(a, m // 2)
                if kind == "max":
                    max_split(a)
                if kind == "proj":
                    rstd_of(0, a)

            for s in prologue:
                misc_pool(*s)
            pool.wait_ge(x_ld, 32)
            pool.wait_ge(late_ld, 48)
            for b in range(NB):
                add_row("bout_row", b, 0)
            for w in range(HALVES):
                for s in slots[w]:
                    misc_pool(*s)
            for s in epilogue:
                misc_pool(*s)
            for b in range(NB):
                rstd_of(1, b)
            for b in range(NB):
                pool.wait_ge(resT_done, NB + b + 1)
                add_row("bo1_row", b, 1)
            for k, b in pieces3:
                if k == "L":
                    for c in range(4):
                        i = 4 * b + c
                        pool.wait_ge(expq_done, i + 1)
                        if i >= 2:
                            pool.wait_ge(qf_done, i - 1)
                        nc.gpsimd.tensor_scalar(mq_[:, i % 2, :], eq_[:, i % 2, :], 1.0, None,
                                                ALU.min).then_inc(minq_done, 1)
                if k == "M":
                    rstd_of(2, b)
                if k == "N":
                    pool.wait_ge(resT_done, 2 * NB + b + 1)
                    add_row("lb_row", b, 2)
                if k == "R":
                    rstd_of(3, b)

        @block.tensor
        def _(pe):
            mm = nc.tensor.matmul
            tr = nc.tensor.transpose

            def scores_for_max(u):
                G, i = divmod(u, HG * NT)
                b, h, qt = G // NG, HG * (G % NG) + i // NT, i % NT
                if i == 0 and G % NG == 0:
                    pe.wait_ge(qk_ld[b % 2], 2 * SLOTS * 16 * (b // 2 + 1))
                if u >= 2:
                    pe.wait_ge(sm_free, u - 1)
                mm(ps[4 + u % 2][:, :], QS[b % 2][0:KROW, h, qt * P:(qt + 1) * P], KS[b % 2][0:KROW, h, :],
                   start=True, stop=True).then_inc(sm_full, 1)

            def scores(w):
                n, hf = divmod(w, 2)
                G, kt = divmod(n, NT)
                b = G // NG
                if kt == 0 and hf == 0:
                    pe.wait_ge(maxrow_ld[G % 2], 48 * (G // 2 + 1))
                if w >= 2:
                    pe.wait_ge(exp_done, w - 1)
                for j in range(2):
                    h = HG * (G % NG) + 2 * hf + j
                    last = mm(S4[2 * hf + j], KS[b % 2][0:KROW + 3, h, kt * P:(kt + 1) * P],
                              QS[b % 2][0:KROW + 3, h, :], start=True, stop=True)
                last.then_inc(s_full, 1)

            def values(n):
                G, kt = divmod(n, NT)
                b = G // NG
                pe.wait_ge(exp_done, 2 * n + 2)
                if n % (NG * NT) == 0:
                    pe.wait_ge(v_done, b + 1)
                if kt == 0 and G:
                    pe.wait_ge(o_evac, G)
                for j in range(HG):
                    h = HG * (G % NG) + j
                    last = mm(ps[6][32 * j:32 * j + 32, :], VA[b % 2][:, kt, h, :], probs[:, n % 2, j, :],
                              start=(kt == 0), stop=(kt == NT - 1), tile_position=(0, 32 * j))
                last.then_inc(pv_done, 1)

            def misc_pe(kind, a, m):
                u = ("m", kind, a, m)
                o = ps[MISC]
                wait_free(pe, u)
                if kind == "rope":
                    if a == 1 and m == 0:
                        pe.wait_ge(x_ld, 32)
                    last = mm(o[:, :], c_["w_qkv"][:, m * D:(m + 1) * D], xT[:, a * T:(a + 1) * T], start=True, stop=True)
                if kind == "val":
                    for t in range(NT):
                        last = mm(o[:, t * D:(t + 1) * D], xT[:, a * T + t * P:a * T + (t + 1) * P],
                                  c_["w_qkv"][:, 4 * D:], start=True, stop=True)
                if kind == "max":
                    pe.wait_ge(sm_free, HG * NT * (a + 1))
                    last = mm(o[0:HG * NT, 0:P], negmax[:, a % 4, :], ident, start=True, stop=True)
                if kind == "heads":
                    if m == 0:
                        pe.wait_ge(o_evac, NG * (a + 1))
                    for g in range(NG):
                        last = tr(o[:, g * P:(g + 1) * P], OU[:, a % 2, g, m * P:(m + 1) * P], ident)
                if kind == "attnT":
                    pe.wait_ge(attn_done, NT * (a + 1))
                    for t in range(NT):
                        last = tr(o[:, t * P:(t + 1) * P], attn[:, a % 2, t, :], ident)
                if kind == "proj":
                    pe.wait_ge(attnT_done, a + 1)
                    if a == 0:
                        pe.wait_ge(late_ld, 48)
                    for t in range(NT):
                        last = mm(o[:, t * D:(t + 1) * D], attnT[:, t * P:(t + 1) * P], c_["w_out"], start=True, stop=True)
                if kind == "resT":
                    pe.wait_ge(res_done, a + 1)
                    for t in range(NT):
                        last = tr(o[:, t * P:(t + 1) * P], res[:, a * NT + t, :], ident)
                if kind == "gate":
                    pe.wait_ge(resT_done, a + 1)
                    for t in range(NT):
                        c = a * T + t * P
                        last = mm(o[:, t * E0:(t + 1) * E0], xT[:, c:c + P], c_["wg"], start=True, stop=True)
                if kind == "combine":
                    pe.wait_ge(cparts_done, a + 1)
                    for t in range(NT):
                        last = mm(o[0:3 * E0, t * P:(t + 1) * P], cparts[:, t, :], identb[:, :], start=True, stop=True)
                last.then_inc(ps_full[MISC], 1)

            S4 = [ps[i][:, :] for i in range(4)]
            pe.wait_ge(early_ld, 32)
            for s in prologue[:-1]:
                misc_pe(*s)
            for u in range(HG * NT):
                scores_for_max(u)
            misc_pe(*prologue[-1])
            for u in range(HG * NT, 2 * HG * NT):
                scores_for_max(u)
            scores(0)
            scores(1)
            for w in range(HALVES):
                if w + 2 < HALVES:
                    scores(w + 2)
                G = w // 8
                if G + 2 < GROUPS:
                    for i in range(2):
                        scores_for_max((G + 2) * HG * NT + 2 * (w % 8) + i)
                for s in slots[w]:
                    misc_pe(*s)
                if w % 2:
                    values(w // 2)
            for s in epilogue:
                misc_pe(*s)

            def down(i):
                b, p = divmod(i, PAIRS)
                pe.wait_ge(hid_done, i + 1)
                u = ("y_e", b)
                if p == 0:
                    if b == 0:
                        pe.wait_ge(o_evac, GROUPS)
                    wait_free(pe, u)
                w2 = c_["w2s"] if p == EP else c_["w2"][:, p * D:(p + 1) * D]
                for t in range(NT):
                    last = mm(ps[6][:, t * D:(t + 1) * D], hid[:, i % 3, t * P:(t + 1) * P], w2,
                              start=(p == 0 and t == 0), stop=(p == EP and t == NT - 1), skip_group_check=True)
                last.then_inc(down_done, 1)
                if p == EP:
                    pe.wait_ge(down_done, i + 1)
                    pe.sem_inc(fullness(u), 1)

            def transposed(u, b):
                wait_free(pe, u)
                for t in range(NT):
                    last = tr(ps[7][:, t * P:(t + 1) * P], res[:, b * NT + t, :], ident)
                last.then_inc(fullness(u), 1)

            pe.wait_ge(exp_done, HALVES)
            pe.wait_ge(sm_free, GROUPS * HG * NT)
            for k, b in pieces2:
                if k == "x2T":
                    pe.wait_ge(res_done, NB + b + 1)
                    transposed(("x2T", b), b)
                    continue
                for p in range(PAIRS):
                    i = b * PAIRS + p
                    xb = xT[:, b * T:(b + 1) * T]
                    for kind, w, ws in (("gate_e", "w1", "w1s"), ("up_e", "w3", "w3s")):
                        u = (kind, i)
                        wait_free(pe, u)
                        wt = c_[ws] if p == EP else c_[w][:, p * 2 * F0:(p + 1) * 2 * F0]
                        mm(bank_of(u)[:, :], wt, xb, start=True, stop=True).then_inc(fullness(u), 1)
                    if p < EP:
                        u = ("comb_e", i)
                        wait_free(pe, u)
                        if p == 0:
                            pe.wait_ge(cT_done, b + 1)
                        mm(bank_of(u)[:, :], sel[:, p, :], cT[:, b, :], start=True, stop=True).then_inc(fullness(u), 1)
                    if i:
                        down(i - 1)
                if b == NB - 1:
                    down(NB * PAIRS - 1)

            for u, w in ((("wqR", 0), "wqT"), (("wkR", 0), "wkT")):
                wait_free(pe, u)
                mm(bank_of(u)[:, :], c_[w], c_["rbd"], start=True, stop=True).then_inc(fullness(u), 1)
            u = ("qb", 0)
            wait_free(pe, u)
            for c in range(4):
                last = mm(bank_of(u)[:, c:c + 1], c_["rbd"][:, c * P:(c + 1) * P], c_["bq_col"], start=True, stop=True)
            last.then_inc(fullness(u), 1)
            u = ("kb", 0)
            wait_free(pe, u)
            mm(bank_of(u)[:, :], c_["bk_rep"], c_["rbd"], start=True, stop=True).then_inc(fullness(u), 1)
            pe.wait_ge(wr_done, 2)
            pe.wait_ge(row_done, 2)
            pe.wait_ge(ks_ld, 48)

            for k, b in pieces3:
                def tile_of(t):
                    return xT[:, b * T + t * P:b * T + (t + 1) * P]
                if k == "L":
                    pe.wait_ge(resT_done, NB + b + 1)
                    for c in range(4):
                        u = ("K", b, c)
                        wait_free(pe, u)
                        mm(bank_of(u)[:, :], tile_of(c), wkR[:, :], start=True, stop=False)
                        mm(bank_of(u)[:, :], onesb[:, :], kstack[:, :], start=False, stop=True).then_inc(fullness(u), 1)
                    u = ("V", b)
                    wait_free(pe, u)
                    for t in range(NT):
                        last = mm(bank_of(u)[:, t * D:(t + 1) * D], tile_of(t), c_["wv1"], start=True, stop=True)
                    last.then_inc(fullness(u), 1)
                    for c in range(4):
                        u = ("Q", b, c)
                        wait_free(pe, u)
                        mm(bank_of(u)[:, :], wqR[:, c * P:(c + 1) * P], xT[:, b * T:(b + 1) * T],
                           start=True, stop=True).then_inc(fullness(u), 1)
                    u = ("KV", b)
                    wait_free(pe, u)
                    pe.wait_ge(kf_done, 4 * (b + 1))
                    pe.wait_ge(v36_done, b + 1)
                    for c in range(4):
                        for t in range(NT):
                            last = mm(bank_of(u)[:, c * KVW:(c + 1) * KVW], KF[:, t, c * P:(c + 1) * P], V36[:, t, c, :],
                                      start=(t == 0), stop=(t == NT - 1))
                    last.then_inc(fullness(u), 1)
                    pe.wait_ge(kvb_done, b + 1)
                    pe.wait_ge(qf_done, 4 * (b + 1))
                    for tp in range(2):
                        u = ("O", b, tp)
                        wait_free(pe, u)
                        for t in range(2):
                            for c in range(4):
                                at = (t * 4 + c) * KVW
                                last = mm(bank_of(u)[:, at:at + KVW], QF[:, b % 2, c, (2 * tp + t) * P:(2 * tp + t + 1) * P],
                                          KVB[:, c, :], start=True, stop=True)
                        last.then_inc(fullness(u), 1)
                if k == "M":
                    u = ("AT", b)
                    pe.wait_ge(attn_done, NB * NT + 2 * (b + 1))
                    wait_free(pe, u)
                    for t in range(NT):
                        last = tr(bank_of(u)[:, t * P:(t + 1) * P], attn[:, b % 2, t, :], ident)
                    last.then_inc(fullness(u), 1)
                    u = ("Y1", b)
                    pe.wait_ge(attnT_done, NB + b + 1)
                    wait_free(pe, u)
                    for t in range(NT):
                        last = mm(bank_of(u)[:, t * D:(t + 1) * D], attnT[:, t * P:(t + 1) * P], c_["wo1"], start=True, stop=True)
                    last.then_inc(fullness(u), 1)
                if k == "N":
                    pe.wait_ge(res_done, 2 * NB + b + 1)
                    transposed(("x3T", b), b)
                    pe.wait_ge(resT_done, 2 * NB + b + 1)
                    u = ("lg", b)
                    wait_free(pe, u)
                    for t in range(NT):
                        last = mm(bank_of(u)[:, t * E1:(t + 1) * E1], tile_of(t), c_["lr"], start=True, stop=True)
                    last.then_inc(fullness(u), 1)
                    u = ("lh", b)
                    wait_free(pe, u)
                    for t in range(NT):
                        last = mm(bank_of(u)[:, t * P:(t + 1) * P], tile_of(t), c_["la"], start=True, stop=True)
                    last.then_inc(fullness(u), 1)
                if k == "R":
                    u = ("ghT", b)
                    pe.wait_ge(gh_done, b + 1)
                    wait_free(pe, u)
                    for t in range(NT):
                        last = tr(bank_of(u)[:, t * P:(t + 1) * P], gh[:, t, :], ident)
                    last.then_inc(fullness(u), 1)
                    u = ("Y2", b)
                    pe.wait_ge(ghT_done, b + 1)
                    wait_free(pe, u)
                    for t in range(NT):
                        mm(bank_of(u)[:, t * D:(t + 1) * D], tile_of(t), c_["lw"], start=True, stop=False)
                        last = mm(bank_of(u)[:, t * D:(t + 1) * D], ghT[:, t * P:(t + 1) * P], c_["lb"], start=False, stop=True)
                    last.then_inc(fullness(u), 1)

        @block.scalar
        def _(act):
            fn = nc.scalar.activation

            def exps(w):
                n, hf = divmod(w, 2)
                act.wait_ge(s_full, w + 1)
                if n >= 2:
                    act.wait_ge(pv_done, n - 1)
                for j in range(2):
                    last = fn(probs[:, n % 2, 2 * hf + j, :], ps[2 * hf + j][:, :], ACT.Exp, scale=float(DH) ** -0.5)
                last.then_inc(exp_done, 1)

            def outputs(G):
                b = G // NG
                act.wait_ge(pv_done, NT * (G + 1))
                if b >= 2 and G % NG == 0:
                    wait_full(act, ("m", "heads", b - 2, 3))
                fn(OU[:, b % 2, G % NG, :], ps[6][:, :], ACT.Copy).then_inc(o_evac, 1)

            def misc_act(kind, a, m):
                u = ("m", kind, a, m)
                o = ps[MISC]
                if kind == "max":
                    wait_full(act, u)
                    if a >= 2:
                        act.wait_ge(maxp_done, a - 1)
                    fn(maxT[:, a % 2, :], o[0:HG * NT, 0:P], ACT.Copy).then_inc(maxT_done, 1)
                    act.wait_ge(maxT_done, a + 1)
                    act.sem_inc(ps_free[MISC], 1)
                if kind == "attnT":
                    wait_full(act, u)
                    if a:
                        wait_full(act, ("m", "proj", a - 1, 0))
                    fn(attnT[:, :], o[:, :], ACT.Copy).then_inc(attnT_done, 1)
                    act.wait_ge(attnT_done, a + 1)
                    act.sem_inc(ps_free[MISC], 1)
                if kind == "resT":
                    wait_full(act, u)
                    fn(xT[:, a * T:(a + 1) * T], o[:, :], ACT.Copy).then_inc(resT_done, 1)
                    act.wait_ge(resT_done, a + 1)
                    act.sem_inc(ps_free[MISC], 1)
                if kind == "gate":
                    wait_full(act, u)
                    if a:
                        act.wait_ge(cparts_done, a)
                    fn(rt[:, 0, :], o[:, 0:NT * E0], ACT.Exp, scale=-1.0).then_inc(expneg_done, 1)
                    act.wait_ge(expneg_done, a + 1)
                    act.sem_inc(ps_free[MISC], 1)
                if kind == "combine":
                    wait_full(act, u)
                    fn(cT[:, a, :], o[0:3 * E0, :], ACT.Copy).then_inc(cT_done, 1)
                    act.wait_ge(cT_done, a + 1)
                    act.sem_inc(ps_free[MISC], 1)

            for s in prologue:
                misc_act(*s)
            for w in range(HALVES):
                exps(w)
                if w % 8 == 1 and w > 8:
                    outputs(w // 8 - 1)
                for s in slots[w]:
                    misc_act(*s)
            outputs(GROUPS - 1)
            for s in epilogue:
                misc_act(*s)

            def transposed(u, b, k):
                wait_full(act, u)
                fn(xT[:, b * T:(b + 1) * T], ps[7][:, :], ACT.Copy).then_inc(resT_done, 1)
                act.wait_ge(resT_done, k * NB + b + 1)
                act.sem_inc(freedom(u), 1)

            for k, b in pieces2:
                if k == "x2T":
                    if b == NB - 1:
                        act.wait_ge(down_done, NB * PAIRS)
                    transposed(("x2T", b), b, 1)
                    continue
                for p in range(PAIRS):
                    i = b * PAIRS + p
                    u = ("gate_e", i)
                    wait_full(act, u)
                    if i >= 2:
                        act.wait_ge(hid_done, i - 1)
                    fn(gate_s[:, i % 2, :], bank_of(u)[:, :], ACT.Silu).then_inc(silu_done, 1)
                    act.wait_ge(silu_done, i + 1)
                    act.sem_inc(freedom(u), 1)

            for u, o in ((("wqR", 0), wqR), (("wkR", 0), wkR)):
                wait_full(act, u)
                fn(o[:, :], bank_of(u)[:, :], ACT.Copy).then_inc(wr_done, 1)
            act.wait_ge(wr_done, 2)
            act.sem_inc(ps_free[0], 1)
            act.sem_inc(ps_free[1], 1)
            act.wait_ge(row_done, 2)

            for k, b in pieces3:
                if k == "L":
                    for c in range(4):
                        i = 4 * b + c
                        u = ("K", b, c)
                        wait_full(act, u)
                        if i >= 2:
                            act.wait_ge(kf_done, i - 1)
                        fn(ek_[:, i % 2, :], bank_of(u)[:, :], ACT.Exp, bias=minus1[:, 0:1]).then_inc(expk_done, 1)
                    for c in range(4):
                        i = 4 * b + c
                        u = ("Q", b, c)
                        wait_full(act, u)
                        if i >= 2:
                            act.wait_ge(minq_done, i - 1)
                        fn(eq_[:, i % 2, :], bank_of(u)[:, :], ACT.Exp, bias=qb[:, c:c + 1]).then_inc(expq_done, 1)
                if k == "M":
                    u = ("AT", b)
                    wait_full(act, u)
                    if b:
                        wait_full(act, ("Y1", b - 1))
                    fn(attnT[:, :], bank_of(u)[:, :], ACT.Copy).then_inc(attnT_done, 1)
                    act.wait_ge(attnT_done, NB + b + 1)
                    act.sem_inc(freedom(u), 1)
                if k == "N":
                    transposed(("x3T", b), b, 2)
                    act.wait_ge(lsub_done, b + 1)
                    fn(rt[:, 1, 0:NT * E1], rt[:, 0, 0:NT * E1], ACT.Exp).then_inc(lexp_done, 1)
                if k == "R":
                    u = ("ghT", b)
                    wait_full(act, u)
                    if b:
                        wait_full(act, ("Y2", b - 1))
                    fn(ghT[:, :], bank_of(u)[:, :], ACT.Copy).then_inc(ghT_done, 1)
                    act.wait_ge(ghT_done, b + 1)
                    act.sem_inc(freedom(u), 1)

        @block.vector
        def _(dve):
            V = nc.vector
            n = [0]

            def link(ins):
                n[0] += 1
                ins.then_inc(dve_chain, 1)
                dve.wait_ge(dve_chain, n[0])

            def tt(o, a, b, op):
                link(V.tensor_tensor(out=o, in0=a, in1=b, op=op))

            def ts(o, a, s1, s2, op0, op1=None):
                if op1 is None:
                    link(V.tensor_scalar(o, a, s1, None, op0))
                else:
                    link(V.tensor_scalar(o, a, s1, s2, op0, op1))

            def r3(k, e):
                return rt[:, k, 0:NT * e].rearrange("p (t e) -> p t e", e=e)

            def norm_start(k, b, y, waits=()):
                dve.wait_ge(bias_done, (NB * (0, 0, 1, 2)[k] + b + 1) if k != 1 else NB)
                link(V.tensor_tensor(out=z[:, b % 2, :, :], in0=y.rearrange("p (t d) -> p t d", d=D),
                                     in1=res[:, b * NT:(b + 1) * NT, :], op=ALU.add))

            def norm_rest(k, b, target):
                for t in range(NT):
                    last = V.bn_stats(stats[:, t, :], z[:, b % 2, t, :])
                link(last)
                for t in range(NT):
                    last = V.bn_aggr(mv[:, b, t, :], stats[:, t, :])
                link(last)
                V.tensor_scalar(var[:, b, :], mv[:, b, :, 1], LN_EPS, None, ALU.add).then_inc(var_done[k], 1)
                dve.wait_ge(rstd_done[k], b + 1)
                for t in range(NT):
                    last = V.tensor_scalar(target[:, b * NT + t, :], z[:, b % 2, t, :], mv[:, b, t, 0:1], rstd[:, b, t:t + 1],
                                           ALU.subtract, ALU.mult)
                return last

            def top(vals, m8, k, e, at, reset):
                thr = m8[:, :, k - 1:k].to_broadcast([P, NT, e])
                gt, eq, inc, le = (r3(at + i, e) for i in range(4))
                cnt = rt[:, at + 4, 0:NT]
                tt(gt, vals, thr, ALU.is_gt)
                tt(eq, vals, thr, ALU.is_equal)
                link(V.reduce_sum(cnt, gt, X))
                ts(cnt, cnt, -1.0, float(k), ALU.mult, ALU.add)
                link(V.tensor_tensor_scan(rt[:, at + 2, 0:NT * e], c_[reset], rt[:, at + 1, 0:NT * e], 0.0, ALU.mult, ALU.add))
                tt(le, inc, cnt.unsqueeze(2).to_broadcast([P, NT, e]), ALU.is_le)
                tt(eq, eq, le, ALU.mult)
                tt(gt, gt, eq, ALU.add)
                return gt

            def route(a):
                s = r3(1, E0)
                ts(rt[:, 0, :], rt[:, 0, :], 1.0, None, ALU.add)
                link(V.reciprocal(rt[:, 1, :], rt[:, 0, :]))
                sg = rt[:, 1, :].rearrange("p (g e) -> p g e", e=4)
                pr = rt[:, 2:4, :].rearrange("p a n -> p (a n)")[:, 0:96].rearrange("p (g e) -> p g e", e=6)
                V.tensor_tensor(out=pr[:, :, 0:3], in0=sg[:, :, 0:3], in1=sg[:, :, 1:4], op=ALU.add)
                V.tensor_tensor(out=pr[:, :, 3:5], in0=sg[:, :, 0:2], in1=sg[:, :, 2:4], op=ALU.add)
                tt(pr[:, :, 5:6], sg[:, :, 0:1], sg[:, :, 3:4], ALU.add)
                gs = r3(4, 8)
                link(V.memset(gs[:, :, 4:8], -1.0))
                link(V.tensor_reduce(out=gs[:, :, 0:4], in_=pr.rearrange("p (t g) e -> p t g e", g=4), axis=X, op=ALU.max))
                m8 = r3(5, 8)
                for t in range(NT):
                    last = V.max(m8[:, t, :], gs[:, t, :])
                link(last)
                allow = top(gs, m8, 2, 8, 6, "reset8")[:, :, 0:4]
                am1 = r3(11, 4)
                ts(am1, allow, -1.0, None, ALU.add)
                s4 = rt[:, 1, :].rearrange("p (g e) -> p g e", e=4)
                mk = rt[:, 12, :].rearrange("p (t g e) -> p t g e", g=4, e=4)
                s44 = rt[:, 1, :].rearrange("p (t g e) -> p t g e", g=4, e=4)
                tt(mk, s44, allow.unsqueeze(3).to_broadcast([P, NT, 4, 4]), ALU.mult)
                tt(mk, mk, am1.unsqueeze(3).to_broadcast([P, NT, 4, 4]), ALU.add)
                masked = r3(12, E0)
                for t in range(NT):
                    last = V.max(m8[:, t, :], masked[:, t, :])
                link(last)
                chosen = top(masked, m8, 4, E0, 13, "reset16")
                w = r3(18, E0)
                tt(w, s, chosen, ALU.mult)
                tot = rt[:, 19, 0:NT]
                link(V.reduce_sum(tot, w, X))
                ts(tot, tot, 1e-6, None, ALU.add)
                link(V.reciprocal(tot, tot))
                tt(w, w, tot.unsqueeze(2).to_broadcast([P, NT, E0]), ALU.mult)
                if a:
                    wait_full(dve, ("m", "combine", a - 1, 0))
                link(V.tensor_copy(cparts[:, :, 0:E0], w))
                tt(w, w, cparts[:, :, 0:E0], ALU.subtract)
                link(V.tensor_copy(cparts[:, :, E0:2 * E0], w))
                V.tensor_tensor(out=cparts[:, :, 2 * E0:], in0=w, in1=cparts[:, :, E0:2 * E0],
                                op=ALU.subtract).then_inc(cparts_done, 1)

            def reduce_scores(u):
                G, i = divmod(u, HG * NT)
                dve.wait_ge(sm_full, u + 1)
                if i == 0 and G >= 4:
                    wait_full(dve, ("m", "max", G - 4, 0))
                V.tensor_reduce(out=negmax[:, G % 4, i:i + 1], in_=ps[4 + u % 2][:, :], axis=X, op=ALU.max,
                                negate=True).then_inc(sm_free, 1)

            def misc_dve(kind, a, m):
                u = ("m", kind, a, m)
                o = ps[MISC]
                if kind == "rope":
                    wait_full(dve, u)
                    if a and m % 2 == 0:
                        dve.wait_ge(split_done, 2 * (a - 1) + m // 2 + 1)
                    V.scalar_tensor_tensor(out=rot[:, m, :], in0=o[:, :], scalar=c_["b_rope"][:, m:m + 1],
                                           in1=c_["cos"] if m % 2 == 0 else c_["sin"],
                                           op0=ALU.add, op1=ALU.mult).then_inc(rot_done, 1)
                    dve.wait_ge(rot_done, 4 * a + m + 1)
                    dve.sem_inc(ps_free[MISC], 1)
                if kind == "val":
                    wait_full(dve, u)
                    if a >= 2:
                        dve.wait_ge(pv_done, NG * NT * (a - 1))
                    for t in range(NT):
                        last = V.tensor_tensor(out=VA[a % 2][:, t, :, 0:DH],
                                               in0=o[:, t * D:(t + 1) * D].rearrange("p (h d) -> p h d", d=DH),
                                               in1=c_["bv_row"].rearrange("p (h d) -> p h d", d=DH), op=ALU.add)
                    last.then_inc(v_done, 1)
                    dve.wait_ge(v_done, a + 1)
                    dve.sem_inc(ps_free[MISC], 1)
                if kind == "heads":
                    wait_full(dve, u)
                    if a >= 2 and m == 0:
                        wait_full(dve, ("m", "attnT", a - 2, 0))
                    v = o[:, :].rearrange("p (h c) -> p h c", c=32)
                    link(V.reciprocal(rden[:, m, :], v[:, :, DH]))
                    V.tensor_tensor(out=attn[:, a % 2, m, :].rearrange("p (h d) -> p h d", d=DH), in0=v[:, :, 0:DH],
                                    in1=rden[:, m, :].unsqueeze(2).to_broadcast([P, H, DH]), op=ALU.mult).then_inc(attn_done, 1)
                    dve.wait_ge(attn_done, NT * a + m + 1)
                    dve.sem_inc(ps_free[MISC], 1)
                if kind == "proj":
                    wait_full(dve, u)
                    norm_start(0, a, o[:, :])
                    dve.sem_inc(ps_free[MISC], 1)
                    norm_rest(0, a, res).then_inc(res_done, 1)
                if kind == "gate":
                    dve.wait_ge(expneg_done, a + 1)
                    route(a)

            for i in range(2):
                V.memset(VA[i][:, :, :, DH + 1:], 0.0)
                last = V.memset(VA[i][:, :, :, DH:DH + 1], 1.0)
            V.memset(minus1[:, :], -1.0)
            dve.wait_ge(early_ld, 32)
            for s in prologue[:-1]:
                misc_dve(*s)
            for u in range(2 * HG * NT):
                reduce_scores(u)
            for w in range(HALVES):
                G = w // 8
                if G + 2 < GROUPS:
                    for i in range(2):
                        reduce_scores((G + 2) * HG * NT + 2 * (w % 8) + i)
                for s in slots[w]:
                    misc_dve(*s)
            for s in epilogue:
                misc_dve(*s)

            for b in range(NB):
                for p in range(PAIRS):
                    i = b * PAIRS + p
                    u = ("up_e", i)
                    dve.wait_ge(silu_done, i + 1)
                    wait_full(dve, u)
                    if i >= 3:
                        dve.wait_ge(down_done, i - 2)
                    if p == EP:
                        V.tensor_tensor(out=hid[:, i % 3, :], in0=gate_s[:, i % 2, :], in1=bank_of(u)[:, :],
                                        op=ALU.mult).then_inc(hid_done, 1)
                        dve.wait_ge(hid_done, i + 1)
                        dve.sem_inc(freedom(u), 1)
                    else:
                        tt(prod[:, i % 2, :], gate_s[:, i % 2, :], bank_of(u)[:, :], ALU.mult)
                        dve.sem_inc(freedom(u), 1)
                        c = ("comb_e", i)
                        wait_full(dve, c)
                        V.tensor_tensor(out=hid[:, i % 3, :], in0=prod[:, i % 2, :], in1=bank_of(c)[:, :],
                                        op=ALU.mult).then_inc(hid_done, 1)
                        dve.wait_ge(hid_done, i + 1)
                        dve.sem_inc(freedom(c), 1)
                u = ("y_e", b)
                wait_full(dve, u)
                norm_start(1, b, ps[6][:, :])
                dve.sem_inc(freedom(u), 1)
                norm_rest(1, b, res).then_inc(res_done, 1)

            u = ("qb", 0)
            wait_full(dve, u)
            V.tensor_copy(qb[:, :], bank_of(u)[:, 0:4])
            V.tensor_scalar(qb1[:, :], bank_of(u)[:, 0:4], 1.0, None, ALU.add).then_inc(row_done, 1)
            u = ("kb", 0)
            wait_full(dve, u)
            V.tensor_scalar(kbias[:, :], bank_of(u)[:, :], 1.0, None, ALU.add).then_inc(row_done, 1)
            dve.wait_ge(row_done, 2)
            dve.sem_inc(ps_free[2], 1)
            dve.sem_inc(ps_free[3], 1)
            link(V.tensor_copy(kparts[0:1, 0, :], kbias[0:1, :]))
            tt(kbias[0:1, :], kbias[0:1, :], kparts[0:1, 0, :], ALU.subtract)
            link(V.tensor_copy(kparts[0:1, 1, :], kbias[0:1, :]))
            V.tensor_tensor(out=kparts[0:1, 2, :], in0=kbias[0:1, :], in1=kparts[0:1, 1, :], op=ALU.subtract).then_inc(kb_done, 1)

            for k, b in pieces3:
                if k == "L":
                    for c in range(4):
                        i = 4 * b + c
                        u = ("K", b, c)
                        dve.wait_ge(expk_done, i + 1)
                        if b and c == 0:
                            wait_full(dve, ("KV", b - 1))
                        V.scalar_tensor_tensor(out=KF[:, c, :], in0=ek_[:, i % 2, :], scalar=1.0, in1=bank_of(u)[:, :],
                                               op0=ALU.min, op1=ALU.max).then_inc(kf_done, 1)
                        dve.wait_ge(kf_done, i + 1)
                        dve.sem_inc(freedom(u), 1)
                    u = ("V", b)
                    wait_full(dve, u)
                    for t in range(NT):
                        last = V.tensor_tensor(out=V36[:, t, :, 0:32],
                                               in0=bank_of(u)[:, t * D:(t + 1) * D].rearrange("p (c d) -> p c d", c=NG),
                                               in1=c_["bv1_row"].rearrange("p (c d) -> p c d", c=NG), op=ALU.add)
                    last.then_inc(v36_done, 1)
                    dve.wait_ge(v36_done, b + 1)
                    dve.sem_inc(freedom(u), 1)
                    for c in range(4):
                        i = 4 * b + c
                        u = ("Q", b, c)
                        dve.wait_ge(minq_done, i + 1)
                        if b >= 2 and c == 0:
                            wait_full(dve, ("O", b - 2, 1))
                        V.scalar_tensor_tensor(out=QF[:, b % 2, c, :], in0=bank_of(u)[:, :], scalar=qb1[:, c:c + 1],
                                               in1=mq_[:, i % 2, :], op0=ALU.add, op1=ALU.max).then_inc(qf_done, 1)
                        dve.wait_ge(qf_done, i + 1)
                        dve.sem_inc(freedom(u), 1)
                    u = ("KV", b)
                    wait_full(dve, u)
                    if b:
                        wait_full(dve, ("O", b - 1, 1))
                    V.tensor_tensor(out=KVB[:, :, :], in0=bank_of(u)[:, 0:4 * KVW].rearrange("p (c k) -> p c k", k=KVW),
                                    in1=c_["mask"].unsqueeze(1).to_broadcast([P, NG, KVW]), op=ALU.mult).then_inc(kvb_done, 1)
                    dve.wait_ge(kvb_done, b + 1)
                    dve.sem_inc(freedom(u), 1)
                    for tp in range(2):
                        u = ("O", b, tp)
                        wait_full(dve, u)
                        if tp == 0 and b >= 2:
                            wait_full(dve, ("AT", b - 2))
                        v = bank_of(u)[:, 0:8 * KVW].rearrange("p (tc k) -> p tc k", k=KVW)
                        nrm = rt[:, 20, 0:32].rearrange("p (tc h) -> p tc h", h=HG)
                        ts(nrm, v[:, :, 32:36], 256e-6, None, ALU.max)
                        link(V.reciprocal(rt[:, 21, 0:32], rt[:, 20, 0:32]))
                        for t in range(2):
                            last = V.tensor_tensor(
                                out=attn[:, b % 2, 2 * tp + t, :].rearrange("p (c h d) -> p c h d", h=HG, d=DH),
                                in0=v[:, 4 * t:4 * t + 4, 0:32].rearrange("p c (h d) -> p c h d", d=DH),
                                in1=rt[:, 21, 16 * t:16 * t + 16].rearrange("p (c h) -> p c h", h=HG).unsqueeze(3)
                                .to_broadcast([P, NG, HG, DH]), op=ALU.mult)
                        last.then_inc(attn_done, 1)
                        dve.wait_ge(attn_done, NB * NT + 2 * b + tp + 1)
                        dve.sem_inc(freedom(u), 1)
                if k == "M":
                    u = ("Y1", b)
                    wait_full(dve, u)
                    norm_start(2, b, bank_of(u)[:, :])
                    dve.sem_inc(freedom(u), 1)
                    norm_rest(2, b, res).then_inc(res_done, 1)
                if k == "N":
                    u = ("lg", b)
                    wait_full(dve, u)
                    lg = bank_of(u)[:, 0:NT * E1].rearrange("p (t e) -> p t e", e=E1)
                    mx = rt[:, 2, 0:NT]
                    link(V.tensor_reduce(out=mx, in_=lg, axis=X, op=ALU.max))
                    V.tensor_tensor(out=r3(0, E1), in0=lg, in1=mx.unsqueeze(2).to_broadcast([P, NT, E1]),
                                    op=ALU.subtract).then_inc(lsub_done, 1)
                    dve.wait_ge(lsub_done, b + 1)
                    dve.sem_inc(freedom(u), 1)
                    dve.wait_ge(lexp_done, b + 1)
                    e = r3(1, E1)
                    tot = rt[:, 3, 0:NT]
                    link(V.reduce_sum(tot, e, X))
                    link(V.reciprocal(tot, tot))
                    tt(gate8[:, :, :], e, tot.unsqueeze(2).to_broadcast([P, NT, E1]), ALU.mult)
                    m8 = r3(5, 8)
                    for t in range(NT):
                        last = V.max(m8[:, t, :], gate8[:, t, :])
                    link(last)
                    chosen = top(gate8[:, :, :], m8, 2, E1, 6, "reset8")
                    tt(gate8[:, :, :], gate8[:, :, :], chosen, ALU.mult)
                    link(V.reduce_sum(tot, gate8[:, :, :], X))
                    ts(tot, tot, 1e-6, None, ALU.add)
                    link(V.reciprocal(tot, tot))
                    tt(gate8[:, :, :], gate8[:, :, :], tot.unsqueeze(2).to_broadcast([P, NT, E1]), ALU.mult)
                    u = ("lh", b)
                    wait_full(dve, u)
                    if b:
                        wait_full(dve, ("ghT", b - 1))
                    for t in range(NT):
                        last = V.tensor_tensor(out=gh[:, t, :].rearrange("p (e r) -> p e r", r=R1),
                                               in0=bank_of(u)[:, t * P:(t + 1) * P].rearrange("p (e r) -> p e r", r=R1),
                                               in1=gate8[:, t, :].unsqueeze(2).to_broadcast([P, E1, R1]), op=ALU.mult)
                    last.then_inc(gh_done, 1)
                    dve.wait_ge(gh_done, b + 1)
                    dve.sem_inc(freedom(u), 1)
                if k == "R":
                    u = ("Y2", b)
                    wait_full(dve, u)
                    norm_start(3, b, bank_of(u)[:, :])
                    dve.sem_inc(freedom(u), 1)
                    norm_rest(3, b, outb).then_inc(store_in, 1)


def rows(v):
    return np.broadcast_to(np.asarray(v)[None, :], (P, v.shape[0]))


def kernel(**inputs):
    import concourse.bacc as bacc
    from concourse.bass_utils import run_bass_kernel_spmd as run
    import ml_dtypes

    a = {k: np.asarray(v) for k, v in inputs.items()}
    x = a["L0_attn_x"].reshape(NB * T, D)
    d = np.arange(D)
    partner = d // DH * DH + (d % DH + DH // 2) % DH
    w, bq = a["L0_attn_W_qkv"], a["L0_attn_b_qkv"]
    wq, wk, wv = w[:, :D], w[:, D:2 * D], w[:, 2 * D:]
    b_q, b_k = bq[:D], bq[D:2 * D]
    inv = (1.0 / np.float32(10000.0) ** (np.arange(0, DH, 2, dtype=np.float32) / np.float32(DH))).astype(np.float32)
    ang = (np.arange(T, dtype=np.float32)[None, :] * inv[d % (DH // 2)][:, None]).astype(np.float64)
    sign = np.where(d % DH < DH // 2, -1.0, 1.0)[:, None]
    early = dict(w_qkv=np.concatenate([wq, wq[:, partner], wk, wk[:, partner], wv], 1),
                 b_rope=np.stack([b_q, b_q[partner], b_k, b_k[partner]], 1),
                 cos=np.cos(ang).astype(np.float32), sin=(np.sin(ang) * sign).astype(np.float32),
                 ident=np.eye(P, dtype=np.float32), bv_row=rows(bq[2 * D:]))
    r = a["L1_attn_random_matrix"]
    rbd = np.zeros((D, H * M1), np.float32)
    for h in range(H):
        rbd[h * DH:(h + 1) * DH, h * M1:(h + 1) * M1] = r
    f = np.arange(P)
    mask = np.zeros((P, KVW), np.float32)
    for h in range(HG):
        mask[h * M1:(h + 1) * M1, h * DH:(h + 1) * DH] = 1.0
        mask[h * M1:(h + 1) * M1, HG * DH + h] = 1.0

    def reset(e):
        v = np.ones((P, NT, e), np.float32)
        v[:, :, 0] = 0.0
        return v.reshape(P, NT * e)

    w2 = a["L0_ffn_w2_e"].transpose(0, 2, 1).reshape(EP, 2 * F0, D).transpose(1, 0, 2).reshape(P, EP * D)
    late = dict(w_out=a["L0_attn_W_out"], bout_row=rows(a["L0_attn_b_out"]), wg=a["L0_ffn_w_gate"].T,
                w1=a["L0_ffn_w1_e"].reshape(E0 * F0, D).T, w3=a["L0_ffn_w3_e"].reshape(E0 * F0, D).T, w2=w2,
                w1s=a["L0_ffn_w1_s"].T, w3s=a["L0_ffn_w3_s"].T, w2s=a["L0_ffn_w2_s"].T, reset16=reset(E0),
                wqT=a["L1_attn_Wq"].T, wkT=a["L1_attn_Wk"].T, wv1=a["L1_attn_Wv"], wo1=a["L1_attn_Wo"], rbd=rbd,
                bq_col=a["L1_attn_bq"][:, None], bk_rep=np.broadcast_to(a["L1_attn_bk"][:, None], (D, P)),
                bv1_row=rows(a["L1_attn_bv"]), bo1_row=rows(a["L1_attn_bo"]), mask=mask,
                lr=a["L1_ffn_R"].T, la=a["L1_ffn_A"].reshape(E1 * R1, D).T, lw=a["L1_ffn_W"].T,
                lb=a["L1_ffn_B"].transpose(0, 2, 1).reshape(E1 * R1, D), lb_row=rows(a["L1_ffn_b"]), reset8=reset(E1))
    sel = np.zeros((3, E0, EP, P), np.float32)
    for e in range(E0):
        sel[:, e, e // 2, (e % 2) * F0:(e % 2 + 1) * F0] = 1.0
    bf = ml_dtypes.bfloat16
    arrays = {
        "in_x": np.ascontiguousarray(x), "in_xT": np.ascontiguousarray(x.T),
        "in_early": np.ascontiguousarray(np.concatenate([early[k] for k in EARLY], 1)),
        "in_late": np.ascontiguousarray(np.concatenate([late[k] for k in LATE], 1)),
        "in_sel": sel.reshape(3 * E0, EP, P).astype(bf), "in_identb": np.eye(P).astype(bf),
    }
    nc = bacc.Bacc("TRN2", target_bir_lowering=False, num_devices=1)
    args = [nc.dram_tensor(k, v.shape, mybir.dt.from_np(v.dtype), kind="ExternalInput").ap() for k, v in arrays.items()]
    parts_dram = nc.dram_tensor("parts_dram", (NB, 2, P, 3, T), BF16, kind="Internal").ap()
    out = nc.dram_tensor("out_y", (NB * T, D), F32, kind="ExternalOutput").ap()
    program(nc, *args, parts_dram, out)
    result = run(nc, [arrays], core_ids=[0])
    return result.results[0]["out_y"].reshape(NB, T, D)
```

```python
from contextlib import ExitStack

import numpy as np

import concourse.bass as bass
from concourse import mybir

P = 128
F32 = mybir.dt.float32
BF16 = mybir.dt.bfloat16
ALU = mybir.AluOpType
ACT = mybir.ActivationFunctionType
X = mybir.AxisListType.X

NB, T, D = 4, 512, 128
NT = T // P
H, DH = 16, 8
HG = 4
NG = H // HG
GROUPS = NB * NG
SLOTS = 9
KROW = 96
E0, F0, EP = 16, 64, 8
E1, R1 = 8, 16
M1 = 32
KVW = HG * DH + HG
LN_EPS = 1e-5
TWO_ONES = float(np.array([0x3F803F80], np.uint32).view(np.float32)[0])

EARLY = dict(w_qkv=5 * D, b_rope=4, cos=T, sin=T, ident=P, bv_row=D)
LATE = dict(w_out=D, bout_row=D, wg=E0, w1=E0 * F0, w3=E0 * F0, w2=EP * D, w1s=D, w3s=D, w2s=D, reset16=NT * E0,
            wqT=D, wkT=D, wv1=D, wo1=D, rbd=H * M1, bq_col=1, bk_rep=P, bv1_row=D, bo1_row=D, mask=KVW,
            lr=E1, la=E1 * R1, lw=D, lb=D, lb_row=D, reset8=NT * E1)


def columns(widths):
    at, out = 0, {}
    for name, n in widths.items():
        out[name] = (at, at + n)
        at += n
    return out, at


EARLY_AT, EARLY_N = columns(EARLY)
LATE_AT, LATE_N = columns(LATE)


def program(nc, x_in, xT_in, early_in, late_in, sel_in, identb_in, parts_dram, out):
    with ExitStack() as ctx:
        def sb(name, shape, dt=F32):
            return ctx.enter_context(nc.sbuf_tensor(name, shape, dt))

        def sem(name):
            return ctx.enter_context(nc.semaphore(name))

        early = sb("early", [P, EARLY_N])
        late = sb("late", [P, LATE_N])
        c_ = {k: early[:, a:b] for k, (a, b) in EARLY_AT.items()}
        c_.update({k: late[:, a:b] for k, (a, b) in LATE_AT.items()})
        ident = c_["ident"]
        identb = sb("identb", [P, P], BF16)
        sel = sb("sel", [3 * E0, EP, P], BF16)
        xT = sb("xT", [P, NB * T])
        res = sb("res", [P, NB * NT, D])
        z = sb("z", [P, 2, NT, D])
        rot = sb("rot", [P, 4, T])
        parts = sb("parts", [P, 2, 3, T], BF16)
        QS = [sb(f"QS{i}", [P, H, T], BF16) for i in range(2)]
        KS = [sb(f"KS{i}", [P, H, T], BF16) for i in range(2)]
        VA = [sb(f"VA{i}", [P, NT, H, 32]) for i in range(2)]
        probs = sb("probs", [P, 2, HG, T])
        OU = sb("OU", [P, 2, NG, T])
        negmax = sb("negmax", [P, 4, HG * NT])
        maxT = sb("maxT", [HG * NT, 2, P])
        maxp = sb("maxp", [HG * NT, 2, 3, P], BF16)
        rden = sb("rden", [P, NT, H])
        attn = sb("attn", [P, 2, NT, D])
        attnT = sb("attnT", [P, T])
        stats = sb("stats", [P, NT, 6])
        mv = sb("mv", [P, NB, NT, 2])
        var = sb("var", [P, NB, NT])
        rstd = sb("rstd", [P, NB, NT])
        minus_half = sb("minus_half", [P, NT])
        minus1 = sb("minus1", [P, 1])
        rt = sb("rt", [P, 24, NT * E0])
        cT = sb("cT", [3 * E0, NB, T], BF16)
        cparts = sb("cparts", [P, NT, 3 * E0], BF16)
        qb = sb("qb", [P, NT])
        qb1 = sb("qb1", [P, NT])
        kparts = sb("kparts", [1, 3, H * M1], BF16)
        kstack = sb("kstack", [3, H * M1], BF16)
        onesb = sb("onesb", [3, P], BF16)
        V36 = sb("V36", [P, NT, NG, KVW])
        KVB = sb("KVB", [P, NG, KVW])
        A0, A1 = (q[:, :, :].rearrange("p h t -> p (h t)").bitcast(F32) for q in QS)
        B0, B1 = (k[:, :, :].rearrange("p h t -> p (h t)").bitcast(F32) for k in KS)
        gate_s = A0[:, 0:2 * T].rearrange("p (i t) -> p i t", t=T)
        prod = A0[:, 2 * T:4 * T].rearrange("p (i t) -> p i t", t=T)
        hid = A0[:, 4 * T:7 * T].rearrange("p (i t) -> p i t", t=T)
        eq_ = B0[:, 0:2 * T].rearrange("p (i t) -> p i t", t=T)
        ek_ = B0[:, 2 * T:4 * T].rearrange("p (i t) -> p i t", t=T)
        mq_ = B0[:, 4 * T:6 * T].rearrange("p (i t) -> p i t", t=T)
        gh = B0[:, 6 * T:7 * T].rearrange("p (n d) -> p n d", n=NT)
        ghT = B0[:, 7 * T:8 * T]
        QF = A1.rearrange("p (i c t) -> p i c t", i=2, c=NT)
        KF = B1[:, 0:4 * T].rearrange("p (n f) -> p n f", n=NT)
        outb = B1[:, 4 * T:8 * T].rearrange("p (n d) -> p n d", d=D)
        wqR, wkR, kbias = (probs[:, 0, i, :] for i in range(3))
        gate8 = sb("gate8", [P, NT, E1])

        psum = ctx.enter_context(nc.psum_tensor("psum", [P, 8, 512], F32))
        ps = [psum[:, i, :] for i in range(8)]

        x_ld, early_ld, late_ld, init_pool, init_dve = (
            sem(n) for n in ("x_ld", "early_ld", "late_ld", "init_pool", "init_dve"))
        sm_full, sm_free, s_full, exp_done, pv_done, o_evac = (
            sem(n) for n in ("sm_full", "sm_free", "s_full", "exp_done", "pv_done", "o_evac"))
        ps_full = [sem(f"ps_full{i}") for i in range(8)]
        rot_done, v_done, maxT_done, maxp_done = (sem(n) for n in ("rot_done", "v_done", "maxT_done", "maxp_done"))
        split_done = [sem(f"split_done{i}") for i in range(2)]
        parts_st = [sem(f"parts_st{i}") for i in range(2)]
        qk_ld = [sem(f"qk_ld{i}") for i in range(2)]
        qk_first = sem("qk_first")
        maxrow_ld = [sem(f"maxrow_ld{i}") for i in range(2)]
        attn_done, attnT_done, resT_done = (sem(n) for n in ("attn_done", "attnT_done", "resT_done"))
        sum_done = [sem(f"sum_done{k}") for k in range(4)]
        stat_done = [sem(f"stat_done{k}") for k in range(4)]
        rstd_done = [sem(f"rstd_done{k}") for k in range(4)]
        res_done = [sem(f"res_done{k}") for k in range(4)]
        expneg_done, cparts_done, cT_done = (sem(n) for n in ("expneg_done", "cparts_done", "cT_done"))
        silu_done, prod_done, hid_done, down_done = (sem(n) for n in ("silu_done", "prod_done", "hid_done", "down_done"))
        dve_chain, pool_chain = (sem(n) for n in ("dve_chain", "pool_chain"))
        wr_done, row_done, kb_done, ks_ld, expq_done, minq_done, qf_done, expk_done, kf_done, v36_done, kvb_done = (
            sem(n) for n in ("wr_done", "row_done", "kb_done", "ks_ld", "expq_done", "minq_done", "qf_done", "expk_done",
                             "kf_done", "v36_done", "kvb_done"))
        lsub_done, lexp_done, gh_done, ghT_done, stored, bias_done = (
            sem(n) for n in ("lsub_done", "lexp_done", "gh_done", "ghT_done", "stored", "bias_done"))

        MISC = 7
        HALVES = GROUPS * NT * 2
        PAIRS = EP + 1
        last = NB - 1
        prologue = [("rope", 0, 0), ("rope", 0, 1), ("rope", 0, 2), ("rope", 0, 3), ("val", 0, 0), ("max", 0, 0)]
        slots = [[] for _ in range(HALVES)]
        for b in range(NB):
            w = 32 * b
            for g in range(4):
                if 4 * b + g + 1 < GROUPS:
                    slots[w + 8 * g].append(("max", 4 * b + g + 1, 0))
            if b == 0:
                for m in range(4):
                    slots[w + m + 1].append(("rope", 1, m))
            if b + 1 < NB:
                slots[w + 7].append(("val", b + 1, 0))
            if b + 2 < NB:
                for m in range(4):
                    slots[w + 20 + 3 * m].append(("rope", b + 2, m))
            if b:
                for i in range(NT):
                    slots[w + 2 + i].append(("heads", b - 1, i))
                for kind, at in (("attnT", 6), ("proj", 9), ("norm", 14), ("resT", 16)):
                    slots[w + at].append((kind, b - 1, 0))
                if b == 1:
                    slots[w + 18].append(("gate", 0, 0))
                    slots[w + 31].append(("combine", 0, 0))
        beside = [[] for _ in range(NB * PAIRS)]
        for at, kind, b, i in ((0, "gate", 1, 0), (1, "heads", 3, 0), (1, "heads", 3, 1), (2, "heads", 3, 2), (2, "heads", 3, 3),
                               (3, "attnT", 3, 0), (6, "combine", 1, 0), (7, "proj", 3, 0), (8, "norm", 3, 0),
                               (9, "resT", 3, 0), (9, "chunk", 0, 0), (11, "norm1", 0, 0), (12, "x2T", 0, 0), (12, "gate", 2, 0),
                               (13, "wR", 0, 0), (14, "wR", 0, 1), (15, "qb", 0, 0), (17, "combine", 2, 0), (17, "kb", 0, 0),
                               (18, "chunk", 1, 0), (20, "norm1", 1, 0), (21, "x2T", 1, 0), (21, "gate", 3, 0),
                               (26, "combine", 3, 0), (27, "chunk", 2, 0), (29, "norm1", 2, 0), (30, "x2T", 2, 0)):
            beside[at].append((kind, b, i))
        def front(b):
            return ([("K", b, c) for c in range(4)] + [("V", b, 0)] + [("Q", b, c) for c in range(4)]
                    + [("KV", b, 0), ("O", b, 0), ("O", b, 1)])

        def back(b):
            return [(k, b, 0) for k in ("AT", "Y1", "norm2", "x3T", "lg", "ghT", "Y2", "norm3")]

        f0 = front(0)
        layer2 = ([("chunk", last, 0)] + f0[:3] + [("norm1", last, 0)] + f0[3:5] + [("x2T", last, 0)] + f0[5:])
        for b in range(1, NB):
            f, k = front(b), back(b - 1)
            layer2 += f[0:1] + k[0:1] + f[1:2] + k[1:2] + f[2:5] + k[2:3] + f[5:7] + k[3:4] + f[7:8] + k[4:5] + f[8:12] + k[5:8]
        layer2 += back(last)

        uses = [[] for _ in range(8)]
        in_misc = ("rope", "val", "max", "heads", "attnT", "proj", "resT", "gate", "combine", "wR", "qb", "kb", "x2T")
        uses[MISC] = [s for one in [prologue] + slots + beside for s in one if s[0] in in_misc]
        for i in range(NB * PAIRS):
            uses[i % 2].append(("gate_e", i, 0))
            uses[2 + i % 2].append(("up_e", i, 0))
            if i % PAIRS < EP:
                uses[4].append(("comb_e", i, 0))
        for b in range(NB):
            uses[5 + b % 2].append(("y_e", b, 0))
        bank_for = {"K": 2, "Q": 0, "V": 4, "KV": 5, "O": 6, "AT": 7, "Y1": 4, "x3T": 7, "lg": 5, "ghT": 7, "Y2": 4, "x2T": 7}
        for kind, b, c in layer2:
            if kind in bank_for:
                uses[bank_for[kind] + (c % 2 if kind in "KQ" else 0)].append((kind, b, c))
            if kind == "lg":
                uses[7].append(("lh", b, 0))
        turn = {u: (bank, n) for bank in range(8) for n, u in enumerate(uses[bank])}

        def read_out(u):
            kind, b, c = u
            if kind == "up_e":
                n, p = divmod(b, PAIRS)
                return (hid_done, b + 1) if p == EP else (prod_done, n * EP + p + 1)
            return {"rope": (rot_done, 4 * b + c + 1), "val": (v_done, b + 1), "max": (maxT_done, b + 1),
                    "heads": (attn_done, NT * b + c + 1), "attnT": (attnT_done, b + 1), "proj": (sum_done[0], b + 1),
                    "resT": (resT_done, b + 1), "gate": (expneg_done, b + 1), "combine": (cT_done, b + 1),
                    "gate_e": (silu_done, b + 1), "comb_e": (hid_done, b + 1), "y_e": (sum_done[1], b + 1),
                    "x2T": (resT_done, NB + b + 1), "wR": (wr_done, c + 1),
                    "qb": (row_done, 1), "kb": (row_done, 2), "Q": (qf_done, 4 * b + c + 1), "K": (kf_done, 4 * b + c + 1),
                    "V": (v36_done, b + 1), "KV": (kvb_done, b + 1), "O": (attn_done, NB * NT + 2 * b + c + 1),
                    "AT": (attnT_done, NB + b + 1), "Y1": (sum_done[2], b + 1), "x3T": (resT_done, 2 * NB + b + 1),
                    "lg": (lsub_done, b + 1), "lh": (gh_done, b + 1), "ghT": (ghT_done, b + 1),
                    "Y2": (sum_done[3], b + 1)}[kind]

        def bank_of(u):
            return ps[turn[u][0]]

        def wait_free(eng, u):
            bank, n = turn[u]
            if n:
                eng.wait_ge(*read_out(uses[bank][n - 1]))

        def wait_full(eng, u):
            bank, n = turn[u]
            eng.wait_ge(ps_full[bank], n + 1 - sum(v[0] == "y_e" for v in uses[bank][:n]))

        def fullness(u):
            return ps_full[turn[u][0]]

        def wide(stack, first, end):
            return stack[first:end, :, :].rearrange("p h t -> p (h t)").bitcast(F32)

        block = ctx.enter_context(nc.Block())

        @block.sync
        def _(sp):
            sp.dma_start(xT[:, 0:T], xT_in[:, 0:T]).then_inc(early_ld, 16)
            sp.dma_start(early[:, :], early_in).then_inc(early_ld, 16)

            def load_stacks(b):
                for p in range(3):
                    for i in (1, 0):
                        sp.wait_ge(split_done[i], 3 * b + p + 1)
                        sp.dma_start(parts_dram[b, i, p].rearrange("d h t -> h d t"), parts[:, i, p, :])\
                            .then_inc(parts_st[i], 16)
                if b >= 2:
                    sp.wait_ge(s_full, 32 * (b - 1))
                else:
                    sp.wait_ge((init_dve, init_pool)[b], 1)
                for h0, h1 in ((0, HG), (HG, H)) if b == 0 else ((0, H),):
                    done = qk_first if b == 0 and h0 == 0 else qk_ld[b % 2]
                    for i in (1, 0):
                        sp.wait_ge(parts_st[i], 48 * (b + 1))
                        dst = (QS, KS)[i][b % 2][:, h0:h1, :].rearrange("r h t -> r (h t)")
                        src = parts_dram[b, i, :, :, h0:h1, :].rearrange("p d h t -> p d (h t)")
                        n = (h1 - h0) * T
                        for s in range(3):
                            rows_ = dst[s * 3 * DH:(s + 1) * 3 * DH, :]
                            if i == 0:
                                sp.dma_start(rows_, src[s].unsqueeze(0).to_broadcast([3, DH, n])).then_inc(done, 16)
                            else:
                                sp.dma_start(rows_, src.rearrange("p d n -> (p d) n")).then_inc(done, 16)

            def load_max(G):
                sp.wait_ge(maxp_done, G + 1)
                if G >= 2:
                    sp.wait_ge(maxrow_ld[G % 2], 48 * (G // 2))
                g = G % NG
                for i in range(3):
                    dst = QS[(G // NG) % 2][KROW + i:KROW + i + 1, HG * g:HG * (g + 1), :]
                    sp.dma_start(dst.rearrange("i h (q t) -> i (h q) t", q=NT), maxp[:, G % 2, i, :])\
                        .then_inc(maxrow_ld[G % 2], 16)

            load_stacks(0)
            sp.dma_start(xT[:, T:], xT_in[:, T:]).then_inc(x_ld, 16)
            sp.dma_start(res[:, :, :], x_in.rearrange("(n p) d -> p n d", p=P)).then_inc(x_ld, 16)
            load_max(0)
            sp.dma_start(late[:, :], late_in).then_inc(late_ld, 16)
            sp.dma_start(sel[:, :, :], sel_in).then_inc(late_ld, 16)
            sp.dma_start(identb[:, :], identb_in).then_inc(late_ld, 16)
            pending = []
            for w in range(HALVES):
                for kind, a, m in slots[w]:
                    if kind == "max":
                        load_max(a)
                    if kind == "rope" and m == 3:
                        pending.append(a)
                if pending and (w < 32 or w % 32 == 0):
                    load_stacks(pending.pop())
            sp.wait_ge(kb_done, 1)
            for i in range(3):
                sp.dma_start(kstack[i:i + 1, :], kparts[0:1, i, :]).then_inc(ks_ld, 16)
            for b in range(NB):
                sp.wait_ge(res_done[3], b + 1)
                sp.dma_start(out[b * T:(b + 1) * T, :].rearrange("(n p) d -> p n d", p=P),
                             outb[:, b * NT:(b + 1) * NT, :]).then_inc(stored, 16)
            sp.wait_ge(stored, 16 * NB)

        @block.gpsimd
        def _(pool):
            n = [0]

            def link(ins):
                n[0] += 1
                ins.then_inc(pool_chain, 1)
                pool.wait_ge(pool_chain, n[0])

            def tt(o, a, b, op):
                return nc.gpsimd.tensor_tensor(out=o, in0=a, in1=b, op=op)

            def rope_split(b, i):
                v = rot[:, 2 * i, :]
                pool.wait_ge(rot_done, 4 * b + 2 * i + 2)
                if b:
                    pool.wait_ge(parts_st[i], 48 * b)
                    link(tt(v, v, c_["cos"], ALU.mult))
                    link(tt(rot[:, 2 * i + 1, :], rot[:, 2 * i + 1, :], c_["sin"], ALU.mult))
                link(tt(v, v, rot[:, 2 * i + 1, :], ALU.add))
                for p in range(3):
                    if p < 2:
                        nc.gpsimd.tensor_scalar(parts[:, i, p, :], v, 1.0, None, ALU.mult).then_inc(split_done[i], 1)
                        pool.wait_ge(split_done[i], 3 * b + p + 1)
                    if p == 0:
                        link(tt(v, v, parts[:, i, 0, :], ALU.subtract))
                    if p == 1:
                        tt(parts[:, i, 2, :], v, parts[:, i, 1, :], ALU.subtract).then_inc(split_done[i], 1)

            def max_split(G):
                pool.wait_ge(maxT_done, G + 1)
                if G >= 2:
                    pool.wait_ge(maxrow_ld[G % 2], 48 * (G // 2))
                v = maxT[:, G % 2, :]
                o = maxp[:, G % 2, :, :]
                link(nc.gpsimd.tensor_scalar(o[:, 0, :], v, 1.0, None, ALU.mult))
                link(tt(v, v, o[:, 0, :], ALU.subtract))
                link(nc.gpsimd.tensor_scalar(o[:, 1, :], v, 1.0, None, ALU.mult))
                tt(o[:, 2, :], v, o[:, 1, :], ALU.subtract).then_inc(maxp_done, 1)

            def deviation(k, b):
                pool.wait_ge(stat_done[k], b + 1)
                link(nc.gpsimd.tensor_scalar(var[:, b, :], mv[:, b, :, 1], LN_EPS, None, ALU.add))
                tt(rstd[:, b, :], var[:, b, :], minus_half[:, :], ALU.pow).then_inc(rstd_done[k], 1)

            def add_row(name, b):
                v = res[:, b * NT:(b + 1) * NT, :]
                tt(v, v, c_[name].unsqueeze(1).to_broadcast([P, NT, D]), ALU.add).then_inc(bias_done, 1)

            def beside_pool(kind, a, m):
                if kind == "rope" and m % 2 == 1 and (a or m == 1):
                    rope_split(a, m // 2)
                if kind == "max":
                    max_split(a)
                if kind == "norm":
                    deviation(0, a)
                if kind == "norm1":
                    deviation(1, a)
                if kind == "norm2":
                    deviation(2, a)
                if kind == "norm3":
                    deviation(3, a)
                if kind == "x2T":
                    pool.wait_ge(resT_done, NB + a + 1)
                    add_row("bo1_row", a)
                if kind == "x3T":
                    pool.wait_ge(resT_done, 2 * NB + a + 1)
                    add_row("lb_row", a)
                if kind == "Q":
                    i = 4 * a + m
                    pool.wait_ge(expq_done, i + 1)
                    if i >= 2:
                        pool.wait_ge(qf_done, i - 1)
                    nc.gpsimd.tensor_scalar(mq_[:, i % 2, :], eq_[:, i % 2, :], 1.0, None, ALU.min).then_inc(minq_done, 1)

            link(nc.gpsimd.memset(minus_half[:, :], -0.5))
            for s in prologue[:4]:
                beside_pool(*s)
            pool.wait_ge(split_done[0], 3)
            link(nc.gpsimd.memset(wide(QS[1], 64, KROW), 0.0))
            link(nc.gpsimd.memset(wide(KS[1], 64, KROW), 0.0))
            nc.gpsimd.memset(wide(KS[1], KROW, P), TWO_ONES).then_inc(init_pool, 1)
            pool.wait_ge(init_pool, 1)
            for s in prologue[4:]:
                beside_pool(*s)
            link(nc.gpsimd.memset(onesb[:, :], 1.0))
            nc.gpsimd.memset(V36[:, :, :, :], 1.0).then_inc(init_pool, 1)
            pool.wait_ge(init_pool, 2)
            pool.wait_ge(x_ld, 32)
            pool.wait_ge(late_ld, 48)
            for w in range(HALVES):
                for s in slots[w]:
                    beside_pool(*s)
                if w % 32 == 6:
                    add_row("bout_row", w // 32)
            for one in beside + [layer2]:
                for s in one:
                    beside_pool(*s)

        @block.tensor
        def _(pe):
            mm = nc.tensor.matmul
            tr = nc.tensor.transpose

            def scores_for_max(u):
                G, i = divmod(u, HG * NT)
                b, h, qt = G // NG, HG * (G % NG) + i // NT, i % NT
                if i == 0 and G == 0:
                    pe.wait_ge(qk_first, 96)
                if i == 0 and (G == 1 or G and G % NG == 0):
                    pe.wait_ge(qk_ld[b % 2], 96 * (b // 2 + 1))
                if u >= 2:
                    pe.wait_ge(sm_free, u - 1)
                mm(ps[4 + u % 2][:, :], QS[b % 2][0:KROW, h, qt * P:(qt + 1) * P], KS[b % 2][0:KROW, h, :],
                   start=True, stop=True).then_inc(sm_full, 1)

            def scores(w):
                n, hf = divmod(w, 2)
                G, kt = divmod(n, NT)
                b = G // NG
                if kt == 0 and hf == 0:
                    pe.wait_ge(maxrow_ld[G % 2], 48 * (G // 2 + 1))
                if w >= 2:
                    pe.wait_ge(exp_done, w - 1)
                for j in range(2):
                    h = HG * (G % NG) + 2 * hf + j
                    last_ = mm(ps[2 * hf + j][:, :], KS[b % 2][0:KROW + 3, h, kt * P:(kt + 1) * P],
                               QS[b % 2][0:KROW + 3, h, :], start=True, stop=True)
                last_.then_inc(s_full, 1)

            def values(n):
                G, kt = divmod(n, NT)
                b = G // NG
                pe.wait_ge(exp_done, 2 * n + 2)
                if n % (NG * NT) == 0:
                    pe.wait_ge(v_done, b + 1)
                if kt == 0 and G:
                    pe.wait_ge(o_evac, G)
                for j in range(HG):
                    h = HG * (G % NG) + j
                    last_ = mm(ps[6][32 * j:32 * j + 32, :], VA[b % 2][:, kt, h, :], probs[:, n % 2, j, :],
                               start=(kt == 0), stop=(kt == NT - 1), tile_position=(0, 32 * j))
                last_.then_inc(pv_done, 1)

            def beside_pe(kind, b, m):
                if kind in ("norm", "norm1", "norm2", "norm3", "chunk"):
                    return
                u = (kind, b, m)
                o = bank_of(u)

                def tile_of(t):
                    return xT[:, b * T + t * P:b * T + (t + 1) * P]

                def cols(t, n_=P):
                    return o[:, t * n_:(t + 1) * n_]

                if kind == "heads" and m == 0:
                    pe.wait_ge(o_evac, NG * (b + 1))
                if kind == "attnT":
                    pe.wait_ge(attn_done, NT * (b + 1))
                if kind == "AT":
                    pe.wait_ge(attn_done, NB * NT + 2 * (b + 1))
                if kind == "proj":
                    pe.wait_ge(attnT_done, b + 1)
                    if b == 0:
                        pe.wait_ge(late_ld, 48)
                if kind == "Y1":
                    pe.wait_ge(attnT_done, NB + b + 1)
                if kind in ("resT", "x2T", "x3T"):
                    pe.wait_ge(res_done[("resT", "x2T", "x3T").index(kind)], b + 1)
                if kind == "gate":
                    pe.wait_ge(resT_done, b + 1)
                if kind == "combine":
                    pe.wait_ge(cparts_done, b + 1)
                if kind == "K" and m == 0:
                    pe.wait_ge(resT_done, NB + b + 1)
                    pe.wait_ge(wr_done, 2)
                    pe.wait_ge(ks_ld, 48)
                if kind == "KV":
                    pe.wait_ge(kf_done, 4 * (b + 1))
                    pe.wait_ge(v36_done, b + 1)
                if kind == "O" and m == 0:
                    pe.wait_ge(kvb_done, b + 1)
                    pe.wait_ge(qf_done, 4 * (b + 1))
                if kind == "lg":
                    pe.wait_ge(resT_done, 2 * NB + b + 1)
                if kind == "ghT":
                    pe.wait_ge(gh_done, b + 1)
                if kind == "Y2":
                    pe.wait_ge(ghT_done, b + 1)
                wait_free(pe, u)

                if kind == "rope":
                    if b == 1 and m == 0:
                        pe.wait_ge(x_ld, 32)
                    last_ = mm(o[:, :], c_["w_qkv"][:, m * D:(m + 1) * D], xT[:, b * T:(b + 1) * T], start=True, stop=True)
                if kind == "val":
                    for t in range(NT):
                        last_ = mm(cols(t), tile_of(t), c_["w_qkv"][:, 4 * D:], start=True, stop=True)
                if kind == "max":
                    pe.wait_ge(sm_free, HG * NT * (b + 1))
                    last_ = mm(o[0:HG * NT, 0:P], negmax[:, b % 4, :], ident, start=True, stop=True)
                if kind == "heads":
                    for g in range(NG):
                        last_ = tr(cols(g), OU[:, b % 2, g, m * P:(m + 1) * P], ident)
                if kind in ("attnT", "AT"):
                    for t in range(NT):
                        last_ = tr(cols(t), attn[:, b % 2, t, :], ident)
                if kind in ("proj", "Y1"):
                    for t in range(NT):
                        last_ = mm(cols(t), attnT[:, t * P:(t + 1) * P], c_["w_out" if kind == "proj" else "wo1"],
                                   start=True, stop=True)
                if kind in ("resT", "x2T", "x3T"):
                    for t in range(NT):
                        last_ = tr(cols(t), res[:, b * NT + t, :], ident)
                if kind == "gate":
                    for t in range(NT):
                        last_ = mm(cols(t, E0), tile_of(t), c_["wg"], start=True, stop=True)
                if kind == "combine":
                    for t in range(NT):
                        last_ = mm(o[0:3 * E0, t * P:(t + 1) * P], cparts[:, t, :], identb[:, :], start=True, stop=True)
                if kind == "wR":
                    last_ = mm(o[:, :], c_[("wqT", "wkT")[m]], c_["rbd"], start=True, stop=True)
                if kind == "qb":
                    for c in range(4):
                        last_ = mm(cols(c, 1), c_["rbd"][:, c * P:(c + 1) * P], c_["bq_col"], start=True, stop=True)
                if kind == "kb":
                    last_ = mm(o[:, :], c_["bk_rep"], c_["rbd"], start=True, stop=True)
                if kind == "K":
                    mm(o[:, :], tile_of(m), wkR[:, :], start=True, stop=False)
                    last_ = mm(o[:, :], onesb[:, :], kstack[:, :], start=False, stop=True)
                if kind == "V":
                    for t in range(NT):
                        last_ = mm(cols(t), tile_of(t), c_["wv1"], start=True, stop=True)
                if kind == "Q":
                    last_ = mm(o[:, :], wqR[:, m * P:(m + 1) * P], xT[:, b * T:(b + 1) * T], start=True, stop=True)
                if kind == "KV":
                    for c in range(4):
                        for t in range(NT):
                            last_ = mm(cols(c, KVW), KF[:, t, c * P:(c + 1) * P], V36[:, t, c, :],
                                       start=(t == 0), stop=(t == NT - 1))
                if kind == "O":
                    for t in range(2):
                        for c in range(4):
                            last_ = mm(cols(t * 4 + c, KVW), QF[:, b % 2, c, (2 * m + t) * P:(2 * m + t + 1) * P],
                                       KVB[:, c, :], start=True, stop=True)
                if kind == "lg":
                    for t in range(NT):
                        last_ = mm(cols(t, E1), tile_of(t), c_["lr"], start=True, stop=True)
                    last_.then_inc(fullness(u), 1)
                    u = ("lh", b, 0)
                    wait_free(pe, u)
                    for t in range(NT):
                        last_ = mm(bank_of(u)[:, t * P:(t + 1) * P], tile_of(t), c_["la"], start=True, stop=True)
                if kind == "ghT":
                    for t in range(NT):
                        last_ = tr(cols(t), gh[:, t, :], ident)
                if kind == "Y2":
                    for t in range(NT):
                        mm(cols(t), tile_of(t), c_["lw"], start=True, stop=False)
                        last_ = mm(cols(t), ghT[:, t * P:(t + 1) * P], c_["lb"], start=False, stop=True)
                last_.then_inc(fullness(u), 1)

            pe.wait_ge(early_ld, 32)
            for s in prologue[:-1]:
                beside_pe(*s)
            for u in range(HG * NT):
                scores_for_max(u)
            beside_pe(*prologue[-1])
            for u in range(HG * NT, 2 * HG * NT):
                scores_for_max(u)
            scores(0)
            scores(1)
            for w in range(HALVES):
                if w + 2 < HALVES:
                    scores(w + 2)
                G = w // 8
                if G + 2 < GROUPS:
                    for i in range(2):
                        scores_for_max((G + 2) * HG * NT + 2 * (w % 8) + i)
                for s in slots[w]:
                    beside_pe(*s)
                if w % 2:
                    values(w // 2)

            def down(i):
                b, p = divmod(i, PAIRS)
                pe.wait_ge(hid_done, i + 1)
                u = ("y_e", b, 0)
                if p == 0:
                    if b == 1:
                        pe.wait_ge(o_evac, GROUPS)
                    wait_free(pe, u)
                w2 = c_["w2s"] if p == EP else c_["w2"][:, p * D:(p + 1) * D]
                for t in range(NT):
                    last_ = mm(bank_of(u)[:, t * D:(t + 1) * D], hid[:, i % 3, t * P:(t + 1) * P], w2,
                               start=(p == 0 and t == 0), stop=(p == EP and t == NT - 1), skip_group_check=True)
                last_.then_inc(down_done, 1)

            pe.wait_ge(exp_done, HALVES)
            pe.wait_ge(sm_free, GROUPS * HG * NT)
            for i in range(NB * PAIRS):
                b, p = divmod(i, PAIRS)
                for kind, w, ws in (("gate_e", "w1", "w1s"), ("up_e", "w3", "w3s")):
                    u = (kind, i, 0)
                    wait_free(pe, u)
                    wt = c_[ws] if p == EP else c_[w][:, p * 2 * F0:(p + 1) * 2 * F0]
                    mm(bank_of(u)[:, :], wt, xT[:, b * T:(b + 1) * T], start=True, stop=True).then_inc(fullness(u), 1)
                if p < EP:
                    u = ("comb_e", i, 0)
                    wait_free(pe, u)
                    if p == 0:
                        pe.wait_ge(cT_done, b + 1)
                    mm(bank_of(u)[:, :], sel[:, p, :], cT[:, b, :], start=True, stop=True).then_inc(fullness(u), 1)
                if i:
                    down(i - 1)
                for s in beside[i]:
                    beside_pe(*s)
            down(NB * PAIRS - 1)
            for s in layer2:
                beside_pe(*s)

        @block.scalar
        def _(act):
            fn = nc.scalar.activation

            def exps(w):
                n, hf = divmod(w, 2)
                act.wait_ge(s_full, w + 1)
                if n >= 2:
                    act.wait_ge(pv_done, n - 1)
                fn(probs[:, n % 2, 2 * hf:2 * hf + 2, :], psum[:, 2 * hf:2 * hf + 2, :], ACT.Exp,
                   scale=float(DH) ** -0.5).then_inc(exp_done, 1)

            def outputs(G):
                b = G // NG
                act.wait_ge(pv_done, NT * (G + 1))
                if b >= 2 and G % NG == 0:
                    wait_full(act, ("heads", b - 2, 3))
                fn(OU[:, b % 2, G % NG, :], ps[6][:, :], ACT.Copy).then_inc(o_evac, 1)

            def beside_act(kind, a, m):
                u = (kind, a, m)
                if kind == "rope" and a:
                    wait_full(act, u)
                    act.wait_ge(split_done[m // 2], 3 * a)
                    fn(rot[:, m, :], bank_of(u)[:, :], ACT.Identity, bias=c_["b_rope"][:, m:m + 1]).then_inc(rot_done, 1)
                if kind == "max":
                    wait_full(act, u)
                    if a >= 2:
                        act.wait_ge(maxp_done, a - 1)
                    fn(maxT[:, a % 2, :], bank_of(u)[0:HG * NT, 0:P], ACT.Copy).then_inc(maxT_done, 1)
                if kind in ("attnT", "AT"):
                    wait_full(act, u)
                    if kind == "AT" and a:
                        wait_full(act, ("Y1", a - 1, 0))
                    if kind == "AT" and not a:
                        wait_full(act, ("proj", last, 0))
                    if kind == "attnT" and a:
                        wait_full(act, ("proj", a - 1, 0))
                    fn(attnT[:, :], bank_of(u)[:, :], ACT.Copy).then_inc(attnT_done, 1)
                if kind in ("resT", "x2T", "x3T"):
                    wait_full(act, u)
                    if kind == "x2T":
                        act.wait_ge(down_done, (a + 1) * PAIRS)
                    fn(xT[:, a * T:(a + 1) * T], bank_of(u)[:, :], ACT.Copy).then_inc(resT_done, 1)
                if kind == "gate":
                    wait_full(act, u)
                    if a:
                        act.wait_ge(cparts_done, a)
                    fn(rt[:, 0, :], bank_of(u)[:, 0:NT * E0], ACT.Exp, scale=-1.0).then_inc(expneg_done, 1)
                if kind == "combine":
                    wait_full(act, u)
                    fn(cT[:, a, :], bank_of(u)[0:3 * E0, :], ACT.Copy).then_inc(cT_done, 1)
                if kind == "wR":
                    wait_full(act, u)
                    fn((wqR, wkR)[m][:, :], bank_of(u)[:, :], ACT.Copy).then_inc(wr_done, 1)
                if kind == "K":
                    i = 4 * a + m
                    wait_full(act, u)
                    if i >= 2:
                        act.wait_ge(kf_done, i - 1)
                    fn(ek_[:, i % 2, :], bank_of(u)[:, :], ACT.Exp, bias=minus1[:, 0:1]).then_inc(expk_done, 1)
                if kind == "Q":
                    i = 4 * a + m
                    wait_full(act, u)
                    if i == 0:
                        act.wait_ge(row_done, 1)
                    if i >= 2:
                        act.wait_ge(minq_done, i - 1)
                    fn(eq_[:, i % 2, :], bank_of(u)[:, :], ACT.Exp, bias=qb[:, m:m + 1]).then_inc(expq_done, 1)
                if kind == "lg":
                    act.wait_ge(lsub_done, a + 1)
                    fn(rt[:, 1, 0:NT * E1], rt[:, 0, 0:NT * E1], ACT.Exp).then_inc(lexp_done, 1)
                if kind == "ghT":
                    wait_full(act, u)
                    if a:
                        wait_full(act, ("Y2", a - 1, 0))
                    fn(ghT[:, :], bank_of(u)[:, :], ACT.Copy).then_inc(ghT_done, 1)

            act.wait_ge(init_dve, 2)
            for s in prologue:
                beside_act(*s)
            for w in range(HALVES):
                exps(w)
                if w % 8 == 1 and w > 8:
                    outputs(w // 8 - 1)
                for s in slots[w]:
                    beside_act(*s)
            outputs(GROUPS - 1)
            for i in range(NB * PAIRS):
                u = ("gate_e", i, 0)
                wait_full(act, u)
                if i >= 2:
                    act.wait_ge(hid_done, i - 1)
                fn(gate_s[:, i % 2, :], bank_of(u)[:, :], ACT.Silu).then_inc(silu_done, 1)
                for s in beside[i]:
                    beside_act(*s)
            for s in layer2:
                beside_act(*s)

        @block.vector
        def _(dve):
            V = nc.vector
            n = [0]

            def link(ins):
                n[0] += 1
                ins.then_inc(dve_chain, 1)
                dve.wait_ge(dve_chain, n[0])

            def after(ins):
                n[0] += 1
                at = n[0]
                ins.then_inc(dve_chain, 1)
                yield
                dve.wait_ge(dve_chain, at)

            running = []

            def step(count):
                for _ in range(count):
                    while running and next(running[0], "end") == "end":
                        running.pop(0)
                        if not running:
                            return

            def finish():
                while running:
                    step(1)

            def tt(o, a, b, op):
                return V.tensor_tensor(out=o, in0=a, in1=b, op=op)

            def r3(k, e):
                return rt[:, k, 0:NT * e].rearrange("p (t e) -> p t e", e=e)

            def add_residual(k, b, y):
                if k == 1:
                    dve.wait_ge(res_done[0], b + 1)
                else:
                    dve.wait_ge(bias_done, NB * (0, 0, 1, 2)[k] + b + 1)
                if k == 3:
                    dve.wait_ge(res_done[2], b + 1)
                elif b >= 2:
                    dve.wait_ge(res_done[3 if k == 2 else k], b - 1)
                elif k:
                    dve.wait_ge(res_done[k - 1], b + 3)
                tt(z[:, b % 2, :, :], y.rearrange("p (t d) -> p t d", d=D), res[:, b * NT:(b + 1) * NT, :], ALU.add)\
                    .then_inc(sum_done[k], 1)

            def statistics(k, b):
                dve.wait_ge(sum_done[k], b + 1)
                for t in range(NT):
                    ins = V.bn_stats(stats[:, t, :], z[:, b % 2, t, :])
                    if t < NT - 1:
                        yield
                yield from after(ins)
                for t in range(NT):
                    ins = V.bn_aggr(mv[:, b, t, :], stats[:, t, :])
                ins.then_inc(stat_done[k], 1)
                yield

            def normalise(k, b):
                dve.wait_ge(rstd_done[k], b + 1)
                target = outb if k == 3 else res
                for t in range(NT):
                    ins = V.tensor_scalar(target[:, b * NT + t, :], z[:, b % 2, t, :], mv[:, b, t, 0:1],
                                          rstd[:, b, t:t + 1], ALU.subtract, ALU.mult)
                    if t == NT - 1:
                        ins.then_inc(res_done[k], 1)
                    yield

            def top(vals, m8, k, e, at, reset):
                thr = m8[:, :, k - 1:k].to_broadcast([P, NT, e])
                gt, eq, inc, le = (r3(at + i, e) for i in range(4))
                cnt = rt[:, at + 4, 0:NT]
                tt(eq, vals, thr, ALU.is_equal)
                yield from after(tt(gt, vals, thr, ALU.is_gt))
                V.tensor_tensor_scan(rt[:, at + 2, 0:NT * e], c_[reset], rt[:, at + 1, 0:NT * e], 0.0, ALU.mult, ALU.add)
                yield from after(V.reduce_sum(cnt, gt, X))
                yield from after(V.tensor_scalar(cnt, cnt, -1.0, float(k), ALU.mult, ALU.add))
                yield from after(tt(le, inc, cnt.unsqueeze(2).to_broadcast([P, NT, e]), ALU.is_le))
                yield from after(tt(eq, eq, le, ALU.mult))
                yield from after(tt(gt, gt, eq, ALU.add))

            def route(a):
                dve.wait_ge(expneg_done, a + 1)
                s = r3(1, E0)
                yield from after(V.tensor_scalar(rt[:, 0, :], rt[:, 0, :], 1.0, None, ALU.add))
                yield from after(V.reciprocal(rt[:, 1, :], rt[:, 0, :]))
                sg = rt[:, 1, :].rearrange("p (g e) -> p g e", e=4)
                pr = rt[:, 2:4, :].rearrange("p a n -> p (a n)")[:, 0:96].rearrange("p (g e) -> p g e", e=6)
                tt(pr[:, :, 0:3], sg[:, :, 0:3], sg[:, :, 1:4], ALU.add)
                tt(pr[:, :, 3:5], sg[:, :, 0:2], sg[:, :, 2:4], ALU.add)
                gs = r3(4, 8)
                V.memset(gs[:, :, 4:8], -1.0)
                yield from after(tt(pr[:, :, 5:6], sg[:, :, 0:1], sg[:, :, 3:4], ALU.add))
                yield from after(V.tensor_reduce(out=gs[:, :, 0:4], in_=pr.rearrange("p (t g) e -> p t g e", g=4), axis=X,
                                                 op=ALU.max))
                m8 = r3(5, 8)
                for t in range(NT):
                    ins = V.max(m8[:, t, :], gs[:, t, :])
                yield from after(ins)
                yield from top(gs, m8, 2, 8, 6, "reset8")
                allow = r3(6, 8)[:, :, 0:4]
                am1 = r3(11, 4)
                V.tensor_scalar(am1, allow, -1.0, None, ALU.add)
                mk = rt[:, 12, :].rearrange("p (t g e) -> p t g e", g=4, e=4)
                s44 = rt[:, 1, :].rearrange("p (t g e) -> p t g e", g=4, e=4)
                yield from after(tt(mk, s44, allow.unsqueeze(3).to_broadcast([P, NT, 4, 4]), ALU.mult))
                yield from after(tt(mk, mk, am1.unsqueeze(3).to_broadcast([P, NT, 4, 4]), ALU.add))
                masked = r3(12, E0)
                for t in range(NT):
                    ins = V.max(m8[:, t, :], masked[:, t, :])
                yield from after(ins)
                yield from top(masked, m8, 4, E0, 13, "reset16")
                w = r3(18, E0)
                yield from after(tt(w, s, r3(13, E0), ALU.mult))
                tot = rt[:, 19, 0:NT]
                yield from after(V.reduce_sum(tot, w, X))
                yield from after(V.tensor_scalar(tot, tot, 1e-6, None, ALU.add))
                yield from after(V.reciprocal(tot, tot))
                yield from after(tt(w, w, tot.unsqueeze(2).to_broadcast([P, NT, E0]), ALU.mult))
                if a:
                    wait_full(dve, ("combine", a - 1, 0))
                yield from after(V.tensor_copy(cparts[:, :, 0:E0], w))
                yield from after(tt(w, w, cparts[:, :, 0:E0], ALU.subtract))
                yield from after(V.tensor_copy(cparts[:, :, E0:2 * E0], w))
                tt(cparts[:, :, 2 * E0:], w, cparts[:, :, E0:2 * E0], ALU.subtract).then_inc(cparts_done, 1)
                yield

            def lora_gates(b):
                dve.wait_ge(lexp_done, b + 1)
                e = r3(1, E1)
                tot = rt[:, 3, 0:NT]
                yield from after(V.reduce_sum(tot, e, X))
                yield from after(V.reciprocal(tot, tot))
                yield from after(tt(gate8[:, :, :], e, tot.unsqueeze(2).to_broadcast([P, NT, E1]), ALU.mult))
                m8 = r3(5, 8)
                for t in range(NT):
                    ins = V.max(m8[:, t, :], gate8[:, t, :])
                yield from after(ins)
                yield from top(gate8[:, :, :], m8, 2, E1, 6, "reset8")
                yield from after(tt(gate8[:, :, :], gate8[:, :, :], r3(6, E1), ALU.mult))
                yield from after(V.reduce_sum(tot, gate8[:, :, :], X))
                yield from after(V.tensor_scalar(tot, tot, 1e-6, None, ALU.add))
                yield from after(V.reciprocal(tot, tot))
                yield from after(tt(gate8[:, :, :], gate8[:, :, :], tot.unsqueeze(2).to_broadcast([P, NT, E1]), ALU.mult))
                u = ("lh", b, 0)
                wait_full(dve, u)
                if b:
                    wait_full(dve, ("ghT", b - 1, 0))
                for t in range(NT):
                    ins = tt(gh[:, t, :].rearrange("p (e r) -> p e r", r=R1),
                             bank_of(u)[:, t * P:(t + 1) * P].rearrange("p (e r) -> p e r", r=R1),
                             gate8[:, t, :].unsqueeze(2).to_broadcast([P, E1, R1]), ALU.mult)
                    if t < NT - 1:
                        yield
                ins.then_inc(gh_done, 1)
                yield

            def reduce_scores(u):
                G, i = divmod(u, HG * NT)
                dve.wait_ge(sm_full, u + 1)
                if i == 0 and G >= 4:
                    wait_full(dve, ("max", G - 4, 0))
                V.tensor_reduce(out=negmax[:, G % 4, i:i + 1], in_=ps[4 + u % 2][:, :], axis=X, op=ALU.max,
                                negate=True).then_inc(sm_free, 1)

            def beside_dve(kind, a, m):
                u = (kind, a, m)
                if kind == "rope" and a == 0:
                    wait_full(dve, u)
                    V.scalar_tensor_tensor(out=rot[:, m, :], in0=bank_of(u)[:, :], scalar=c_["b_rope"][:, m:m + 1],
                                           in1=c_["cos"] if m % 2 == 0 else c_["sin"],
                                           op0=ALU.add, op1=ALU.mult).then_inc(rot_done, 1)
                    if m == 3:
                        dve.wait_ge(rot_done, 4)
                        v = rot[:, 2, :]
                        link(tt(v, v, rot[:, 3, :], ALU.add))
                        V.tensor_copy(parts[:, 1, 0, :], v).then_inc(split_done[1], 1)
                        dve.wait_ge(split_done[1], 1)
                        link(tt(v, v, parts[:, 1, 0, :], ALU.subtract))
                        V.tensor_copy(parts[:, 1, 1, :], v).then_inc(split_done[1], 1)
                        dve.wait_ge(split_done[1], 2)
                        tt(parts[:, 1, 2, :], v, parts[:, 1, 1, :], ALU.subtract).then_inc(split_done[1], 1)
                if kind == "val":
                    wait_full(dve, u)
                    if a >= 2:
                        dve.wait_ge(pv_done, NG * NT * (a - 1))
                    for t in range(NT):
                        ins = tt(VA[a % 2][:, t, :, 0:DH], bank_of(u)[:, t * D:(t + 1) * D].rearrange("p (h d) -> p h d", d=DH),
                                 c_["bv_row"].rearrange("p (h d) -> p h d", d=DH), ALU.add)
                    ins.then_inc(v_done, 1)
                if kind == "heads":
                    wait_full(dve, u)
                    if a >= 2 and m == 0:
                        wait_full(dve, ("attnT", a - 2, 0))
                    v = bank_of(u)[:, :].rearrange("p (h c) -> p h c", c=32)
                    link(V.reciprocal(rden[:, m, :], v[:, :, DH]))
                    tt(attn[:, a % 2, m, :].rearrange("p (h d) -> p h d", d=DH), v[:, :, 0:DH],
                       rden[:, m, :].unsqueeze(2).to_broadcast([P, H, DH]), ALU.mult).then_inc(attn_done, 1)
                if kind in ("proj", "Y1", "Y2"):
                    wait_full(dve, u)
                    k = {"proj": 0, "Y1": 2, "Y2": 3}[kind]
                    add_residual(k, a, bank_of(u)[:, :])
                    running.append(statistics(k, a))
                if kind == "chunk":
                    dve.wait_ge(down_done, (a + 1) * PAIRS)
                    add_residual(1, a, bank_of(("y_e", a, 0))[:, :])
                    running.append(statistics(1, a))
                if kind in ("norm", "norm1", "norm2", "norm3", "resT", "x2T", "x3T", "combine", "ghT"):
                    finish()
                if kind[:4] == "norm":
                    running.append(normalise(int(kind[4:] or 0), a))
                if kind == "gate":
                    running.append(route(a))
                if kind == "qb":
                    wait_full(dve, u)
                    V.tensor_copy(qb[:, :], bank_of(u)[:, 0:4])
                    V.tensor_scalar(qb1[:, :], bank_of(u)[:, 0:4], 1.0, None, ALU.add).then_inc(row_done, 1)
                if kind == "kb":
                    wait_full(dve, u)
                    V.tensor_scalar(kbias[:, :], bank_of(u)[:, :], 1.0, None, ALU.add).then_inc(row_done, 1)
                    dve.wait_ge(row_done, 2)
                    link(V.tensor_copy(kparts[0:1, 0, :], kbias[0:1, :]))
                    link(tt(kbias[0:1, :], kbias[0:1, :], kparts[0:1, 0, :], ALU.subtract))
                    link(V.tensor_copy(kparts[0:1, 1, :], kbias[0:1, :]))
                    tt(kparts[0:1, 2, :], kbias[0:1, :], kparts[0:1, 1, :], ALU.subtract).then_inc(kb_done, 1)
                if kind == "K":
                    i = 4 * a + m
                    dve.wait_ge(expk_done, i + 1)
                    if a and m == 0:
                        wait_full(dve, ("KV", a - 1, 0))
                    V.scalar_tensor_tensor(out=KF[:, m, :], in0=ek_[:, i % 2, :], scalar=1.0, in1=bank_of(u)[:, :],
                                           op0=ALU.min, op1=ALU.max).then_inc(kf_done, 1)
                    step(3)
                if kind == "V":
                    wait_full(dve, u)
                    if a:
                        wait_full(dve, ("KV", a - 1, 0))
                    for t in range(NT):
                        ins = tt(V36[:, t, :, 0:HG * DH],
                                 bank_of(u)[:, t * D:(t + 1) * D].rearrange("p (c d) -> p c d", c=NG),
                                 c_["bv1_row"].rearrange("p (c d) -> p c d", c=NG), ALU.add)
                    ins.then_inc(v36_done, 1)
                    step(3)
                if kind == "Q":
                    i = 4 * a + m
                    dve.wait_ge(minq_done, i + 1)
                    if a >= 2 and m == 0:
                        wait_full(dve, ("O", a - 2, 1))
                    V.scalar_tensor_tensor(out=QF[:, a % 2, m, :], in0=bank_of(u)[:, :], scalar=qb1[:, m:m + 1],
                                           in1=mq_[:, i % 2, :], op0=ALU.add, op1=ALU.max).then_inc(qf_done, 1)
                    step(3)
                if kind == "KV":
                    wait_full(dve, u)
                    if a:
                        wait_full(dve, ("O", a - 1, 1))
                    tt(KVB[:, :, :], bank_of(u)[:, 0:4 * KVW].rearrange("p (c k) -> p c k", k=KVW),
                       c_["mask"].unsqueeze(1).to_broadcast([P, NG, KVW]), ALU.mult).then_inc(kvb_done, 1)
                    step(8)
                if kind == "O":
                    wait_full(dve, u)
                    if m == 0 and a >= 2:
                        wait_full(dve, ("AT", a - 2, 0))
                    v = bank_of(u)[:, 0:8 * KVW].rearrange("p (tc k) -> p tc k", k=KVW)
                    nrm = rt[:, 20, 0:32].rearrange("p (tc h) -> p tc h", h=HG)
                    link(V.tensor_scalar(nrm, v[:, :, HG * DH:], 256e-6, None, ALU.max))
                    link(V.reciprocal(rt[:, 21, 0:32], rt[:, 20, 0:32]))
                    for t in range(2):
                        ins = tt(attn[:, a % 2, 2 * m + t, :].rearrange("p (c h d) -> p c h d", h=HG, d=DH),
                                 v[:, 4 * t:4 * t + 4, 0:32].rearrange("p c (h d) -> p c h d", d=DH),
                                 rt[:, 21, 16 * t:16 * t + 16].rearrange("p (c h) -> p c h", h=HG).unsqueeze(3)
                                 .to_broadcast([P, NG, HG, DH]), ALU.mult)
                    ins.then_inc(attn_done, 1)
                    step(8)
                if kind == "lg":
                    wait_full(dve, u)
                    lg = bank_of(u)[:, 0:NT * E1].rearrange("p (t e) -> p t e", e=E1)
                    mx = rt[:, 2, 0:NT]
                    link(V.tensor_reduce(out=mx, in_=lg, axis=X, op=ALU.max))
                    tt(r3(0, E1), lg, mx.unsqueeze(2).to_broadcast([P, NT, E1]), ALU.subtract).then_inc(lsub_done, 1)
                    running.append(lora_gates(a))

            V.memset(wide(QS[0], 64, KROW), 0.0)
            V.memset(wide(KS[0], 64, KROW), 0.0)
            V.memset(wide(KS[0], KROW, P), TWO_ONES).then_inc(init_dve, 1)
            V.memset(minus1[:, :], -1.0).then_inc(init_dve, 1)
            dve.wait_ge(early_ld, 32)
            for s in prologue[:4]:
                beside_dve(*s)
            for i in range(2):
                V.memset(VA[i][:, :, :, DH + 1:], 0.0)
                V.memset(VA[i][:, :, :, DH:DH + 1], 1.0)
            beside_dve(*prologue[4])
            for u in range(2 * HG * NT):
                reduce_scores(u)
            for w in range(HALVES):
                G = w // 8
                for i in range(2):
                    if G + 2 < GROUPS:
                        reduce_scores((G + 2) * HG * NT + 2 * (w % 8) + i)
                    step(2)
                for s in slots[w]:
                    beside_dve(*s)
            finish()

            for i in range(NB * PAIRS):
                b, p = divmod(i, PAIRS)
                u = ("up_e", i, 0)
                dve.wait_ge(silu_done, i + 1)
                wait_full(dve, u)
                if i >= 3:
                    dve.wait_ge(down_done, i - 2)
                if p == EP:
                    tt(hid[:, i % 3, :], gate_s[:, i % 2, :], bank_of(u)[:, :], ALU.mult).then_inc(hid_done, 1)
                else:
                    tt(prod[:, i % 2, :], gate_s[:, i % 2, :], bank_of(u)[:, :], ALU.mult).then_inc(prod_done, 1)
                    step(2)
                    dve.wait_ge(prod_done, b * EP + p + 1)
                    c = ("comb_e", i, 0)
                    wait_full(dve, c)
                    tt(hid[:, i % 3, :], prod[:, i % 2, :], bank_of(c)[:, :], ALU.mult).then_inc(hid_done, 1)
                step(4)
                for s in beside[i]:
                    beside_dve(*s)
            finish()
            for s in layer2:
                beside_dve(*s)
            finish()


def rows(v):
    return np.broadcast_to(np.asarray(v)[None, :], (P, v.shape[0]))


def kernel(**inputs):
    import concourse.bacc as bacc
    from concourse.bass_utils import run_bass_kernel_spmd as run
    import ml_dtypes

    a = {k: np.asarray(v) for k, v in inputs.items()}
    x = a["L0_attn_x"].reshape(NB * T, D)
    d = np.arange(D)
    partner = d // DH * DH + (d % DH + DH // 2) % DH
    w, bq = a["L0_attn_W_qkv"], a["L0_attn_b_qkv"]
    wq, wk, wv = w[:, :D], w[:, D:2 * D], w[:, 2 * D:]
    b_q, b_k = bq[:D], bq[D:2 * D]
    inv = (1.0 / np.float32(10000.0) ** (np.arange(0, DH, 2, dtype=np.float32) / np.float32(DH))).astype(np.float32)
    ang = (np.arange(T, dtype=np.float32)[None, :] * inv[d % (DH // 2)][:, None]).astype(np.float64)
    sign = np.where(d % DH < DH // 2, -1.0, 1.0)[:, None]
    early = dict(w_qkv=np.concatenate([wq, wq[:, partner], wk, wk[:, partner], wv], 1),
                 b_rope=np.stack([b_q, b_q[partner], b_k, b_k[partner]], 1),
                 cos=np.cos(ang).astype(np.float32), sin=(np.sin(ang) * sign).astype(np.float32),
                 ident=np.eye(P, dtype=np.float32), bv_row=rows(bq[2 * D:]))
    r = a["L1_attn_random_matrix"]
    rbd = np.zeros((D, H * M1), np.float32)
    for h in range(H):
        rbd[h * DH:(h + 1) * DH, h * M1:(h + 1) * M1] = r
    f = np.arange(P)
    mask = np.zeros((P, KVW), np.float32)
    for h in range(HG):
        mask[h * M1:(h + 1) * M1, h * DH:(h + 1) * DH] = 1.0
        mask[h * M1:(h + 1) * M1, HG * DH + h] = 1.0

    def reset(e):
        v = np.ones((P, NT, e), np.float32)
        v[:, :, 0] = 0.0
        return v.reshape(P, NT * e)

    w2 = a["L0_ffn_w2_e"].transpose(0, 2, 1).reshape(EP, 2 * F0, D).transpose(1, 0, 2).reshape(P, EP * D)
    late = dict(w_out=a["L0_attn_W_out"], bout_row=rows(a["L0_attn_b_out"]), wg=a["L0_ffn_w_gate"].T,
                w1=a["L0_ffn_w1_e"].reshape(E0 * F0, D).T, w3=a["L0_ffn_w3_e"].reshape(E0 * F0, D).T, w2=w2,
                w1s=a["L0_ffn_w1_s"].T, w3s=a["L0_ffn_w3_s"].T, w2s=a["L0_ffn_w2_s"].T, reset16=reset(E0),
                wqT=a["L1_attn_Wq"].T, wkT=a["L1_attn_Wk"].T, wv1=a["L1_attn_Wv"], wo1=a["L1_attn_Wo"], rbd=rbd,
                bq_col=a["L1_attn_bq"][:, None], bk_rep=np.broadcast_to(a["L1_attn_bk"][:, None], (D, P)),
                bv1_row=rows(a["L1_attn_bv"]), bo1_row=rows(a["L1_attn_bo"]), mask=mask,
                lr=a["L1_ffn_R"].T, la=a["L1_ffn_A"].reshape(E1 * R1, D).T, lw=a["L1_ffn_W"].T,
                lb=a["L1_ffn_B"].transpose(0, 2, 1).reshape(E1 * R1, D), lb_row=rows(a["L1_ffn_b"]), reset8=reset(E1))
    sel = np.zeros((3, E0, EP, P), np.float32)
    for e in range(E0):
        sel[:, e, e // 2, (e % 2) * F0:(e % 2 + 1) * F0] = 1.0
    bf = ml_dtypes.bfloat16
    arrays = {
        "in_x": np.ascontiguousarray(x), "in_xT": np.ascontiguousarray(x.T),
        "in_early": np.ascontiguousarray(np.concatenate([early[k] for k in EARLY], 1)),
        "in_late": np.ascontiguousarray(np.concatenate([late[k] for k in LATE], 1)),
        "in_sel": sel.reshape(3 * E0, EP, P).astype(bf), "in_identb": np.eye(P).astype(bf),
    }
    nc = bacc.Bacc("TRN2", target_bir_lowering=False, num_devices=1)
    args = [nc.dram_tensor(k, v.shape, mybir.dt.from_np(v.dtype), kind="ExternalInput").ap() for k, v in arrays.items()]
    parts_dram = nc.dram_tensor("parts_dram", (NB, 2, 3, DH, H, T), BF16, kind="Internal").ap()
    out = nc.dram_tensor("out_y", (NB * T, D), F32, kind="ExternalOutput").ap()
    program(nc, *args, parts_dram, out)
    result = run(nc, [arrays], core_ids=[0])
    return result.results[0]["out_y"].reshape(NB, T, D)
```

```python
from contextlib import ExitStack

import numpy as np

import concourse.bass as bass
from concourse import mybir

P = 128
F32 = mybir.dt.float32
BF16 = mybir.dt.bfloat16
ALU = mybir.AluOpType
ACT = mybir.ActivationFunctionType
X = mybir.AxisListType.X

NB, T, D = 4, 512, 128
NT = T // P
H, DH = 16, 8
HG = 4
NG = H // HG
GROUPS = NB * NG
KROW = 96
AHEAD = 2 * HG * NT + 4
E0, F0, EP = 16, 64, 8
E1, R1 = 8, 16
M1 = 32
HW = HG * DH
KVW = HW + 1
LN_EPS = 1e-5
TWO_ONES = float(np.array([0x3F803F80], np.uint32).view(np.float32)[0])

EARLY = dict(w_kq=4 * D, b_rope=4, cos=T, sin=T, w_v=D, ident=P, bv_row=D)
LATE = dict(w_out=D, bout_row=D, wg=E0, w1=E0 * F0, w3=E0 * F0, w2=EP * D, w1s=D, w3s=D, w2s=D, reset16=NT * E0,
            wqT=D, wkT=D, wv1=D, wo1=D, rbd=H * M1, bq_rep=P, bk_rep=P, bv1_row=D, bo1_row=D, mask=HW,
            lr=E1, la=E1 * R1, lw=D, lb=D, lb_row=D, reset8=NT * E1)


def columns(widths):
    at, out = 0, {}
    for name, n in widths.items():
        out[name] = (at, at + n)
        at += n
    return out, at


EARLY_AT, EARLY_N = columns(EARLY)
LATE_AT, LATE_N = columns(LATE)


def program(nc, x_in, xT_in, early_in, late_in, sel_in, identb_in, parts_dram, out):
    with ExitStack() as ctx:
        def sb(name, shape, dt=F32):
            return ctx.enter_context(nc.sbuf_tensor(name, shape, dt))

        def sem(name):
            return ctx.enter_context(nc.semaphore(name))

        early = sb("early", [P, EARLY_N])
        late = sb("late", [P, LATE_N])
        c_ = {k: early[:, a:b] for k, (a, b) in EARLY_AT.items()}
        c_.update({k: late[:, a:b] for k, (a, b) in LATE_AT.items()})
        ident = c_["ident"]
        identb = sb("identb", [P, P], BF16)
        sel = sb("sel", [3 * E0, EP, P], BF16)
        xT = sb("xT", [P, NB * T])
        res = sb("res", [P, NB * NT, D])
        z = sb("z", [P, 3, NT, D])
        rot = sb("rot", [P, 4, T])
        parts = sb("parts", [P, 2, 3, T], BF16)
        QS = [sb(f"QS{i}", [P, H, T], BF16) for i in range(2)]
        KS = [sb(f"KS{i}", [P, H, T], BF16) for i in range(2)]
        VA = [sb(f"VA{i}", [P, NT, H, 32]) for i in range(2)]
        probs = sb("probs", [P, 2, HG, T])
        OU = sb("OU", [P, 2, NG, T])
        negmax = sb("negmax", [P, 4, HG * NT])
        maxT = sb("maxT", [HG * NT, 2, P])
        maxp = sb("maxp", [HG * NT, 2, 3, P], BF16)
        rden = sb("rden", [P, NT, H])
        attn = sb("attn", [P, 2, NT, D])
        attnT = sb("attnT", [P, T])
        stats = sb("stats", [P, NT, 6])
        mv = sb("mv", [P, NB, NT, 2])
        var = sb("var", [P, NB, NT])
        rstd = sb("rstd", [P, NB, NT])
        minus_half = sb("minus_half", [P, NT])
        minus1 = sb("minus1", [P, 1])
        rt = sb("rt", [P, 24, NT * E0])
        cT = sb("cT", [3 * E0, NB, T], BF16)
        cparts = sb("cparts", [P, NT, 3 * E0], BF16)
        onesb = sb("onesb", [3, T], BF16)
        VK = sb("VK", [P, NT, NG, KVW])
        KVB = sb("KVB", [P, 2, NG, HW])
        A0, A1 = (q[:, :, :].rearrange("p h t -> p (h t)").bitcast(F32) for q in QS)
        B0, B1 = (k[:, :, :].rearrange("p h t -> p (h t)").bitcast(F32) for k in KS)
        gate_s = A0[:, 0:2 * T].rearrange("p (i t) -> p i t", t=T)
        prod = A0[:, 2 * T:4 * T].rearrange("p (i t) -> p i t", t=T)
        hid = A0[:, 4 * T:7 * T].rearrange("p (i t) -> p i t", t=T)
        eq_ = B0[:, 0:2 * T].rearrange("p (i t) -> p i t", t=T)
        ek_ = B0[:, 2 * T:4 * T].rearrange("p (i t) -> p i t", t=T)
        gh = B0[:, 6 * T:7 * T].rearrange("p (n d) -> p n d", n=NT)
        ghT = B0[:, 7 * T:8 * T]
        QF = A1.rearrange("p (i c t) -> p i c t", i=2, c=NT)
        KF = B1[:, 0:4 * T].rearrange("p (n f) -> p n f", n=NT)
        outb = B1[:, 4 * T:8 * T].rearrange("p (n d) -> p n d", d=D)
        wqR, wkR, bias_row = (probs[:, 0, i, :] for i in range(3))
        bias_parts = probs[0:1, 1, 0:3, :].rearrange("p i t -> p (i t)").bitcast(BF16)\
            .rearrange("p (q i t) -> p q i t", q=2, i=3)
        bias_stack = probs[0:3, 1, 3, :].bitcast(BF16).rearrange("p (q t) -> p q t", q=2)
        gate8 = sb("gate8", [P, NT, E1])
        rl = sb("rl", [P, 11, NT * E1])

        psum = ctx.enter_context(nc.psum_tensor("psum", [P, 8, 512], F32))
        ps = [psum[:, i, :] for i in range(8)]

        x_ld, res_ld, rope_ld, table_ld, early_ld, late_ld, init_pool, init_dve = (
            sem(n) for n in ("x_ld", "res_ld", "rope_ld", "table_ld", "early_ld", "late_ld", "init_pool", "init_dve"))
        sm_full, sm_free, s_full, exp_done, pv_done, o_evac = (
            sem(n) for n in ("sm_full", "sm_free", "s_full", "exp_done", "pv_done", "o_evac"))
        ps_full = [sem(f"ps_full{i}") for i in range(8)]
        rot0_done, rot_done, v_done, maxT_done, maxp_done = (
            sem(n) for n in ("rot0_done", "rot_done", "v_done", "maxT_done", "maxp_done"))
        split_done = [sem(f"split_done{i}") for i in range(2)]
        parts_st = [sem(f"parts_st{i}") for i in range(2)]
        qk_ld = [sem(f"qk_ld{i}") for i in range(2)]
        qk_first = sem("qk_first")
        maxrow_ld = [sem(f"maxrow_ld{i}") for i in range(2)]
        attn_done, attnT_done, resT_done, x2T_done, x3T_done = (
            sem(n) for n in ("attn_done", "attnT_done", "resT_done", "x2T_done", "x3T_done"))
        sum_done = [sem(f"sum_done{k}") for k in range(4)]
        stat_done = [sem(f"stat_done{k}") for k in range(4)]
        rstd_done = [sem(f"rstd_done{k}") for k in range(4)]
        res_done = [sem(f"res_done{k}") for k in range(4)]
        expneg_done, cparts_done, cT_done = (sem(n) for n in ("expneg_done", "cparts_done", "cT_done"))
        tanh_done, gated_done, prod_done, hid_done, down_done = (
            sem(n) for n in ("tanh_done", "gated_done", "prod_done", "hid_done", "down_done"))
        dve_chain, pool_chain = (sem(n) for n in ("dve_chain", "pool_chain"))
        wr_done, row_done, kb_done, ks_ld, expq_done, qf_done, expk_done, kf_done, vk_done, kvb_done = (
            sem(n) for n in ("wr_done", "row_done", "kb_done", "ks_ld", "expq_done", "qf_done", "expk_done",
                             "kf_done", "vk_done", "kvb_done"))
        sums_done = [sem(f"sums_done{i}") for i in range(2)]
        floor_done, lh_done, lsub_done, lexp_done, gh_done, ghT_done, stored = (
            sem(n) for n in ("floor_done", "lh_done", "lsub_done", "lexp_done", "gh_done", "ghT_done", "stored"))
        bias_done = [sem(f"bias_done{k}") for k in range(4)]

        MISC = 7
        HALVES = GROUPS * NT * 2
        PAIRS = EP + 1
        last = NB - 1
        ropes = [("rope", b, m) for b in range(2) for m in range(4)]
        slots = [[] for _ in range(HALVES)]
        for b in range(NB):
            w = 32 * b
            for g in range(4):
                if 4 * b + g + 1 < GROUPS:
                    slots[max(0, w + 8 * g - 2)].append(("max", 4 * b + g + 1, 0))
            if b + 1 < NB:
                slots[max(1, w - 1)].append(("stacks", b + 1, 0))
                slots[w + 13].append(("val", b + 1, 0))
            if b + 2 < NB:
                for m, at in enumerate((7, 8, 16, 17)):
                    slots[w + at].append(("rope", b + 2, m))
                slots[w + 15].append(("split", b + 2, 0))
                slots[w + 23].append(("split", b + 2, 1))
            if b:
                for i, at in enumerate((1, 3, 5, 9)):
                    slots[w + at].append(("heads", b - 1, i))
                for kind, at in (("attnT", 12), ("proj", 15), ("norm", 24), ("resT", 26)):
                    slots[w + at].append((kind, b - 1, 0))
        for at, kind, b in ((1, "gate", 0), (16, "combine", 0), (17, "gate", 1), (31, "combine", 1)):
            slots[32 * last + at].append((kind, b, 0))
        beside = [[] for _ in range(NB * PAIRS + 12)]
        for at, kind, b, i in ((0, "gate", 2, 0), (0, "heads", 3, 0), (1, "heads", 3, 1), (2, "heads", 3, 2), (3, "heads", 3, 3),
                               (4, "attnT", 3, 0), (5, "wR", 0, 0), (5, "proj", 3, 0), (6, "wR", 0, 1), (7, "kb", 0, 0),
                               (7, "norm", 3, 0), (8, "combine", 2, 0), (8, "kb", 0, 1), (9, "resT", 3, 0),
                               (13, "gate", 3, 0), (20, "combine", 3, 0)):
            beside[at].append((kind, b, i))
        a_round = (("K", 0, 0), ("AT", 1, 0), ("K", 0, 1), ("Y1", 1, 0), ("K", 0, 2), ("ghT", 2, 0), ("K", 0, 3),
                   ("V", 0, 0), ("norm2", 1, 0), ("Y2", 2, 0), ("Q", 0, 0), ("Q", 0, 1), ("x3T", 1, 0), ("Q", 0, 2),
                   ("norm3", 2, 0), ("lg", 1, 0), ("Q", 0, 3), ("KV", 0, 0), ("O", 0, 1), ("O", 0, 0), ("OT", 0, 1),
                   ("OT", 0, 0))
        round_at = (4, 4, 5, 5, 5, 6, 6, 7, 7, 7, 8, 8, 9, 9, 9, 10, 10, 11, 12, 12, 12, 12)
        for n in range(NB):
            w = PAIRS * (n + 1)
            for at, kind in ((0, "chunk"), (1, "norm1"), (3, "x2T")):
                beside[w + at].append((kind, n, 0))
            if n + 1 < NB:
                for (kind, back, c), at in zip(a_round, round_at):
                    if n >= back:
                        beside[w + at].append((kind, n - back, c))
        layer2 = [s for one in beside[NB * PAIRS:] for s in one]
        del beside[NB * PAIRS:]
        crowded = {s for one in beside for s in one} | set(layer2)
        for n in range(last, NB + 2):
            layer2 += [(kind, n - back, c) for kind, back, c in a_round if 0 <= n - back < NB]

        uses = [[] for _ in range(8)]
        in_misc = ("rope", "val", "max", "heads", "attnT", "proj", "resT", "gate", "combine", "wR", "kb", "x2T")
        uses[MISC] = [s for one in [[("val", 0, 0), ("max", 0, 0)]] + slots for s in one if s[0] in in_misc]
        for s in ropes:
            uses[s[2]].append(s)
        for i in range(NB * PAIRS):
            uses[i % 2].append(("gate_e", i, 0))
            uses[2 + i % 2].append(("up_e", i, 0))
            if i % PAIRS < EP:
                uses[4].append(("comb_e", i, 0))
        for b in range(NB):
            uses[5].append(("y_e", b, 0))
        bank_for = {"K": 2, "Q": 0, "V": 4, "KV": 5, "O": 5, "OT": 5, "AT": 7, "Y1": 4, "x3T": 7, "lg": 5, "ghT": 7, "Y2": 6, "x2T": 7}
        swap = 0
        for one in beside + [layer2]:
            for kind, b, c in one:
                if kind in in_misc:
                    bank = MISC
                elif kind not in bank_for:
                    continue
                elif (kind, b, c) in crowded:
                    swap = 0 if kind == "lg" else 1 - swap
                    bank = 6 + swap
                else:
                    bank = bank_for[kind] + (c % 2 if kind in ("K", "Q", "O", "OT") else 0)
                uses[bank].append((kind, b, c))
                if kind == "lg":
                    uses[7].append(("lh", b, 0))
        turn = {u: (bank, n) for bank in range(8) for n, u in enumerate(uses[bank])}

        def read_out(u):
            kind, b, c = u
            if kind == "up_e":
                n, p = divmod(b, PAIRS)
                return (hid_done, b + 1) if p == EP else (prod_done, n * EP + p + 1)
            return {"rope": (rot_done, 4 * (b - 1) + c + 1) if b else (rot0_done, c + 1), "val": (v_done, b + 1),
                    "max": (maxT_done, b + 1),
                    "heads": (attn_done, NT * b + c + 1), "attnT": (attnT_done, b + 1), "proj": (sum_done[0], b + 1),
                    "resT": (resT_done, b + 1), "gate": (expneg_done, b + 1), "combine": (cT_done, b + 1),
                    "gate_e": (gated_done, b + 1), "comb_e": (hid_done, b + 1), "y_e": (sum_done[1], b + 1),
                    "x2T": (x2T_done, b + 1), "wR": (wr_done, c + 1),
                    "kb": (row_done, c + 1), "Q": (qf_done, 4 * b + c + 1), "K": (kf_done, 4 * b + c + 1),
                    "V": (vk_done, b + 1), "KV": (kvb_done, b + 1), "O": (sums_done[c % 2], b + 1),
                    "OT": (floor_done, b + 1) if c else (attn_done, NB * NT + b + 1),
                    "AT": (attnT_done, NB + b + 1), "Y1": (sum_done[2], b + 1), "x3T": (x3T_done, b + 1),
                    "lg": (lsub_done, b + 1), "lh": (lh_done, b + 1), "ghT": (ghT_done, b + 1),
                    "Y2": (sum_done[3], b + 1)}[kind]

        def sm_bank(u):
            return ps[(4, 5, 0, 1, 2, 3)[u % 6] if u < HG * NT else 4 + u % 2]

        def bank_of(u):
            return ps[turn[u][0]]

        def wait_free(eng, u):
            bank, n = turn[u]
            if n:
                eng.wait_ge(*read_out(uses[bank][n - 1]))

        def wait_full(eng, u):
            bank, n = turn[u]
            eng.wait_ge(ps_full[bank], n + 1 - sum(v[0] == "y_e" for v in uses[bank][:n]))

        def fullness(u):
            return ps_full[turn[u][0]]

        def wide(stack, first, end):
            return stack[first:end, :, :].rearrange("p h t -> p (h t)").bitcast(F32)

        block = ctx.enter_context(nc.Block())

        @block.sync
        def _(sp):
            sp.dma_start(xT[:, 0:T], xT_in[:, 0:T]).then_inc(rope_ld, 16)
            for a, z_, done in (("w_kq", "w_kq", rope_ld), ("b_rope", "sin", table_ld), ("w_v", "bv_row", early_ld)):
                cols = slice(EARLY_AT[a][0], EARLY_AT[z_][1])
                sp.dma_start(early[:, cols], early_in[:, cols]).then_inc(done, 16)
            sp.dma_start(xT[:, T:2 * T], xT_in[:, T:2 * T]).then_inc(x_ld, 16)

            def store_parts(b):
                for i in range(2):
                    sp.wait_ge(split_done[i], 3 * (b + 1))
                    sp.dma_start(parts_dram[b, i].rearrange("p r t -> r p t"), parts[:, i, :, :]).then_inc(parts_st[i], 16)

            def load_stacks(b, h0, h1, done):
                for i in range(2):
                    sp.wait_ge(parts_st[i], 16 * (b + 1))
                    dst = (KS, QS)[i][b % 2][:, h0:h1, :].rearrange("r h t -> r (h t)")
                    src = parts_dram[b, i].rearrange("p (d h) t -> p d h t", h=H)[:, :, h0:h1, :]\
                        .rearrange("p d h t -> p d (h t)")
                    n = (h1 - h0) * T
                    if i == 0:
                        sp.dma_start(dst[0:9 * DH, :], src.rearrange("p d n -> (p d) n").unsqueeze(0)
                                     .to_broadcast([3, 3 * DH, n])).then_inc(done, 16)
                    else:
                        for p in range(3):
                            sp.dma_start(dst[p * 3 * DH:(p + 1) * 3 * DH, :], src[p].unsqueeze(0)
                                         .to_broadcast([3, DH, n])).then_inc(done, 16)

            def load_max(G):
                sp.wait_ge(maxp_done, G + 1)
                if G >= 2:
                    sp.wait_ge(maxrow_ld[G % 2], 48 * (G // 2))
                g = G % NG
                for i in range(3):
                    dst = QS[(G // NG) % 2][KROW + i:KROW + i + 1, HG * g:HG * (g + 1), :]
                    sp.dma_start(dst.rearrange("i h (q t) -> i (h q) t", q=NT), maxp[:, G % 2, i, :])\
                        .then_inc(maxrow_ld[G % 2], 16)

            store_parts(0)
            sp.wait_ge(init_dve, 2)
            sp.wait_ge(init_pool, 1)
            load_stacks(0, 0, HG, qk_first)
            load_stacks(0, HG, H, qk_ld[0])
            sp.dma_start(xT[:, 2 * T:], xT_in[:, 2 * T:]).then_inc(x_ld, 16)
            load_max(0)
            store_parts(1)
            sp.dma_start(res[:, :, :], x_in.rearrange("(n p) d -> p n d", p=P)).then_inc(res_ld, 16)
            for w in range(HALVES):
                for kind, a, m in slots[w]:
                    if kind == "max":
                        load_max(a)
                    if kind == "split" and m == 1:
                        store_parts(a)
                    if kind == "stacks":
                        if a >= 2:
                            sp.wait_ge(s_full, 32 * (a - 1))
                        else:
                            sp.wait_ge(init_pool, 2)
                        load_stacks(a, 0, H, qk_ld[a % 2])
                if w == 7:
                    sp.dma_start(late[:, :], late_in).then_inc(late_ld, 16)
                    sp.dma_start(sel[:, :, :], sel_in).then_inc(late_ld, 16)
                    sp.dma_start(identb[:, :], identb_in).then_inc(late_ld, 16)
            sp.wait_ge(kb_done, 2)
            for i in range(3):
                sp.dma_start(bias_stack[i:i + 1, :, :], bias_parts[0:1, :, i, :]).then_inc(ks_ld, 16)
            for b in range(NB):
                sp.wait_ge(res_done[3], b + 1)
                sp.dma_start(out[b * T:(b + 1) * T, :].rearrange("(n p) d -> p n d", p=P),
                             outb[:, b * NT:(b + 1) * NT, :]).then_inc(stored, 16)
            sp.wait_ge(stored, 16 * NB)

        @block.gpsimd
        def _(pool):
            n = [0]

            def link(ins):
                n[0] += 1
                ins.then_inc(pool_chain, 1)
                pool.wait_ge(pool_chain, n[0])

            def tt(o, a, b, op):
                return nc.gpsimd.tensor_tensor(out=o, in0=a, in1=b, op=op)

            def rope_split(b, i):
                v = rot[:, 2 * i, :]
                pool.wait_ge(rot_done, 4 * (b - 1) + 2 * i + 2)
                pool.wait_ge(parts_st[i], 16 * b)
                link(tt(v, v, c_["cos"], ALU.mult))
                link(tt(rot[:, 2 * i + 1, :], rot[:, 2 * i + 1, :], c_["sin"], ALU.mult))
                link(tt(v, v, rot[:, 2 * i + 1, :], ALU.add))
                nc.gpsimd.tensor_scalar(parts[:, i, 0, :], v, 1.0, None, ALU.mult).then_inc(split_done[i], 1)

            def rest_split(b, i):
                v = rot[:, 2 * i, :]
                pool.wait_ge(split_done[i], 3 * b + 1)
                link(tt(v, v, parts[:, i, 0, :], ALU.subtract))
                nc.gpsimd.tensor_scalar(parts[:, i, 1, :], v, 1.0, None, ALU.mult).then_inc(split_done[i], 1)
                pool.wait_ge(split_done[i], 3 * b + 2)
                tt(parts[:, i, 2, :], v, parts[:, i, 1, :], ALU.subtract).then_inc(split_done[i], 1)

            def deviation(k, b):
                pool.wait_ge(stat_done[k], b + 1)
                link(nc.gpsimd.tensor_scalar(var[:, b, :], mv[:, b, :, 1], LN_EPS, None, ALU.add))
                tt(rstd[:, b, :], var[:, b, :], minus_half[:, :], ALU.pow).then_inc(rstd_done[k], 1)

            def add_row(name, k, b):
                v = res[:, b * NT:(b + 1) * NT, :]
                tt(v, v, c_[name].unsqueeze(1).to_broadcast([P, NT, D]), ALU.add).then_inc(bias_done[k], 1)

            def beside_pool(kind, a, m):
                if kind == "rope" and m % 2 == 1 and a:
                    rope_split(a, m // 2)
                if kind == "split":
                    rest_split(a, m)
                if kind == "norm":
                    deviation(0, a)
                if kind == "norm1":
                    deviation(1, a)
                if kind == "norm2":
                    deviation(2, a)
                if kind == "norm3":
                    deviation(3, a)
                if kind == "x2T":
                    pool.wait_ge(x2T_done, a + 1)
                    add_row("bo1_row", 2, a)
                if kind == "x3T":
                    pool.wait_ge(x3T_done, a + 1)
                    add_row("lb_row", 3, a)

            link(nc.gpsimd.memset(minus_half[:, :], -0.5))
            nc.gpsimd.memset(wide(KS[0], 64, KROW), 0.0).then_inc(init_pool, 1)
            pool.wait_ge(init_pool, 1)
            link(nc.gpsimd.memset(wide(QS[1], 64, KROW), 0.0))
            link(nc.gpsimd.memset(wide(KS[1], 64, KROW), 0.0))
            nc.gpsimd.memset(wide(KS[1], KROW, P), TWO_ONES).then_inc(init_pool, 1)
            pool.wait_ge(init_pool, 2)
            pool.wait_ge(table_ld, 16)
            beside_pool("rope", 1, 1)
            beside_pool("split", 1, 0)
            for i in range(2):
                link(nc.gpsimd.memset(VA[i][:, :, :, DH + 1:], 0.0))
                nc.gpsimd.memset(VA[i][:, :, :, DH:DH + 1], 1.0).then_inc(init_pool, 1)
                pool.wait_ge(init_pool, i + 3)
            beside_pool("rope", 1, 3)
            beside_pool("split", 1, 1)
            link(nc.gpsimd.memset(onesb[:, :], 1.0))
            nc.gpsimd.memset(VK[:, :, :, :], 1.0).then_inc(init_pool, 1)
            pool.wait_ge(init_pool, 5)
            for w in range(HALVES):
                for s in slots[w]:
                    beside_pool(*s)
                if w == 7:
                    pool.wait_ge(res_ld, 16)
                    pool.wait_ge(late_ld, 48)
                if w % 32 == 7:
                    add_row("bout_row", 0, w // 32)
            for one in beside + [layer2]:
                for s in one:
                    beside_pool(*s)

        @block.tensor
        def _(pe):
            mm = nc.tensor.matmul
            tr = nc.tensor.transpose

            def scores_for_max(u):
                G, i = divmod(u, HG * NT)
                b, h, qt = G // NG, HG * (G % NG) + i // NT, i % NT
                if i == 0 and G == 0:
                    pe.wait_ge(qk_first, 64)
                if i == 0 and (G == 1 or G and G % NG == 0):
                    pe.wait_ge(qk_ld[b % 2], 64 * (b // 2 + 1))
                if G == 0 and u >= 6:
                    pe.wait_ge(sm_free, u - 5)
                if G:
                    pe.wait_ge(sm_free, u - 3 if u < HG * NT + 2 else u - 1)
                mm(sm_bank(u)[:, :], QS[b % 2][0:KROW, h, qt * P:(qt + 1) * P], KS[b % 2][0:KROW, h, :],
                   start=True, stop=True).then_inc(sm_full, 1)

            def scores(w):
                n, hf = divmod(w, 2)
                G, kt = divmod(n, NT)
                b = G // NG
                if w == 0:
                    pe.wait_ge(init_dve, 3)
                    pe.wait_ge(sm_free, HG * NT)
                if kt == 0 and hf == 0:
                    pe.wait_ge(maxrow_ld[G % 2], 48 * (G // 2 + 1))
                if w >= 2:
                    pe.wait_ge(exp_done, w - 1)
                for j in range(2):
                    h = HG * (G % NG) + 2 * hf + j
                    last_ = mm(ps[2 * hf + j][:, :], KS[b % 2][0:KROW + 3, h, kt * P:(kt + 1) * P],
                               QS[b % 2][0:KROW + 3, h, :], start=True, stop=True)
                last_.then_inc(s_full, 1)

            def values(n, half):
                G, kt = divmod(n, NT)
                b = G // NG
                q = slice(half * T // 2, (half + 1) * T // 2)
                if half == 0:
                    pe.wait_ge(exp_done, 2 * n + 2)
                    if n % (NG * NT) == 0:
                        pe.wait_ge(v_done, b + 1)
                        pe.wait_ge(init_pool, 4)
                    if kt == 0 and G:
                        pe.wait_ge(o_evac, G)
                for j in range(HG):
                    h = HG * (G % NG) + j
                    last_ = mm(ps[6][32 * j:32 * j + 32, q], VA[b % 2][:, kt, h, :], probs[:, n % 2, j, q],
                               start=(kt == 0 and half == 0), stop=(kt == NT - 1), tile_position=(0, 32 * j),
                               skip_group_check=True)
                if half:
                    last_.then_inc(pv_done, 1)

            def base_layer(b):
                for t in range(NT):
                    n = b * T + t * P
                    mm(bank_of(("Y2", b, 0))[:, t * P:(t + 1) * P], xT[:, n:n + P], c_["lw"], start=(t == 0), stop=False,
                       skip_group_check=True)

            def beside_pe(kind, b, m):
                if kind in ("norm", "norm1", "norm2", "norm3", "chunk", "stacks", "split"):
                    return
                u = (kind, b, m)
                o = bank_of(u)

                def tile_of(t):
                    return xT[:, b * T + t * P:b * T + (t + 1) * P]

                def cols(t, n_=P):
                    return o[:, t * n_:(t + 1) * n_]

                if kind == "heads" and m == 0:
                    pe.wait_ge(o_evac, NG * (b + 1))
                if kind == "attnT":
                    pe.wait_ge(attn_done, NT * (b + 1))
                if kind == "AT":
                    pe.wait_ge(attn_done, NB * NT + b + 1)
                if kind == "proj":
                    pe.wait_ge(attnT_done, b + 1)
                    if b == 0:
                        pe.wait_ge(late_ld, 48)
                if kind == "Y1":
                    pe.wait_ge(attnT_done, NB + b + 1)
                if kind in ("resT", "x2T", "x3T"):
                    pe.wait_ge(res_done[("resT", "x2T", "x3T").index(kind)], b + 1)
                if kind == "gate":
                    pe.wait_ge(resT_done, b + 1)
                if kind == "combine":
                    pe.wait_ge(cparts_done, b + 1)
                if kind == "K" and m == 0:
                    pe.wait_ge(x2T_done, b + 1)
                    pe.wait_ge(wr_done, 2)
                    pe.wait_ge(ks_ld, 48)
                if kind == "KV":
                    pe.wait_ge(kf_done, 4 * (b + 1))
                    pe.wait_ge(vk_done, b + 1)
                if kind == "OT":
                    pe.wait_ge(sums_done[m], b + 1)
                if kind == "O" and m == 1:
                    pe.wait_ge(kvb_done, b + 1)
                    pe.wait_ge(qf_done, 4 * (b + 1))
                if kind == "lg":
                    pe.wait_ge(x3T_done, b + 1)
                if kind == "ghT":
                    pe.wait_ge(gh_done, b + 1)
                if kind == "Y2":
                    pe.wait_ge(ghT_done, b + 1)
                wait_free(pe, u)

                if kind == "rope":
                    if b and m == 0:
                        pe.wait_ge(x_ld, 16 * min(b, 2))
                    last_ = mm(o[:, :], c_["w_kq"][:, m * D:(m + 1) * D], xT[:, b * T:(b + 1) * T], start=True, stop=True)
                if kind == "val":
                    if b == 2:
                        pe.wait_ge(x_ld, 32)
                    for t in range(NT):
                        last_ = mm(cols(t), tile_of(t), c_["w_v"], start=True, stop=True)
                if kind == "max":
                    pe.wait_ge(sm_free, HG * NT * (b + 1))
                    last_ = mm(o[0:HG * NT, 0:P], negmax[:, b % 4, :], ident, start=True, stop=True)
                if kind == "heads":
                    for g in range(NG):
                        last_ = tr(cols(g), OU[:, b % 2, g, m * P:(m + 1) * P], ident)
                if kind in ("attnT", "AT"):
                    for t in range(NT):
                        last_ = tr(cols(t), attn[:, b % 2, t, :], ident)
                if kind in ("proj", "Y1"):
                    for t in range(NT):
                        last_ = mm(cols(t), attnT[:, t * P:(t + 1) * P], c_["w_out" if kind == "proj" else "wo1"],
                                   start=True, stop=True)
                if kind in ("resT", "x2T", "x3T"):
                    for t in range(NT):
                        last_ = tr(cols(t), res[:, b * NT + t, :], ident)
                if kind == "gate":
                    for t in range(NT):
                        last_ = mm(cols(t, E0), tile_of(t), c_["wg"], start=True, stop=True)
                if kind == "combine":
                    for t in range(NT):
                        last_ = mm(o[0:3 * E0, t * P:(t + 1) * P], cparts[:, t, :], identb[:, :], start=True, stop=True)
                if kind == "wR":
                    last_ = mm(o[:, :], c_[("wqT", "wkT")[m]], c_["rbd"], start=True, stop=True)
                if kind == "kb":
                    last_ = mm(o[:, :], c_[("bk_rep", "bq_rep")[m]], c_["rbd"], start=True, stop=True)
                if kind == "K":
                    mm(o[:, :], tile_of(m), wkR[:, :], start=True, stop=False)
                    last_ = mm(o[:, :], onesb[:, 0:P], bias_stack[:, 0, :], start=False, stop=True)
                if kind == "V":
                    for t in range(NT):
                        last_ = mm(cols(t), tile_of(t), c_["wv1"], start=True, stop=True)
                if kind == "Q":
                    mm(o[:, :], wqR[:, m * P:(m + 1) * P], xT[:, b * T:(b + 1) * T], start=True, stop=False)
                    last_ = mm(o[:, :], bias_stack[:, 1, m * P:(m + 1) * P], onesb[:, :], start=False, stop=True)
                if kind == "KV":
                    for c in range(4):
                        for t in range(NT):
                            last_ = mm(cols(c, KVW), KF[:, t, c * P:(c + 1) * P], VK[:, t, c, :],
                                       start=(t == 0), stop=(t == NT - 1))
                if kind == "O":
                    for c in range(NG):
                        last_ = mm(o[HW * c:HW * (c + 1), :], KVB[:, m, c, :], QF[:, b % 2, c, :],
                                   start=True, stop=True, tile_position=(0, HW * c))
                if kind == "OT":
                    for t in range(NT):
                        v = OU[:, 0, m, t * P:(t + 1) * P]
                        if m:
                            last_ = mm(cols(t, H), v, ident[:, 0:P:DH], start=True, stop=True)
                        else:
                            last_ = tr(cols(t), v, ident)
                if kind == "lg":
                    for t in range(NT):
                        last_ = mm(cols(t, E1), tile_of(t), c_["lr"], start=True, stop=True)
                    last_.then_inc(fullness(u), 1)
                    u = ("lh", b, 0)
                    wait_free(pe, u)
                    for t in range(NT):
                        last_ = mm(bank_of(u)[:, t * P:(t + 1) * P], tile_of(t), c_["la"], start=True, stop=True)
                    if b == last:
                        last_.then_inc(fullness(u), 1)
                        wait_free(pe, ("Y2", b, 0))
                        base_layer(b)
                        return
                if kind == "ghT":
                    for t in range(NT):
                        last_ = tr(cols(t), gh[:, t, :], ident)
                if kind == "Y2":
                    if b != last:
                        base_layer(b)
                    for t in range(NT):
                        last_ = mm(cols(t), ghT[:, t * P:(t + 1) * P], c_["lb"], start=False, stop=True,
                                   skip_group_check=True)
                last_.then_inc(fullness(u), 1)

            pe.wait_ge(rope_ld, 32)
            for s in ropes[:4]:
                beside_pe(*s)
            pe.wait_ge(early_ld, 16)
            beside_pe("val", 0, 0)
            for s in ropes[4:]:
                beside_pe(*s)
            pe.wait_ge(rot_done, 4)
            for u in range(HG * NT + 1):
                scores_for_max(u)
            beside_pe("max", 0, 0)
            for u in range(HG * NT + 1, AHEAD):
                scores_for_max(u)
                if u in (AHEAD - 10, AHEAD - 9, AHEAD - 6):
                    scores((AHEAD - 10, AHEAD - 9, AHEAD - 6).index(u))
            for n in range(HALVES // 2):
                def ahead(i):
                    u = AHEAD + 4 * n + i
                    if u < GROUPS * HG * NT:
                        scores_for_max(u)

                if 2 * n + 3 < HALVES:
                    scores(2 * n + 3)
                ahead(0)
                values(n, 0)
                ahead(1)
                for s in slots[2 * n]:
                    beside_pe(*s)
                values(n, 1)
                ahead(2)
                if 2 * n + 4 < HALVES:
                    scores(2 * n + 4)
                ahead(3)
                for s in slots[2 * n + 1]:
                    beside_pe(*s)

            def down(i):
                b, p = divmod(i, PAIRS)
                pe.wait_ge(hid_done, i + 1)
                u = ("y_e", b, 0)
                if p == 0:
                    wait_free(pe, u)
                w2 = c_["w2s"] if p == EP else c_["w2"][:, p * D:(p + 1) * D]
                for t in range(NT):
                    last_ = mm(bank_of(u)[:, t * D:(t + 1) * D], hid[:, i % 3, t * P:(t + 1) * P], w2,
                               start=(p == 0 and t == 0), stop=(p == EP and t == NT - 1), skip_group_check=True)
                last_.then_inc(down_done, 1)

            pe.wait_ge(exp_done, HALVES)
            pe.wait_ge(sm_free, GROUPS * HG * NT)
            for i in range(NB * PAIRS):
                b, p = divmod(i, PAIRS)
                for kind, w, ws in (("gate_e", "w1", "w1s"), ("up_e", "w3", "w3s")):
                    u = (kind, i, 0)
                    wait_free(pe, u)
                    wt = c_[ws] if p == EP else c_[w][:, p * 2 * F0:(p + 1) * 2 * F0]
                    mm(bank_of(u)[:, :], wt, xT[:, b * T:(b + 1) * T], start=True, stop=True).then_inc(fullness(u), 1)
                if p < EP:
                    u = ("comb_e", i, 0)
                    wait_free(pe, u)
                    if p == 0:
                        pe.wait_ge(cT_done, b + 1)
                    mm(bank_of(u)[:, :], sel[:, p, :], cT[:, b, :], start=True, stop=True).then_inc(fullness(u), 1)
                for s in beside[i][:1]:
                    beside_pe(*s)
                if i:
                    down(i - 1)
                for s in beside[i][1:]:
                    beside_pe(*s)
            down(NB * PAIRS - 1)
            for s in layer2:
                beside_pe(*s)

        @block.scalar
        def _(act):
            fn = nc.scalar.activation

            def exps(w):
                n, hf = divmod(w, 2)
                act.wait_ge(s_full, w + 1)
                if n >= 2:
                    act.wait_ge(pv_done, n - 1)
                fn(probs[:, n % 2, 2 * hf:2 * hf + 2, :], psum[:, 2 * hf:2 * hf + 2, :], ACT.Exp,
                   scale=float(DH) ** -0.5).then_inc(exp_done, 1)

            def outputs(G):
                b = G // NG
                act.wait_ge(pv_done, NT * (G + 1))
                if b >= 2 and G % NG == 0:
                    wait_full(act, ("heads", b - 2, 3))
                fn(OU[:, b % 2, G % NG, :], ps[6][:, :], ACT.Copy).then_inc(o_evac, 1)

            def beside_act(kind, a, m):
                u = (kind, a, m)
                if kind == "rope" and a:
                    wait_full(act, u)
                    act.wait_ge(split_done[m // 2], 3 * a)
                    fn(rot[:, m, :], bank_of(u)[:, :], ACT.Identity, bias=c_["b_rope"][:, m:m + 1]).then_inc(rot_done, 1)
                if kind == "O":
                    wait_full(act, u)
                    if a:
                        wait_full(act, ("OT", a - 1, m))
                    fn(OU[:, 0, m, :], bank_of(u)[:, :], ACT.Copy).then_inc(sums_done[m], 1)
                if kind in ("attnT", "AT"):
                    wait_full(act, u)
                    if kind == "AT" and a:
                        wait_full(act, ("Y1", a - 1, 0))
                    if kind == "AT" and not a:
                        wait_full(act, ("proj", last, 0))
                    if kind == "attnT" and a:
                        wait_full(act, ("proj", a - 1, 0))
                    fn(attnT[:, :], bank_of(u)[:, :], ACT.Copy).then_inc(attnT_done, 1)
                if kind in ("resT", "x2T", "x3T"):
                    wait_full(act, u)
                    if kind == "x2T":
                        act.wait_ge(down_done, (a + 1) * PAIRS)
                    fn(xT[:, a * T:(a + 1) * T], bank_of(u)[:, :], ACT.Copy)\
                        .then_inc({"resT": resT_done, "x2T": x2T_done, "x3T": x3T_done}[kind], 1)
                if kind == "gate":
                    wait_full(act, u)
                    if a:
                        act.wait_ge(cparts_done, a)
                    fn(rt[:, 0, :], bank_of(u)[:, 0:NT * E0], ACT.Exp, scale=-1.0).then_inc(expneg_done, 1)
                if kind == "combine":
                    wait_full(act, u)
                    fn(cT[:, a, :], bank_of(u)[0:3 * E0, :], ACT.Copy).then_inc(cT_done, 1)
                if kind == "wR":
                    wait_full(act, u)
                    fn((wqR, wkR)[m][:, :], bank_of(u)[:, :], ACT.Copy).then_inc(wr_done, 1)
                if kind == "K":
                    i = 4 * a + m
                    wait_full(act, u)
                    if i >= 2:
                        act.wait_ge(kf_done, i - 1)
                    fn(ek_[:, i % 2, :], bank_of(u)[:, :], ACT.Exp, bias=minus1[:, 0:1]).then_inc(expk_done, 1)
                if kind == "Q":
                    i = 4 * a + m
                    wait_full(act, u)
                    if i >= 2:
                        act.wait_ge(qf_done, i - 1)
                    fn(eq_[:, i % 2, :], bank_of(u)[:, :], ACT.Exp, bias=minus1[:, 0:1]).then_inc(expq_done, 1)
                if kind == "lg":
                    act.wait_ge(lsub_done, a + 1)
                    fn(rl[:, 1, :], rl[:, 0, :], ACT.Exp).then_inc(lexp_done, 1)
                    wait_full(act, ("lh", a, 0))
                    if a:
                        wait_full(act, ("ghT", a - 1, 0))
                    fn(gh.rearrange("p n d -> p (n d)"), bank_of(("lh", a, 0))[:, :], ACT.Copy).then_inc(lh_done, 1)
                if kind == "ghT":
                    wait_full(act, u)
                    if a:
                        wait_full(act, ("Y2", a - 1, 0))
                    fn(ghT[:, :], bank_of(u)[:, :], ACT.Copy).then_inc(ghT_done, 1)

            act.wait_ge(init_dve, 1)
            fn(rt[:, 23, 0:1], minus1[:, 0:1], ACT.Exp)
            for s in ropes[4:]:
                beside_act(*s)
            for w in range(3):
                exps(w)
            for n in range(HALVES // 2):
                if 2 * n + 3 < HALVES:
                    exps(2 * n + 3)
                if n % NT == NT - 1:
                    outputs(n // NT)
                for s in slots[2 * n]:
                    beside_act(*s)
                if 2 * n + 4 < HALVES:
                    exps(2 * n + 4)
                for s in slots[2 * n + 1]:
                    beside_act(*s)
            for i in range(NB * PAIRS):
                u = ("gate_e", i, 0)
                wait_full(act, u)
                if i >= 2:
                    act.wait_ge(hid_done, i - 1)
                fn(gate_s[:, i % 2, :], bank_of(u)[:, :], ACT.Tanh, scale=0.5).then_inc(tanh_done, 1)
                for s in beside[i]:
                    beside_act(*s)
            for s in layer2:
                beside_act(*s)

        @block.vector
        def _(dve):
            V = nc.vector
            n = [0]

            def link(ins):
                n[0] += 1
                ins.then_inc(dve_chain, 1)
                dve.wait_ge(dve_chain, n[0])

            def after(ins):
                n[0] += 1
                at = n[0]
                ins.then_inc(dve_chain, 1)
                yield
                dve.wait_ge(dve_chain, at)

            urgent, routing = [], []

            def step(count):
                for _ in range(count):
                    while urgent or routing:
                        chain = urgent or routing
                        if next(chain[0], "end") != "end":
                            break
                        chain.pop(0)

            def finish(everything=False):
                while urgent or everything and routing:
                    step(1)

            def tt(o, a, b, op):
                return V.tensor_tensor(out=o, in0=a, in1=b, op=op)

            def r3(k, e, tile=rt):
                return tile[:, k, 0:NT * e].rearrange("p (t e) -> p t e", e=e)

            def z_of(k, b):
                return z[:, 2 if k == 1 else b % 2, :, :]

            def add_residual(k, b, y):
                dve.wait_ge(*((res_done[0] if k == 1 else bias_done[k]), b + 1))
                if k == 0 and b >= 2:
                    dve.wait_ge(res_done[0], b - 1)
                if k == 1 and b:
                    dve.wait_ge(res_done[1], b)
                if k == 2:
                    dve.wait_ge(*((res_done[3], b - 1) if b >= 2 else (res_done[0], b + 3)))
                if k == 3:
                    dve.wait_ge(res_done[2], b + 1)
                tt(z_of(k, b), y.rearrange("p (t d) -> p t d", d=D), res[:, b * NT:(b + 1) * NT, :], ALU.add)\
                    .then_inc(sum_done[k], 1)

            stats_used = []

            def statistics(k, b):
                dve.wait_ge(sum_done[k], b + 1)
                if stats_used:
                    dve.wait_ge(*stats_used[-1])
                stats_used.append((stat_done[k], b + 1))
                for t in range(NT):
                    ins = V.bn_stats(stats[:, t, :], z_of(k, b)[:, t, :])
                    if t < NT - 1:
                        yield
                yield from after(ins)
                for t in range(NT):
                    ins = V.bn_aggr(mv[:, b, t, :], stats[:, t, :])
                ins.then_inc(stat_done[k], 1)
                yield

            def normalise(k, b):
                dve.wait_ge(rstd_done[k], b + 1)
                target = outb if k == 3 else res
                for t in range(NT):
                    ins = V.tensor_scalar(target[:, b * NT + t, :], z_of(k, b)[:, t, :], mv[:, b, t, 0:1],
                                          rstd[:, b, t:t + 1], ALU.subtract, ALU.mult)
                    if t == NT - 1:
                        ins.then_inc(res_done[k], 1)
                    yield

            def top(tile, vals, m8, k, e, at, reset):
                thr = m8[:, :, k - 1:k].to_broadcast([P, NT, e])
                gt, eq, inc, le = (r3(at + i, e, tile) for i in range(4))
                cnt = tile[:, at + 4, 0:NT]
                tt(eq, vals, thr, ALU.is_equal)
                yield from after(tt(gt, vals, thr, ALU.is_gt))
                V.tensor_tensor_scan(tile[:, at + 2, 0:NT * e], c_[reset], tile[:, at + 1, 0:NT * e], 0.0, ALU.mult, ALU.add)
                yield from after(V.reduce_sum(cnt, gt, X))
                yield from after(V.tensor_scalar(cnt, cnt, -1.0, float(k), ALU.mult, ALU.add))
                yield from after(tt(le, inc, cnt.unsqueeze(2).to_broadcast([P, NT, e]), ALU.is_le))
                yield from after(tt(eq, eq, le, ALU.mult))
                yield from after(tt(gt, gt, eq, ALU.add))

            def route(a):
                dve.wait_ge(expneg_done, a + 1)
                s = r3(1, E0)
                yield from after(V.tensor_scalar(rt[:, 0, :], rt[:, 0, :], 1.0, None, ALU.add))
                yield from after(V.reciprocal(rt[:, 1, :], rt[:, 0, :]))
                sg = rt[:, 1, :].rearrange("p (g e) -> p g e", e=4)
                pr = rt[:, 2:4, :].rearrange("p a n -> p (a n)")[:, 0:96].rearrange("p (g e) -> p g e", e=6)
                tt(pr[:, :, 0:3], sg[:, :, 0:3], sg[:, :, 1:4], ALU.add)
                tt(pr[:, :, 3:5], sg[:, :, 0:2], sg[:, :, 2:4], ALU.add)
                gs = r3(4, 8)
                V.memset(gs[:, :, 4:8], -1.0)
                yield from after(tt(pr[:, :, 5:6], sg[:, :, 0:1], sg[:, :, 3:4], ALU.add))
                yield from after(V.tensor_reduce(out=gs[:, :, 0:4], in_=pr.rearrange("p (t g) e -> p t g e", g=4), axis=X,
                                                 op=ALU.max))
                m8 = r3(5, 8)
                for t in range(NT):
                    ins = V.max(m8[:, t, :], gs[:, t, :])
                yield from after(ins)
                yield from top(rt, gs, m8, 2, 8, 6, "reset8")
                allow = r3(6, 8)[:, :, 0:4]
                am1 = r3(11, 4)
                V.tensor_scalar(am1, allow, -1.0, None, ALU.add)
                mk = rt[:, 12, :].rearrange("p (t g e) -> p t g e", g=4, e=4)
                s44 = rt[:, 1, :].rearrange("p (t g e) -> p t g e", g=4, e=4)
                yield from after(tt(mk, s44, allow.unsqueeze(3).to_broadcast([P, NT, 4, 4]), ALU.mult))
                yield from after(tt(mk, mk, am1.unsqueeze(3).to_broadcast([P, NT, 4, 4]), ALU.add))
                masked = r3(12, E0)
                for t in range(NT):
                    ins = V.max(m8[:, t, :], masked[:, t, :])
                yield from after(ins)
                yield from top(rt, masked, m8, 4, E0, 13, "reset16")
                w = r3(18, E0)
                yield from after(tt(w, s, r3(13, E0), ALU.mult))
                tot = rt[:, 19, 0:NT]
                yield from after(V.reduce_sum(tot, w, X))
                yield from after(V.tensor_scalar(tot, tot, 1e-6, None, ALU.add))
                yield from after(V.reciprocal(tot, tot))
                yield from after(tt(w, w, tot.unsqueeze(2).to_broadcast([P, NT, E0]), ALU.mult))
                if a:
                    wait_full(dve, ("combine", a - 1, 0))
                yield from after(V.tensor_copy(cparts[:, :, 0:E0], w))
                yield from after(tt(w, w, cparts[:, :, 0:E0], ALU.subtract))
                yield from after(V.tensor_copy(cparts[:, :, E0:2 * E0], w))
                tt(cparts[:, :, 2 * E0:], w, cparts[:, :, E0:2 * E0], ALU.subtract).then_inc(cparts_done, 1)
                yield

            def lora_gates(b):
                dve.wait_ge(lexp_done, b + 1)
                e = r3(1, E1, rl)
                tot = rl[:, 3, 0:NT]
                yield from after(V.reduce_sum(tot, e, X))
                yield from after(V.reciprocal(tot, tot))
                yield from after(tt(gate8[:, :, :], e, tot.unsqueeze(2).to_broadcast([P, NT, E1]), ALU.mult))
                m8 = r3(5, 8, rl)
                for t in range(NT):
                    ins = V.max(m8[:, t, :], gate8[:, t, :])
                yield from after(ins)
                yield from top(rl, gate8[:, :, :], m8, 2, E1, 6, "reset8")
                yield from after(tt(gate8[:, :, :], gate8[:, :, :], r3(6, E1, rl), ALU.mult))
                yield from after(V.reduce_sum(tot, gate8[:, :, :], X))
                yield from after(V.tensor_scalar(tot, tot, 1e-6, None, ALU.add))
                yield from after(V.reciprocal(tot, tot))
                yield from after(tt(gate8[:, :, :], gate8[:, :, :], tot.unsqueeze(2).to_broadcast([P, NT, E1]), ALU.mult))
                dve.wait_ge(lh_done, b + 1)
                v = gh.rearrange("p n (e r) -> p n e r", r=R1)
                tt(v, v, gate8[:, :, :].unsqueeze(3).to_broadcast([P, NT, E1, R1]), ALU.mult).then_inc(gh_done, 1)
                yield

            def reduce_scores(u):
                G, i = divmod(u, HG * NT)
                dve.wait_ge(sm_full, u + 1)
                if i == 0 and G >= 4:
                    wait_full(dve, ("max", G - 4, 0))
                V.tensor_reduce(out=negmax[:, G % 4, i:i + 1], in_=sm_bank(u)[:, :], axis=X, op=ALU.max,
                                negate=True).then_inc(sm_free, 1)

            def split_max(G):
                u = ("max", G, 0)
                wait_full(dve, u)
                if G >= 2:
                    dve.wait_ge(maxrow_ld[G % 2], 48 * (G // 2))
                    dve.wait_ge(maxp_done, G - 1)
                v = maxT[:, G % 2, :]
                o = maxp[:, G % 2, :, :]
                m = bank_of(u)[0:HG * NT, 0:P]
                yield from after(V.tensor_copy(o[:, 0, :], m))
                tt(v, m, o[:, 0, :], ALU.subtract).then_inc(maxT_done, 1)
                yield
                dve.wait_ge(maxT_done, G + 1)
                yield from after(V.tensor_copy(o[:, 1, :], v))
                tt(o[:, 2, :], v, o[:, 1, :], ALU.subtract).then_inc(maxp_done, 1)
                yield

            def beside_dve(kind, a, m):
                u = (kind, a, m)
                if kind == "max":
                    urgent.insert(0, split_max(a))
                if kind == "rope" and a == 0:
                    wait_full(dve, u)
                    if m == 0:
                        dve.wait_ge(table_ld, 16)
                    V.scalar_tensor_tensor(out=rot[:, m, :], in0=bank_of(u)[:, :], scalar=c_["b_rope"][:, m:m + 1],
                                           in1=c_["cos"] if m % 2 == 0 else c_["sin"],
                                           op0=ALU.add, op1=ALU.mult).then_inc(rot0_done, 1)
                    if m % 2:
                        dve.wait_ge(rot0_done, m + 1)
                        i = m // 2
                        v = rot[:, m - 1, :]
                        link(tt(v, v, rot[:, m, :], ALU.add))
                        V.tensor_copy(parts[:, i, 0, :], v).then_inc(split_done[i], 1)
                        dve.wait_ge(split_done[i], 1)
                        link(tt(v, v, parts[:, i, 0, :], ALU.subtract))
                        V.tensor_copy(parts[:, i, 1, :], v).then_inc(split_done[i], 1)
                        dve.wait_ge(split_done[i], 2)
                        tt(parts[:, i, 2, :], v, parts[:, i, 1, :], ALU.subtract).then_inc(split_done[i], 1)
                if kind == "val":
                    wait_full(dve, u)
                    if a >= 2:
                        dve.wait_ge(pv_done, NG * NT * (a - 1))
                    tt(VA[a % 2][:, :, :, 0:DH], bank_of(u)[:, :].rearrange("p (t h d) -> p t h d", t=NT, d=DH),
                       c_["bv_row"].rearrange("p (h d) -> p h d", d=DH).unsqueeze(1).to_broadcast([P, NT, H, DH]),
                       ALU.add).then_inc(v_done, 1)
                if kind == "heads":
                    wait_full(dve, u)
                    if a >= 2 and m == 0:
                        wait_full(dve, ("attnT", a - 2, 0))
                    v = bank_of(u)[:, :].rearrange("p (h c) -> p h c", c=32)
                    link(V.reciprocal(rden[:, m, :], v[:, :, DH]))
                    tt(attn[:, a % 2, m, :].rearrange("p (h d) -> p h d", d=DH), v[:, :, 0:DH],
                       rden[:, m, :].unsqueeze(2).to_broadcast([P, H, DH]), ALU.mult).then_inc(attn_done, 1)
                if kind in ("proj", "Y1", "Y2"):
                    wait_full(dve, u)
                    k = {"proj": 0, "Y1": 2, "Y2": 3}[kind]
                    add_residual(k, a, bank_of(u)[:, :])
                    urgent.append(statistics(k, a))
                if kind == "chunk":
                    dve.wait_ge(down_done, (a + 1) * PAIRS)
                    add_residual(1, a, bank_of(("y_e", a, 0))[:, :])
                    urgent.append(statistics(1, a))
                if kind in ("norm", "norm1", "norm2", "norm3", "resT", "x2T", "x3T", "combine", "ghT"):
                    finish(kind in ("combine", "ghT"))
                if kind[:4] == "norm":
                    urgent.append(normalise(int(kind[4:] or 0), a))
                if kind == "gate":
                    routing.append(route(a))
                if kind == "kb":
                    wait_full(dve, u)
                    if m:
                        dve.wait_ge(kb_done, m)
                    V.tensor_scalar(bias_row[:, :], bank_of(u)[:, :], 1.0, None, ALU.add).then_inc(row_done, 1)
                    dve.wait_ge(row_done, m + 1)
                    v, o = bias_row[0:1, :], bias_parts[0:1, m, :, :]
                    link(V.tensor_copy(o[:, 0, :], v))
                    link(tt(v, v, o[:, 0, :], ALU.subtract))
                    link(V.tensor_copy(o[:, 1, :], v))
                    tt(o[:, 2, :], v, o[:, 1, :], ALU.subtract).then_inc(kb_done, 1)
                if kind == "K":
                    i = 4 * a + m
                    dve.wait_ge(expk_done, i + 1)
                    if a and m == 0:
                        wait_full(dve, ("KV", a - 1, 0))
                    V.scalar_tensor_tensor(out=KF[:, m, :], in0=ek_[:, i % 2, :], scalar=1.0, in1=bank_of(u)[:, :],
                                           op0=ALU.min, op1=ALU.max).then_inc(kf_done, 1)
                    step(3)
                if kind == "V":
                    wait_full(dve, u)
                    if a:
                        wait_full(dve, ("KV", a - 1, 0))
                    tt(VK[:, :, :, 0:HW], bank_of(u)[:, :].rearrange("p (t c d) -> p t c d", t=NT, c=NG),
                       c_["bv1_row"].rearrange("p (c d) -> p c d", c=NG).unsqueeze(1).to_broadcast([P, NT, NG, HW]),
                       ALU.add).then_inc(vk_done, 1)
                    step(3)
                if kind == "Q":
                    i = 4 * a + m
                    dve.wait_ge(expq_done, i + 1)
                    if a >= 2 and m == 0:
                        wait_full(dve, ("O", a - 2, 0))
                    V.scalar_tensor_tensor(out=QF[:, a % 2, m, :], in0=eq_[:, i % 2, :], scalar=1.0, in1=bank_of(u)[:, :],
                                           op0=ALU.min, op1=ALU.max).then_inc(qf_done, 1)
                    step(3)
                if kind == "KV":
                    wait_full(dve, u)
                    if a:
                        wait_full(dve, ("O", a - 1, 0))
                    kv = bank_of(u)[:, 0:NG * KVW].rearrange("p (c k) -> p c k", k=KVW)
                    own = c_["mask"].unsqueeze(1).to_broadcast([P, NG, HW])
                    tt(KVB[:, 1, :, :], own, kv[:, :, HW:KVW].to_broadcast([P, NG, HW]), ALU.mult)
                    tt(KVB[:, 0, :, :], kv[:, :, 0:HW], own, ALU.mult).then_inc(kvb_done, 1)
                    step(8)
                if kind == "OT" and m == 1:
                    wait_full(dve, u)
                    V.tensor_scalar(rt[:, 20, :], bank_of(u)[:, 0:NT * H], 256e-6, None, ALU.max).then_inc(floor_done, 1)
                    step(1)
                    dve.wait_ge(floor_done, a + 1)
                    link(V.reciprocal(rt[:, 21, :], rt[:, 20, :]))
                if kind == "OT" and m == 0:
                    wait_full(dve, u)
                    if a >= 2:
                        wait_full(dve, ("AT", a - 2, 0))
                    tt(attn[:, a % 2, :, :].rearrange("p t (h d) -> p t h d", d=DH),
                       bank_of(u)[:, :].rearrange("p (t h d) -> p t h d", t=NT, d=DH),
                       rt[:, 21, :].rearrange("p (t h) -> p t h", h=H).unsqueeze(3).to_broadcast([P, NT, H, DH]),
                       ALU.mult).then_inc(attn_done, 1)
                    step(8)
                if kind == "lg":
                    wait_full(dve, u)
                    lg = bank_of(u)[:, 0:NT * E1].rearrange("p (t e) -> p t e", e=E1)
                    mx = rl[:, 2, 0:NT]
                    link(V.tensor_reduce(out=mx, in_=lg, axis=X, op=ALU.max))
                    tt(r3(0, E1, rl), lg, mx.unsqueeze(2).to_broadcast([P, NT, E1]), ALU.subtract).then_inc(lsub_done, 1)
                    routing.append(lora_gates(a))

            V.memset(minus1[:, :], -1.0).then_inc(init_dve, 1)
            V.memset(wide(QS[0], 64, KROW), 0.0).then_inc(init_dve, 1)
            for s in ropes[:4]:
                beside_dve(*s)
            dve.wait_ge(early_ld, 16)
            beside_dve("val", 0, 0)
            V.memset(wide(KS[0], KROW, P), TWO_ONES).then_inc(init_dve, 1)
            for u in range(AHEAD):
                reduce_scores(u)
                if u == HG * NT:
                    beside_dve("max", 0, 0)
                    finish()
            for w in range(HALVES):
                for i in range(2):
                    if AHEAD + 2 * w + i < GROUPS * HG * NT:
                        reduce_scores(AHEAD + 2 * w + i)
                    step(2)
                for s in slots[w]:
                    beside_dve(*s)
            for i in range(NB * PAIRS):
                b, p = divmod(i, PAIRS)
                g, u = ("gate_e", i, 0), ("up_e", i, 0)
                dve.wait_ge(tanh_done, i + 1)
                h_ = gate_s[:, i % 2, :]
                V.scalar_tensor_tensor(out=h_, in0=h_, scalar=1.0, in1=bank_of(g)[:, :], op0=ALU.add, op1=ALU.mult)\
                    .then_inc(gated_done, 1)
                step(1)
                wait_full(dve, u)
                dve.wait_ge(gated_done, i + 1)
                if i >= 3:
                    dve.wait_ge(down_done, i - 2)
                if p == EP:
                    V.scalar_tensor_tensor(out=hid[:, i % 3, :], in0=h_, scalar=0.5, in1=bank_of(u)[:, :],
                                           op0=ALU.mult, op1=ALU.mult).then_inc(hid_done, 1)
                else:
                    tt(prod[:, i % 2, :], h_, bank_of(u)[:, :], ALU.mult).then_inc(prod_done, 1)
                    step(2)
                    dve.wait_ge(prod_done, b * EP + p + 1)
                    c = ("comb_e", i, 0)
                    wait_full(dve, c)
                    tt(hid[:, i % 3, :], prod[:, i % 2, :], bank_of(c)[:, :], ALU.mult).then_inc(hid_done, 1)
                step(3)
                for s in beside[i]:
                    beside_dve(*s)
            for s in layer2:
                beside_dve(*s)
            finish()


def rows(v):
    return np.broadcast_to(np.asarray(v)[None, :], (P, v.shape[0]))


def kernel(**inputs):
    import concourse.bacc as bacc
    from concourse.bass_utils import run_bass_kernel_spmd as run
    import ml_dtypes

    a = {k: np.asarray(v) for k, v in inputs.items()}
    x = a["L0_attn_x"].reshape(NB * T, D)
    f = np.arange(D)
    order = f % H * DH + f // H
    partner = f % H * DH + (f // H + DH // 2) % DH
    d = f // H
    w, bq = a["L0_attn_W_qkv"], a["L0_attn_b_qkv"]
    wq, wk, wv = w[:, :D], w[:, D:2 * D], w[:, 2 * D:]
    b_q, b_k = bq[:D], bq[D:2 * D]
    inv = (1.0 / np.float32(10000.0) ** (np.arange(0, DH, 2, dtype=np.float32) / np.float32(DH))).astype(np.float32)
    ang = (np.arange(T, dtype=np.float32)[None, :] * inv[d % (DH // 2)][:, None]).astype(np.float64)
    sign = np.where(d < DH // 2, -1.0, 1.0)[:, None]
    early = dict(w_kq=np.concatenate([wk[:, order], wk[:, partner], wq[:, order], wq[:, partner]], 1), w_v=wv,
                 b_rope=np.stack([b_k[order], b_k[partner], b_q[order], b_q[partner]], 1),
                 cos=np.cos(ang).astype(np.float32), sin=(np.sin(ang) * sign).astype(np.float32),
                 ident=np.eye(P, dtype=np.float32), bv_row=rows(bq[2 * D:]))
    r = a["L1_attn_random_matrix"]
    rbd = np.zeros((D, H * M1), np.float32)
    for h in range(H):
        rbd[h * DH:(h + 1) * DH, h * M1:(h + 1) * M1] = r
    mask = np.zeros((P, HW), np.float32)
    for h in range(HG):
        mask[h * M1:(h + 1) * M1, h * DH:(h + 1) * DH] = 1.0

    def reset(e):
        v = np.ones((P, NT, e), np.float32)
        v[:, :, 0] = 0.0
        return v.reshape(P, NT * e)

    w2 = a["L0_ffn_w2_e"].transpose(0, 2, 1).reshape(EP, 2 * F0, D).transpose(1, 0, 2).reshape(P, EP * D)
    late = dict(w_out=a["L0_attn_W_out"], bout_row=rows(a["L0_attn_b_out"]), wg=a["L0_ffn_w_gate"].T,
                w1=a["L0_ffn_w1_e"].reshape(E0 * F0, D).T, w3=a["L0_ffn_w3_e"].reshape(E0 * F0, D).T, w2=w2,
                w1s=a["L0_ffn_w1_s"].T, w3s=a["L0_ffn_w3_s"].T, w2s=a["L0_ffn_w2_s"].T, reset16=reset(E0),
                wqT=a["L1_attn_Wq"].T, wkT=a["L1_attn_Wk"].T, wv1=a["L1_attn_Wv"], wo1=a["L1_attn_Wo"], rbd=rbd,
                bq_rep=np.broadcast_to(a["L1_attn_bq"][:, None], (D, P)), bk_rep=np.broadcast_to(a["L1_attn_bk"][:, None], (D, P)),
                bv1_row=rows(a["L1_attn_bv"]), bo1_row=rows(a["L1_attn_bo"]), mask=mask,
                lr=a["L1_ffn_R"].T, la=a["L1_ffn_A"].reshape(E1 * R1, D).T, lw=a["L1_ffn_W"].T,
                lb=a["L1_ffn_B"].transpose(0, 2, 1).reshape(E1 * R1, D), lb_row=rows(a["L1_ffn_b"]), reset8=reset(E1))
    sel = np.zeros((3, E0, EP, P), np.float32)
    for e in range(E0):
        sel[:, e, e // 2, (e % 2) * F0:(e % 2 + 1) * F0] = 0.5
    bf = ml_dtypes.bfloat16
    arrays = {
        "in_x": np.ascontiguousarray(x), "in_xT": np.ascontiguousarray(x.T),
        "in_early": np.ascontiguousarray(np.concatenate([early[k] for k in EARLY], 1)),
        "in_late": np.ascontiguousarray(np.concatenate([late[k] for k in LATE], 1)),
        "in_sel": sel.reshape(3 * E0, EP, P).astype(bf), "in_identb": np.eye(P).astype(bf),
    }
    nc = bacc.Bacc("TRN2", target_bir_lowering=False, num_devices=1)
    args = [nc.dram_tensor(k, v.shape, mybir.dt.from_np(v.dtype), kind="ExternalInput").ap() for k, v in arrays.items()]
    parts_dram = nc.dram_tensor("parts_dram", (NB, 2, 3, D, T), BF16, kind="Internal").ap()
    out = nc.dram_tensor("out_y", (NB * T, D), F32, kind="ExternalOutput").ap()
    program(nc, *args, parts_dram, out)
    result = run(nc, [arrays], core_ids=[0])
    return result.results[0]["out_y"].reshape(NB, T, D)
```
